# Optimizing a Trainium2 kernel written in Bass

```python
import numpy as np
import jax
import jax.numpy as jnp

def _softmax(x, axis=-1):
    return jax.nn.softmax(x, axis=axis)

def _gelu(x):
    return jax.nn.gelu(x, approximate=True)

def _silu(x):
    return jax.nn.silu(x)

def _sigmoid(x):
    return jax.nn.sigmoid(x)

def _layernorm(x, axis=-1, eps=1e-05):
    m = jnp.mean(x, axis=axis, keepdims=True)
    v = jnp.var(x, axis=axis, keepdims=True)
    return (x - m) / jnp.sqrt(v + eps)

def _scatter_add(tgt, idx, src, axis=0):
    return tgt.at[idx].add(src)

def _segment_sum(src, seg, n):
    return jax.ops.segment_sum(src, seg, n)
kernel_name = 'mk_seq_postln_d1_jaxref_r8_f37a06'

def setup_inputs(seed: int=0):
    np.random.seed(seed)
    _w = jnp.asarray

    def _L0_attn_setup():
        import math
        import jax, jax.numpy as jnp
        import numpy as np
        HEAD_DIM = 128
        NUM_HEADS = 16
        ROPE_BASE = 10000.0

        def _rope_tables(seq_len, dim, dtype):
            inv_freq = 1.0 / ROPE_BASE ** (jnp.arange(0, dim, 2, dtype=jnp.float32) / dim)
            t = jnp.arange(seq_len, dtype=jnp.float32)
            freqs = jnp.einsum('i,j->ij', t, inv_freq)
            emb = jnp.concatenate([freqs, freqs], axis=-1)
            return (jnp.cos(emb).astype(dtype), jnp.sin(emb).astype(dtype))

        def _rotate_half(x):
            x1, x2 = jnp.split(x, 2, axis=-1)
            return jnp.concatenate([-x2, x1], axis=-1)

        def _apply_rope(x, cos, sin):
            return x * cos[None, :, None, :] + _rotate_half(x) * sin[None, :, None, :]
        key = jax.random.key(seed)
        k1, k2, k3 = jax.random.split(key, 3)
        B, S, dim = (2, 256, 256)
        out_dim = (NUM_HEADS + 2 * NUM_HEADS) * HEAD_DIM
        x = jax.random.normal(k1, (B, S, dim), dtype=jnp.float32)
        w_qkv = jax.random.normal(k2, (out_dim, dim), dtype=jnp.float32) * 0.02
        w_out = jax.random.normal(k3, (dim, NUM_HEADS * HEAD_DIM), dtype=jnp.float32) * 0.02
        return {'x': x, 'w_qkv': w_qkv, 'w_out': w_out}
    _L0_attn_in = _L0_attn_setup()

    def _L0_ffn_setup():
        import jax, jax.numpy as jnp
        import numpy as np
        B, S, H = (1, 128, 256)
        I = 176
        E = 32
        K = 6
        G = 8
        TG = 3
        NSH = 2
        SCALE = 16.0
        C = 48

        def _moe_forward(x3, gate_w, w_gate_up, w_down, ws_gate_up, ws_down):
            b, s, h = x3.shape
            x = x3.reshape(-1, h)
            T = x.shape[0]
            logits = x @ gate_w.T
            grouped = logits.reshape(T, G, E // G)
            group_scores = jnp.max(grouped, axis=-1)
            _, group_idx = jax.lax.top_k(group_scores, TG)
            group_keep = jnp.zeros((T, G), bool).at[jnp.arange(T)[:, None], group_idx].set(True)
            masked = jnp.where(group_keep[..., None], grouped, 0.0)
            scores = masked.reshape(T, E)
            probs = jax.nn.softmax(scores.astype(jnp.float32), axis=-1)
            topk_w, topk_idx = jax.lax.top_k(probs, K)
            topk_w = topk_w * SCALE
            flat_e = topk_idx.reshape(-1)
            tok_idx = jnp.repeat(jnp.arange(T), K)
            oh = jax.nn.one_hot(flat_e, E, dtype=jnp.int32)
            pos = jnp.take_along_axis(jnp.cumsum(oh, axis=0) - 1, flat_e[:, None], axis=1)[:, 0]
            valid = pos < C
            slot = jnp.where(valid, flat_e * C + pos, E * C)
            buf = jnp.zeros((E * C + 1, h), x.dtype).at[slot].set(x[tok_idx])
            xb = buf[:E * C].reshape(E, C, h)
            gu = jnp.einsum('ech,ehf->ecf', xb, w_gate_up)
            g, u = jnp.split(gu, 2, axis=-1)
            act = jax.nn.silu(g) * u
            yb = jnp.einsum('eci,eih->ech', act, w_down)
            yflat = jnp.concatenate([yb.reshape(E * C, h), jnp.zeros((1, h), yb.dtype)], axis=0)
            y_pairs = yflat[slot].reshape(T, K, h)
            out = jnp.einsum('tk,tkh->th', topk_w.astype(x.dtype), y_pairs)
            gu_s = x @ ws_gate_up
            gs, us = jnp.split(gu_s, 2, axis=-1)
            out = out + jax.nn.silu(gs) * us @ ws_down
            return out.reshape(b, s, h)
        key = jax.random.key(seed)
        ks = jax.random.split(key, 6)
        s = 0.02
        return {'hidden_states': jax.random.normal(ks[0], (B, S, H), jnp.float32), 'gate_w': jax.random.normal(ks[1], (E, H), jnp.float32) * s, 'w_gate_up': jax.random.normal(ks[2], (E, H, 2 * I), jnp.float32) * s, 'w_down': jax.random.normal(ks[3], (E, I, H), jnp.float32) * s, 'ws_gate_up': jax.random.normal(ks[4], (H, 2 * I * NSH), jnp.float32) * s, 'ws_down': jax.random.normal(ks[5], (I * NSH, H), jnp.float32) * s}
    _L0_ffn_in = _L0_ffn_setup()
    _d = {'L0_attn_x': _L0_attn_in['x'], 'L0_attn_w_qkv': _L0_attn_in['w_qkv'], 'L0_attn_w_out': _L0_attn_in['w_out'], 'L0_ffn_gate_w': _L0_ffn_in['gate_w'], 'L0_ffn_w_gate_up': _L0_ffn_in['w_gate_up'], 'L0_ffn_w_down': _L0_ffn_in['w_down'], 'L0_ffn_ws_gate_up': _L0_ffn_in['ws_gate_up'], 'L0_ffn_ws_down': _L0_ffn_in['ws_down']}
    _x0 = _d['L0_attn_x']
    _d['L0_attn_x'] = jax.random.normal(jax.random.fold_in(jax.random.key(seed), 1), (4, 512, 256), dtype=_x0.dtype)
    del _x0
    return _d

def reference(L0_attn_x, L0_attn_w_qkv, L0_attn_w_out, L0_ffn_gate_w, L0_ffn_w_gate_up, L0_ffn_w_down, L0_ffn_ws_gate_up, L0_ffn_ws_down):

    def _L0_attn_ref(x, w_qkv, w_out):
        import math
        import jax, jax.numpy as jnp
        import numpy as np
        HEAD_DIM = 128
        NUM_HEADS = 16
        ROPE_BASE = 10000.0

        def _rope_tables(seq_len, dim, dtype):
            inv_freq = 1.0 / ROPE_BASE ** (jnp.arange(0, dim, 2, dtype=jnp.float32) / dim)
            t = jnp.arange(seq_len, dtype=jnp.float32)
            freqs = jnp.einsum('i,j->ij', t, inv_freq)
            emb = jnp.concatenate([freqs, freqs], axis=-1)
            return (jnp.cos(emb).astype(dtype), jnp.sin(emb).astype(dtype))

        def _rotate_half(x):
            x1, x2 = jnp.split(x, 2, axis=-1)
            return jnp.concatenate([-x2, x1], axis=-1)

        def _apply_rope(x, cos, sin):
            return x * cos[None, :, None, :] + _rotate_half(x) * sin[None, :, None, :]
        B, S, _ = x.shape
        H, D = (NUM_HEADS, HEAD_DIM)
        qkv = jnp.einsum('bsd,od->bso', x, w_qkv)
        qkv = qkv.reshape(B, S, 3 * H, D)
        q = qkv[:, :, :H, :]
        k = qkv[:, :, H:2 * H, :]
        v = qkv[:, :, 2 * H:, :]
        cos, sin = _rope_tables(S, D, x.dtype)
        q = _apply_rope(q, cos, sin)
        k = _apply_rope(k, cos, sin)
        scale = 1.0 / math.sqrt(D)
        logits = jnp.einsum('bqhd,bkhd->bhqk', q, k) * scale
        attn = jax.nn.softmax(logits.astype(jnp.float32), axis=-1).astype(logits.dtype)
        out = jnp.einsum('bhqk,bkhd->bqhd', attn, v)
        out = out.reshape(B, S, H * D)
        return jnp.einsum('bso,do->bsd', out, w_out)

    def _L0_ffn_ref(hidden_states, gate_w, w_gate_up, w_down, ws_gate_up, ws_down):
        import jax, jax.numpy as jnp
        import numpy as np
        B, S, H = (1, 128, 256)
        I = 176
        E = 32
        K = 6
        G = 8
        TG = 3
        NSH = 2
        SCALE = 16.0
        C = 48

        def _moe_forward(x3, gate_w, w_gate_up, w_down, ws_gate_up, ws_down):
            b, s, h = x3.shape
            x = x3.reshape(-1, h)
            T = x.shape[0]
            logits = x @ gate_w.T
            grouped = logits.reshape(T, G, E // G)
            group_scores = jnp.max(grouped, axis=-1)
            _, group_idx = jax.lax.top_k(group_scores, TG)
            group_keep = jnp.zeros((T, G), bool).at[jnp.arange(T)[:, None], group_idx].set(True)
            masked = jnp.where(group_keep[..., None], grouped, 0.0)
            scores = masked.reshape(T, E)
            probs = jax.nn.softmax(scores.astype(jnp.float32), axis=-1)
            topk_w, topk_idx = jax.lax.top_k(probs, K)
            topk_w = topk_w * SCALE
            flat_e = topk_idx.reshape(-1)
            tok_idx = jnp.repeat(jnp.arange(T), K)
            oh = jax.nn.one_hot(flat_e, E, dtype=jnp.int32)
            pos = jnp.take_along_axis(jnp.cumsum(oh, axis=0) - 1, flat_e[:, None], axis=1)[:, 0]
            valid = pos < C
            slot = jnp.where(valid, flat_e * C + pos, E * C)
            buf = jnp.zeros((E * C + 1, h), x.dtype).at[slot].set(x[tok_idx])
            xb = buf[:E * C].reshape(E, C, h)
            gu = jnp.einsum('ech,ehf->ecf', xb, w_gate_up)
            g, u = jnp.split(gu, 2, axis=-1)
            act = jax.nn.silu(g) * u
            yb = jnp.einsum('eci,eih->ech', act, w_down)
            yflat = jnp.concatenate([yb.reshape(E * C, h), jnp.zeros((1, h), yb.dtype)], axis=0)
            y_pairs = yflat[slot].reshape(T, K, h)
            out = jnp.einsum('tk,tkh->th', topk_w.astype(x.dtype), y_pairs)
            gu_s = x @ ws_gate_up
            gs, us = jnp.split(gu_s, 2, axis=-1)
            out = out + jax.nn.silu(gs) * us @ ws_down
            return out.reshape(b, s, h)
        return _moe_forward(hidden_states, gate_w, w_gate_up, w_down, ws_gate_up, ws_down)
    x = L0_attn_x
    x = _layernorm(x + _L0_attn_ref(x, L0_attn_w_qkv, L0_attn_w_out), axis=-1)
    x = _layernorm(x + _L0_ffn_ref(x, L0_ffn_gate_w, L0_ffn_w_gate_up, L0_ffn_w_down, L0_ffn_ws_gate_up, L0_ffn_ws_down), axis=-1)
    return x

_drawn_inputs = setup_inputs


def setup_inputs(seed=0):
    import zlib

    import numpy as np

    out = dict(_drawn_inputs(seed))
    spreads = {}
    factors = {'L0_attn_w_qkv': 4.431,
     'L0_attn_w_out': 4.41,
     'L0_ffn_gate_w': 3.175,
     'L0_ffn_ws_gate_up': 2.844,
     'L0_ffn_ws_down': 2.853}
    for name, (base, spread) in spreads.items():
        noise = np.random.default_rng([zlib.crc32(name.encode()), seed]).standard_normal(out[name].shape)
        drawn = base * np.exp(spread * noise) if base else spread * noise
        out[name] = jnp.asarray(drawn.astype(out[name].dtype))
    for name, factor in factors.items():
        out[name] = (out[name] * factor).astype(out[name].dtype)
    return out
```

```python
from contextlib import ExitStack

import concourse.bass as bass
from concourse import mybir

F32 = mybir.dt.float32
F32R = mybir.dt.float32r
BF16 = mybir.dt.bfloat16
U32 = mybir.dt.uint32
ALU = mybir.AluOpType
ACT = mybir.ActivationFunctionType
AX = mybir.AxisListType

P = 128
B, S, D = 4, 512, 256
T = B * S
DC = D // P
H, DH = 16, 128
HALF = DH // 2
PAIRS = H // 2
QT = S // P
HEADS = B * PAIRS * 2
PER_PAIR = 2 * B

TILES = T // P
QUARTERS = TILES // QT
E, I = 32, 176
GROUPS, KEPT = 8, 3
PICKED = 6
SCALE = 16.0
CAP = 48
ROWS = 64
DUOS = E // 2
IJ, IW = 2, I // 2
SH = 2 * I
SH_CHUNKS = [(f, min(P, SH - f)) for f in range(0, SH, P)]
EPS = 1e-5
XW = D + E
REGION = T + ROWS
FAR = 4096.0
RING = 4

CONST_AT = [0]
for _width in (P, GROUPS * GROUPS, CAP, TILES * E, 1, 1, 1):
    CONST_AT.append(CONST_AT[-1] + _width)
MASK_AT = [0, P, 2 * P, 2 * P + 3 * TILES]
MASKS = MASK_AT[-1]
CONSTS = CONST_AT[-1] + MASKS

PASSES = ((1, 0), (0, 1), (0, 0))


def layer(nc, xT_in, wqk_in, wv_in, wo_in, rope_in, gate_in, wsg_in, wsd_in, wgu_in, wd_in, const_in_, out):
    with ExitStack() as ctx:
        scope = [ctx]

        def sb(name, shape, dt=F32):
            return scope[0].enter_context(nc.sbuf_tensor(name, shape, dt))

        def pair_of(name, shape):
            return [sb(name + part, shape, F32R) for part in ("_hi", "_lo")]

        def bank(name, dt=F32):
            return ctx.enter_context(nc.psum_tensor(name, [P, 512], dt))

        def sem(name):
            return ctx.enter_context(nc.semaphore(name))

        acc = sb("acc", [P, DC, T])
        x = pair_of("x", [P, DC, T])
        consts = sb("consts", [P, CONSTS])
        ident, tri, places, resets, empty_row, region_of, eps = [
            consts[:, a:b] for a, b in zip(CONST_AT, CONST_AT[1:])]
        masks = sb("masks", [P, MASKS], BF16)
        before, ones, token_parts = [masks[:, a:b] for a, b in zip(MASK_AT, MASK_AT[1:])]
        zeros = sb("zeros", [P, 2 * D])
        attention_only = ExitStack()
        scope[0] = attention_only
        rope = sb("rope", [P, 2, 2, S])
        wqk_raw = sb("wqk_raw", [P, DC, 4 * DH])
        wv_raw = sb("wv_raw", [P, DC, 2 * DH])
        wo_raw = sb("wo_raw", [P, 2, D])
        wqk = pair_of("wqk", [P, DC, 4 * DH])
        wv = pair_of("wv", [P, DC, 2 * DH])
        wo = pair_of("wo", [P, 2, D])
        qk_cos = sb("qk_cos", [P, 2, S])
        qk_rot = sb("qk_rot", [P, 2, S])
        qk = [pair_of(f"qk{i}", [P, 2, S]) for i in range(2)]
        v = [pair_of(f"v{i}", [P, QT, 2 * DH]) for i in range(2)]
        prob = [sb(f"prob{i}", [P, QT, S]) for i in range(2)]
        neg_max = sb("neg_max", [P, 2, QT])
        row_sum = sb("row_sum", [P, 2, QT])
        inv_sum = sb("inv_sum", [P, 2, QT])
        pT = [pair_of(f"pT{i}", [P, S]) for i in range(2)]
        o = [pair_of(f"o{i}", [P, S]) for i in range(4)]

        attention_only.close()

        scope[0] = ctx
        x1 = sb("x1", [P, TILES, D])
        gate_raw, gate = sb("gate_raw", [P, DC, E]), pair_of("gate", [P, DC, E])
        wsg_raw, wsg = sb("wsg_raw", [P, DC, 2 * SH]), pair_of("wsg", [P, DC, 2 * SH])
        wsd_raw, wsd = sb("wsd_raw", [P, len(SH_CHUNKS), D]), pair_of("wsd", [P, len(SH_CHUNKS), D])
        sh_gate, sh_up = [[sb(f"sh_{n}{i}", [P, S]) for i in range(2)] for n in ("gate", "up")]
        sh = pair_of("sh", [P, len(SH_CHUNKS), S])
        stats = sb("stats", [P, TILES, 6])
        moments = sb("moments", [P, TILES, 2])
        std, rstd = sb("std", [P, TILES]), sb("rstd", [P, TILES])
        logits = sb("logits", [P, TILES, E])
        group_max, group_rank = sb("group_max", [P, TILES * GROUPS]), sb("group_rank", [P, TILES * GROUPS])
        above, equal = [sb(n, [P, TILES * GROUPS * GROUPS]) for n in ("above", "equal")]
        masked = sb("masked", [P, TILES, E])
        top = sb("top", [P, TILES, 8])
        expd = sb("expd", [P, TILES, E])
        over, same, upto = [sb(n, [P, TILES, E]) for n in ("over", "same", "upto")]
        n_over, total, inv_total = [sb(n, [P, TILES]) for n in ("n_over", "total", "inv_total")]
        picked, picked_b = sb("picked", [P, TILES, E]), sb("picked_b", [P, TILES, E], BF16)
        weight = sb("weight", [P, TILES, E])
        key = sb("key", [P, TILES, E])
        onehot = [sb(f"onehot{i}", [P, E, ROWS], BF16) for i in range(2)]
        found = sb("found", [P, DUOS, 3])
        token, vacant, row = [sb(n, [P, DUOS]) for n in ("token", "vacant", "row")]
        gather_row, add_row = sb("gather_row", [P, DUOS], U32), sb("add_row", [P, DUOS], U32)
        xg = [sb(f"xg{i}", [P, XW]) for i in range(RING)]
        xgT = [sb(f"xgT{i}", [P, DC, P]) for i in range(2)]
        eg = [sb(f"eg{i}", [P, I]) for i in range(2)]
        eh = [sb(f"eh{i}", [P, I]) for i in range(2)]
        ehT = [sb(f"ehT{i}", [IW, IJ, P]) for i in range(2)]
        ey = [sb(f"ey{i}", [P, D]) for i in range(2)]
        experts_only = ExitStack()
        scope[0] = experts_only
        wgu = [sb(f"wgu{i}", [P, 2, DC, 2 * I]) for i in range(RING)]
        wd = [sb(f"wd{i}", [IW, 2, IJ, D]) for i in range(RING)]
        experts_only.close()
        scope[0] = ctx
        routed = sb("routed", [P, 2, TILES, D])
        table = nc.dram_tensor("table", (T, XW), F32, kind="Internal").ap()
        sums = nc.dram_tensor("sums", (2 * REGION, D), F32, kind="Internal").ap()

        ps_s = [bank(f"ps_s{i}") for i in range(2)]
        ps_t = [bank(f"ps_t{i}") for i in range(2)]
        ps_o = bank("ps_o")
        ps_qk = ctx.enter_context(nc.psum_tensor("ps_qk", [P, 2, 512], F32))
        ps_vy = bank("ps_vy")
        ps_y = [ps_vy, ps_o]

        x_in = [sem(f"x_in{b}") for b in range(B)]
        const_in = sem("const_in")
        wqk_in_s, wv_in_s, wo_in_s = sem("wqk_in"), sem("wv_in"), sem("wo_in")
        x_hi, x_lo = sem("x_hi"), sem("x_lo")
        wqk_hi, wqk_lo = sem("wqk_hi_s"), sem("wqk_lo_s")
        wv_hi, wv_lo = sem("wv_hi_s"), sem("wv_lo_s")
        wo_hi, wo_lo = sem("wo_hi_s"), sem("wo_lo_s")
        qk_proj = sem("qk_proj")
        qk_cosed, qk_swapped, qk_sined, qk_sum = sem("qk_cosed"), sem("qk_swapped"), sem("qk_sined"), sem("qk_sum")
        qk_hi, qk_lo = sem("qk_hi_s"), sem("qk_lo_s")
        v_proj, v_hi, v_lo = sem("v_proj"), sem("v_hi_s"), sem("v_lo_s")
        scored, maxed, exped, normed = sem("scored"), sem("maxed"), sem("exped"), sem("normed")
        inverted = sem("inverted")
        turned, pT_hi, pT_lo, mixed = sem("turned"), sem("pT_hi_s"), sem("pT_lo_s"), sem("mixed")
        o_hi, o_lo = sem("o_hi_s"), sem("o_lo_s")
        y_proj, y_added = sem("y_proj"), sem("y_added")
        stored = sem("stored")

        zeroed, cleared, masks_done = sem("zeroed"), sem("cleared"), sem("masks_done")
        gate_loaded, wsg_loaded, wsd_loaded = sem("gate_loaded"), sem("wsg_loaded"), sem("wsd_loaded")
        gate_hi_done, wsg_hi_done, wsd_hi_done = sem("gate_hi_done"), sem("wsg_hi_done"), sem("wsd_hi_done")
        gate_split, wsg_split, wsd_split = sem("gate_split"), sem("wsg_split"), sem("wsd_split")
        r_turned, r_stats, r_std, r_rstd = sem("r_turned"), sem("r_stats"), sem("r_std"), sem("r_rstd")
        x1_done = sem("x1_done")
        x1_turned, x1T_hi, x1T_lo, gated = sem("x1_turned"), sem("x1T_hi"), sem("x1T_lo"), sem("gated")
        dve_step, pool_step = sem("dve_step"), sem("pool_step")
        shifted, softexp = sem("shifted"), sem("softexp")
        picked_done, placed, weighted = sem("picked_done"), sem("placed"), sem("weighted")
        pads_zeroed, onehot_done, found_part, found_all = sem("pads_zeroed"), sem("onehot_done"), sem("found_part"), sem("found_all")
        rows_done, tabled = sem("rows_done"), sem("tabled")
        sh_projected, sh_silu, sh_copied, sh_product = sem("sh_projected"), sem("sh_silu"), sem("sh_copied"), sem("sh_product")
        sh_hi, sh_lo, sh_down, sh_added, based = sem("sh_hi_s"), sem("sh_lo_s"), sem("sh_down"), sem("sh_added"), sem("based")
        w_loaded = [sem(f"w_loaded{i}") for i in range(RING)]
        gathered = [sem(f"gathered{i}") for i in range(RING)]
        xg_turned, xgT_done, e_up, e_silu, e_hidden = sem("xg_turned"), sem("xgT_done"), sem("e_up"), sem("e_silu"), sem("e_hidden")
        eh_turned, ehT_done, e_down, e_scaled0, e_scaled1 = sem("eh_turned"), sem("ehT_done"), sem("e_down"), sem("e_scaled0"), sem("e_scaled1")
        summed = sem("summed")
        sums_in = [sem(f"sums_in{q}") for q in range(QUARTERS)]
        f_raw = sem("f_raw")
        f_sum, f_stats, f_std, f_rstd, f_done = sem("f_sum"), sem("f_stats"), sem("f_std"), sem("f_rstd"), sem("f_done")

        block = ctx.enter_context(nc.Block())

        def await_(eng, semaphore, count):
            if not isinstance(count, int) or count > 0:
                eng.wait_ge(semaphore, count)

        def half_at(s, lag):
            return s - lag - (s - lag) % 2, (s - lag) % 2

        def there(base, n, of=HEADS):
            return not isinstance(base, int) or 0 <= base + n < of

        def pipeline(eng, first, slot, last=None):
            for s in range(first, 4):
                slot(0, s)
            with eng.Fori(0, (PAIRS - 1) * PER_PAIR, PER_PAIR) as base:
                for s in range(4, 4 + PER_PAIR):
                    slot(base, s)
            for s in range(4, 11):
                slot((PAIRS - 1) * PER_PAIR, s)

        @block.sync
        def _(sp):
            for b in range(B):
                sp.dma_start(acc[:, :, b * S:(b + 1) * S], xT_in[:, :, b * S:(b + 1) * S]).then_inc(x_in[b], 16)
                if b == 0:
                    sp.dma_start(wqk_raw[:], wqk_in[0]).then_inc(wqk_in_s, 16)
                    sp.dma_start(rope[:], rope_in).then_inc(const_in, 16)
                    sp.dma_start(wv_raw[:], wv_in[0]).then_inc(wv_in_s, 16)
                    sp.dma_start(wo_raw[:], wo_in[0]).then_inc(wo_in_s, 16)
                    sp.dma_start(consts[:], const_in_).then_inc(const_in, 16)
            sp.wait_ge(zeroed, 1)
            for r in range(0, T, 2 * P):
                sp.dma_start(sums[REGION + r:REGION + r + 2 * P, :].rearrange("(p a) d -> p (a d)", a=2),
                             zeros[:]).then_inc(cleared, 16)
            for r in (T, REGION + T):
                sp.dma_start(sums[r:r + ROWS, :], zeros[0:ROWS, 0:D]).then_inc(cleared, 16)
            with sp.Fori(1, PAIRS) as p:
                sp.wait_ge(wqk_lo, p)
                sp.dma_start(wqk_raw[:], wqk_in[bass.ds(p, 1)].rearrange("a p c n -> (a p) c n")).then_inc(wqk_in_s, 16)
                sp.wait_ge(wv_lo, p)
                sp.dma_start(wv_raw[:], wv_in[bass.ds(p, 1)].rearrange("a p c n -> (a p) c n")).then_inc(wv_in_s, 16)
                sp.wait_ge(wo_lo, p)
                sp.dma_start(wo_raw[:], wo_in[bass.ds(p, 1)].rearrange("a p c n -> (a p) c n")).then_inc(wo_in_s, 16)
            sp.wait_ge(y_added, HEADS)
            sp.dma_start(gate_raw[:], gate_in).then_inc(gate_loaded, 16)
            sp.dma_start(wsg_raw[:], wsg_in).then_inc(wsg_loaded, 16)
            sp.dma_start(wsd_raw[:], wsd_in).then_inc(wsd_loaded, 16)
            for k in range(RING):
                sp.dma_start(wgu[k][:], wgu_in[k]).then_inc(w_loaded[k], 16)
                sp.dma_start(wd[k][:], wd_in[k]).then_inc(w_loaded[k], 16)
            rows = table.rearrange("(t p) w -> p t w", p=P)
            sp.wait_ge(x1_done, TILES)
            sp.dma_start(rows[:, :, 0:D], x1[:]).then_inc(tabled, 16)
            sp.wait_ge(weighted, 1)
            sp.dma_start(rows[:, :, D:XW], weight[:]).then_inc(tabled, 16)
            sp.wait_ge(sh_added, TILES)
            sp.dma_start(sums[0:T, :].rearrange("(t p) d -> p t d", p=P), x1[:]).then_inc(based, 16)
            with sp.Fori(1, DUOS // RING) as it:
                for k in range(RING):
                    sp.wait_ge(e_down, it * RING + (k - RING + 1))
                    sp.dma_start(wgu[k][:], wgu_in[bass.ds(it * RING + k, 1)].rearrange("a p e c i -> (a p) e c i")).then_inc(w_loaded[k], 16)
                    sp.dma_start(wd[k][:], wd_in[bass.ds(it * RING + k, 1)].rearrange("a p e j d -> (a p) e j d")).then_inc(w_loaded[k], 16)
            by_tile = lambda rows: rows.rearrange("(t p) d -> p t d", p=P)
            sp.wait_ge(summed, 16 * DUOS)
            for q in range(QUARTERS):
                for r in range(2):
                    first = r * REGION + q * QT * P
                    sp.dma_start(routed[:, r, q * QT:(q + 1) * QT, :],
                                 by_tile(sums[first:first + QT * P, :])).then_inc(sums_in[q], 16)
            for q in range(QUARTERS):
                sp.wait_ge(f_done, (q + 1) * QT)
                sp.dma_start(by_tile(out[q * QT * P:(q + 1) * QT * P, :]),
                             x1[:, q * QT:(q + 1) * QT, :]).then_inc(stored, 16)
            sp.wait_ge(stored, 16 * QUARTERS)

        @block.tensor
        def _(pe):
            def project_qk(base, n, part):
                b, head = n // 2 % B, n % 2
                if part == 0:
                    await_(pe, qk_swapped, base + n)
                    if n % PER_PAIR == 0:
                        pe.wait_ge(wqk_lo, pair(base, n) + 1)
                col = (2 * part + head) * DH
                k = 0
                for c in range(DC):
                    for w_part, x_part in PASSES:
                        mm = pe.matmul(ps_qk[:, part, :], wqk[w_part][:, c, col:col + DH],
                                       x[x_part][:, c, b * S:(b + 1) * S], start=k == 0, stop=k == 5)
                        k += 1
                if part == 1:
                    mm.then_inc(qk_proj, 1)

            def project_v(base, n, half):
                b = n // 2 % B
                await_(pe, y_added, base + n - 3 + half)
                if half == 0 and n % PER_PAIR == 0:
                    pe.wait_ge(wv_lo, pair(base, n) + 1)
                for j in range(2):
                    t0 = b * S + (2 * half + j) * P
                    k = 0
                    for c in range(DC):
                        for x_part, w_part in PASSES:
                            mm = pe.matmul(ps_vy[:, j * 2 * DH:(j + 1) * 2 * DH], x[x_part][:, c, t0:t0 + P],
                                           wv[w_part][:, c, :], start=k == 0, stop=k == 5)
                            k += 1
                mm.then_inc(v_proj, 1)

            def project_y(base, n, half):
                if there(base, n + 2 + 2 * half):
                    pe.wait_ge(v_lo, base + n + 4 + half)
                else:
                    pe.wait_ge(y_added, base + n + half)
                if half == 0:
                    pe.wait_ge(o_lo, base + n + 2)
                    if n % PER_PAIR == 0:
                        pe.wait_ge(wo_lo, pair(base, n) + 1)
                k = 0
                for head in range(2):
                    for w_part, o_part in PASSES:
                        mm = pe.matmul(ps_vy[:], wo[w_part][:, head, half * P:(half + 1) * P],
                                       o[(n + head) % 4][o_part][:], start=k == 0, stop=k == 5)
                        k += 1
                mm.then_inc(y_proj, 1)

            def score(base, n, i):
                if i == 0:
                    pe.wait_ge(qk_lo, base + n + 1)
                await_(pe, exped, base * QT + (n * QT + i - 1))
                for k, (q_part, k_part) in enumerate(PASSES):
                    mm = pe.matmul(ps_s[i % 2][:], qk[n % 2][q_part][:, 0, i * P:(i + 1) * P],
                                   qk[n % 2][k_part][:, 1, :], start=k == 0, stop=k == 2)
                mm.then_inc(scored, 1)

            def turn(base, n, j):
                if j == 0:
                    pe.wait_ge(normed, base * QT + (n * QT + QT))
                await_(pe, pT_lo, base * QT + (n * QT + j - 1))
                for i in range(QT):
                    mm = pe.transpose(ps_t[j % 2][:, i * P:(i + 1) * P], prob[n % 2][:, i, j * P:(j + 1) * P], ident)
                mm.then_inc(turned, 1)

            def mix(base, n, j):
                pe.wait_ge(pT_lo, base * QT + (n * QT + j + 1))
                if j == 0:
                    pe.wait_ge(v_lo, base + (n - n % 2 + 2))
                    await_(pe, o_lo, base + n)
                head = n % 2
                for k, (v_part, p_part) in enumerate(PASSES):
                    mm = pe.matmul(ps_o[:], v[n // 2 % 2][v_part][:, j, head * DH:(head + 1) * DH],
                                   pT[j % 2][p_part][:], start=j == 0 and k == 0, stop=j == QT - 1 and k == 2)
                mm.then_inc(mixed, 1)

            def slot(base, s):
                scoring, projecting = there(base, s), there(base, s + 2)
                mixing = there(base, s - 1)
                y_head, y_half = half_at(s, 3)
                v_head, v_half = half_at(s, -1)
                if scoring:
                    score(base, s, 0)
                if projecting:
                    project_qk(base, s + 2, 0)
                if there(base, s - 2):
                    mix(base, s - 2, 3)
                if mixing:
                    turn(base, s - 1, 0)
                if scoring:
                    score(base, s, 1)
                if projecting:
                    project_qk(base, s + 2, 1)
                if mixing:
                    turn(base, s - 1, 1)
                if scoring:
                    score(base, s, 2)
                if there(base, y_head):
                    project_y(base, y_head, y_half)
                if mixing:
                    turn(base, s - 1, 2)
                    mix(base, s - 1, 0)
                if scoring:
                    score(base, s, 3)
                if mixing:
                    mix(base, s - 1, 1)
                if there(base, v_head):
                    project_v(base, v_head, v_half)
                if mixing:
                    turn(base, s - 1, 3)
                    mix(base, s - 1, 2)

            def pair(base, n):
                return base // PER_PAIR + n // PER_PAIR if isinstance(base, int) else pair_reg[0] + n // PER_PAIR

            pair_reg = [0]
            pe.wait_ge(const_in, 32)
            for s in range(-2, 4):
                if -2 <= s:
                    pe.wait_ge(x_lo, min(B, (s + 2) // 2 + 1))
                slot(0, s)
            with pe.Fori(0, PAIRS - 1) as pair_index:
                pair_reg[0] = pair_index
                for s in range(4, 4 + PER_PAIR):
                    slot(pair_index * PER_PAIR, s)
            for s in range(4, 11):
                slot((PAIRS - 1) * PER_PAIR, s)

            def turn_sum(t):
                await_(pe, x1_done, t - 1)
                for c in range(DC):
                    mm = pe.transpose(ps_s[t % 2][:, c * P:(c + 1) * P], acc[:, c, t * P:(t + 1) * P], ident)
                mm.then_inc(r_turned, 1)

            def turn_x1(t):
                pe.wait_ge(x1_done, t + 1)
                await_(pe, x1T_lo, t - 1)
                for c in range(DC):
                    mm = pe.transpose(ps_t[t % 2][:, c * P:(c + 1) * P], x1[:, t, c * P:(c + 1) * P], ident)
                mm.then_inc(x1_turned, 1)

            def project_logits(t):
                pe.wait_ge(x1T_lo, t + 1)
                if t == 0:
                    pe.wait_ge(gate_split, 1)
                k = 0
                for c in range(DC):
                    for x_part, w_part in PASSES:
                        mm = pe.matmul(ps_o[:, t * E:(t + 1) * E], x[x_part][:, c, t * P:(t + 1) * P],
                                       gate[w_part][:, c, :], start=k == 0, stop=k == 5)
                        k += 1
                mm.then_inc(gated, 1)

            pe.wait_ge(y_added, HEADS)
            for t in range(TILES + 4):
                if t < TILES:
                    turn_sum(t)
                if 0 <= t - 2 < TILES:
                    turn_x1(t - 2)
                if 0 <= t - 4:
                    project_logits(t - 4)

            def shared_up(b, j):
                m = b * len(SH_CHUNKS) + j
                f, size = SH_CHUNKS[j]
                if m == 0:
                    pe.wait_ge(wsg_split, 1)
                    pe.wait_ge(x1_done, TILES)
                    pe.wait_ge(x1T_lo, TILES)
                await_(pe, sh_copied, m - 1)
                for bank_, f0 in ((ps_s[m % 2], f), (ps_t[m % 2], SH + f)):
                    k = 0
                    for c in range(DC):
                        for w_part, x_part in PASSES:
                            mm = pe.matmul(bank_[0:size, :], wsg[w_part][:, c, f0:f0 + size],
                                           x[x_part][:, c, b * S:(b + 1) * S], start=k == 0, stop=k == 5)
                            k += 1
                mm.then_inc(sh_projected, 1)

            def shared_down(b):
                pe.wait_ge(sh_lo, (b + 1) * len(SH_CHUNKS))
                if b == 0:
                    pe.wait_ge(wsd_split, 1)
                for i in range(QT):
                    t = b * QT + i
                    await_(pe, sh_added, t - 1)
                    k = 0
                    for j, (_, size) in enumerate(SH_CHUNKS):
                        for h_part, w_part in PASSES:
                            mm = pe.matmul(ps_qk[:, t % 2, 0:D], sh[h_part][0:size, j, i * P:(i + 1) * P],
                                           wsd[w_part][0:size, j, :], start=k == 0, stop=k == 8)
                            k += 1
                    mm.then_inc(sh_down, 1)

            def find(i):
                pe.wait_ge(onehot_done, i + 1)
                for d in range(DUOS):
                    mm = pe.matmul(ps_o[:, 3 * d:3 * d + 3],
                                   onehot[i % 2][:, 2 * d:2 * d + 2, :].rearrange("p e r -> p (e r)"),
                                   token_parts[:, 3 * i:3 * i + 3], start=i == 0 and d == 0,
                                   stop=i == TILES - 1, skip_group_check=True)
                mm.then_inc(found_part, 1)

            for j in range(len(SH_CHUNKS)):
                shared_up(0, j)
            shared_up(1, 0)
            shared_down(0)
            for j in range(1, len(SH_CHUNKS)):
                shared_up(1, j)
            pe.wait_ge(picked_done, 1)
            pe.wait_ge(masks_done, 1)
            flat = picked_b[:].rearrange("p t e -> p (t e)")
            pe.matmul(ps_vy[:], before, flat, start=True, stop=False, skip_group_check=True)
            for k in range(1, TILES):
                mm = pe.matmul(ps_vy[:, k * E:], ones, flat[:, 0:(TILES - k) * E], start=False,
                               stop=k == TILES - 1, skip_group_check=True)
            mm.then_inc(placed, 1)
            for i in range(TILES):
                find(i)
                if i % 2:
                    b, part = divmod(i // 2, 4)
                    if part == 1:
                        shared_down(b + 1)
                    else:
                        shared_up(b + 2, (0, 0, 1, 2)[part])
            shared_down(3)

            def turn_rows(it, base, n):
                pe.wait_ge(gathered[n % RING], (it + (n // RING + 1)) * 16)
                await_(pe, xgT_done, base + n)
                for c in range(DC):
                    mm = pe.transpose(ps_s[0][:, c * P:(c + 1) * P], xg[n % RING][:, c * P:(c + 1) * P], ident)
                mm.then_inc(xg_turned, 1)

            def expert_up(it, base, n):
                pe.wait_ge(w_loaded[n % RING], (it + (n // RING + 1)) * 32)
                pe.wait_ge(xgT_done, base + n + 1)
                await_(pe, e_hidden, base + n - 1)
                for e in range(2):
                    rows = slice(e * ROWS, (e + 1) * ROWS)
                    for c in range(DC):
                        mm = pe.matmul(ps_t[n % 2][rows, 0:2 * I], xgT[n % 2][:, c, rows], wgu[n % RING][:, e, c, :],
                                       start=c == 0, stop=c == DC - 1)
                mm.then_inc(e_up, 1)

            def turn_hidden(it, base, n):
                pe.wait_ge(e_hidden, base + n + 1)
                await_(pe, ehT_done, base + n)
                for j in range(IJ):
                    mm = pe.transpose(ps_s[1][0:IW, j * P:(j + 1) * P], eh[n % 2][:, j * IW:(j + 1) * IW], ident)
                mm.then_inc(eh_turned, 1)

            def expert_down(it, base, n):
                pe.wait_ge(ehT_done, base + n + 1)
                await_(pe, e_scaled0, base + n - 1)
                await_(pe, e_scaled1, base + n - 1)
                for e in range(2):
                    rows = slice(e * ROWS, (e + 1) * ROWS)
                    for j in range(IJ):
                        mm = pe.matmul(ps_y[n % 2][rows, 0:D], ehT[n % 2][:, j, rows], wd[n % RING][:, e, j, :],
                                       start=j == 0, stop=j == IJ - 1)
                mm.then_inc(e_down, 1)

            def duo_slot(it, base, s):
                if there(base, s, DUOS):
                    expert_up(it, base, s)
                if there(base, s - 1, DUOS):
                    turn_hidden(it, base, s - 1)
                if there(base, s - 2, DUOS):
                    expert_down(it, base, s - 2)
                if there(base, s + 1, DUOS):
                    turn_rows(it, base, s + 1)

            pe.wait_ge(sh_copied, B * len(SH_CHUNKS))
            pe.wait_ge(rows_done, 1)

            def experts(slot):
                for s in range(-1, 2 + RING):
                    slot(0, 0, s)
                with pe.Fori(1, DUOS // RING - 1) as it:
                    for s in range(2, 2 + RING):
                        slot(it, it * RING, s)
                for s in range(2, 2 + RING):
                    slot(DUOS // RING - 1, DUOS - RING, s)

            experts(duo_slot)

        @block.scalar
        def _(act):
            def exp(base, n, i):
                act.wait_ge(maxed, base * QT + (n * QT + i + 1))
                if i == 0:
                    await_(act, turned, base * QT + (n - 1) * QT)
                nc.scalar.activation(prob[n % 2][:, i, :], ps_s[i % 2][:], ACT.Exp, bias=neg_max[:, n % 2, i:i + 1],
                                     accum_out=row_sum[:, n % 2, i:i + 1]).then_inc(exped, 1)

            def split_o(base, n):
                act.wait_ge(mixed, base * QT + (n + 1) * QT)
                nc.scalar.copy(o[n % 4][0][:], ps_o[:]).then_inc(o_hi, 1)

            def split_pT(base, n, j):
                act.wait_ge(turned, base * QT + (n * QT + j + 1))
                await_(act, mixed, base * QT + (n * QT + j - 1))
                nc.scalar.copy(pT[j % 2][0][:], ps_t[j % 2][:]).then_inc(pT_hi, 1)

            def swap_qk(base, n, half):
                if half == 0:
                    act.wait_ge(qk_cosed, base + n + 1)
                    await_(act, qk_lo, base + n)
                    nc.scalar.copy(qk_rot[0:HALF, :, :], ps_qk[HALF:P, :, :])
                else:
                    nc.scalar.copy(qk_rot[HALF:P, :, :], ps_qk[0:HALF, :, :]).then_inc(qk_swapped, 1)

            def split_v(base, n, half):
                act.wait_ge(v_proj, base + n + half + 1)
                if half == 0:
                    await_(act, mixed, (base + (n - 2)) * QT)
                nc.scalar.copy(v[n // 2 % 2][0][:, 2 * half:2 * half + 2, :],
                               ps_vy[:].rearrange("p (j d) -> p j d", j=2)).then_inc(v_hi, 1)

            def slot(base, s):
                scoring, mixing, projecting = there(base, s), there(base, s - 1), there(base, s + 2)
                v_head, v_half = half_at(s, -1)
                if scoring:
                    exp(base, s, 0)
                if there(base, s - 2):
                    split_o(base, s - 2)
                if mixing:
                    split_pT(base, s - 1, 0)
                if scoring:
                    exp(base, s, 1)
                if mixing:
                    split_pT(base, s - 1, 1)
                if projecting:
                    swap_qk(base, s + 2, 0)
                if scoring:
                    exp(base, s, 2)
                if mixing:
                    split_pT(base, s - 1, 2)
                if projecting:
                    swap_qk(base, s + 2, 1)
                if there(base, v_head):
                    split_v(base, v_head, v_half)
                if mixing:
                    split_pT(base, s - 1, 3)
                if scoring:
                    exp(base, s, 3)

            pipeline(act, -2, slot)

            for loaded, whole, parts, done in ((gate_loaded, gate_raw, gate, gate_hi_done), (wsg_loaded, wsg_raw, wsg, wsg_hi_done),
                                               (wsd_loaded, wsd_raw, wsd, wsd_hi_done)):
                act.wait_ge(loaded, 16)
                nc.scalar.copy(parts[0][:], whole[:]).then_inc(done, 1)
            for t in range(TILES + 2):
                if t < TILES:
                    act.wait_ge(r_stats, t + 1)
                    nc.scalar.activation(std[:, t:t + 1], moments[:, t, 1:2], ACT.Sqrt, bias=eps).then_inc(r_std, 1)
                if 0 <= t - 2:
                    u = t - 2
                    act.wait_ge(x1_turned, u + 1)
                    nc.scalar.copy(x[0][:, :, u * P:(u + 1) * P],
                                   ps_t[u % 2][:, 0:D].rearrange("p (c t) -> p c t", c=DC)).then_inc(x1T_hi, 1)

            def shared_act(m):
                size = SH_CHUNKS[m % len(SH_CHUNKS)][1]
                act.wait_ge(sh_projected, m + 1)
                await_(act, sh_lo, m - 1)
                nc.scalar.activation(sh_gate[m % 2][0:size, :], ps_s[m % 2][0:size, :], ACT.Silu).then_inc(sh_silu, 1)
                nc.scalar.copy(sh_up[m % 2][0:size, :], ps_t[m % 2][0:size, :]).then_inc(sh_copied, 1)

            def shared_split(m):
                b, j = divmod(m, len(SH_CHUNKS))
                size = SH_CHUNKS[j][1]
                act.wait_ge(sh_product, m + 1)
                await_(act, sh_down, b * QT)
                nc.scalar.copy(sh[0][0:size, j, :], sh_up[m % 2][0:size, :]).then_inc(sh_hi, 1)

            def softmax_exp():
                act.wait_ge(shifted, 1)
                nc.scalar.activation(expd[:], expd[:], ACT.Exp).then_inc(softexp, 1)

            n_up = B * len(SH_CHUNKS)
            for m in range(n_up + 1):
                if m < n_up:
                    shared_act(m)
                if m > 0:
                    shared_split(m - 1)
                if m == 2:
                    softmax_exp()

            def expert_silu(it, base, n):
                act.wait_ge(e_up, base + n + 1)
                await_(act, e_hidden, base + n - 1)
                nc.scalar.activation(eg[n % 2][:], ps_t[n % 2][:, 0:I], ACT.Silu).then_inc(e_silu, 1)

            def keep_hidden(it, base, n):
                act.wait_ge(eh_turned, base + n + 1)
                await_(act, e_down, base + n - 1)
                nc.scalar.copy(ehT[n % 2][:], ps_s[1][0:IW, 0:IJ * P].rearrange("p (j r) -> p j r", j=IJ)).then_inc(ehT_done, 1)

            def scale_rows(it, base, n):
                act.wait_ge(e_down, base + n + 1)
                await_(act, summed, (base + n - 1) * 16)
                col = base * 2 + (D + 2 * n + 1)
                nc.scalar.activation(ey[n % 2][ROWS:P, :], ps_y[n % 2][ROWS:P, 0:D], ACT.Copy,
                                     scale=xg[n % RING][ROWS:P, bass.ds(col, 1)]).then_inc(e_scaled1, 1)

            def duo_slot(it, base, s):
                if there(base, s, DUOS):
                    expert_silu(it, base, s)
                if there(base, s - 1, DUOS):
                    keep_hidden(it, base, s - 1)
                if there(base, s - 2, DUOS):
                    scale_rows(it, base, s - 2)

            def experts(slot):
                for s in range(-1, 2 + RING):
                    slot(0, 0, s)
                with act.Fori(1, DUOS // RING - 1) as it:
                    for s in range(2, 2 + RING):
                        slot(it, it * RING, s)
                for s in range(2, 2 + RING):
                    slot(DUOS // RING - 1, DUOS - RING, s)

            experts(duo_slot)

            for q in range(QUARTERS):
                tiles = slice(q * QT, (q + 1) * QT)
                act.wait_ge(f_stats, q + 1)
                nc.scalar.activation(std[:, tiles], moments[:, tiles, 1], ACT.Sqrt, bias=eps).then_inc(f_std, 1)

        @block.vector
        def _(dve):
            def row_max(base, n, i):
                dve.wait_ge(scored, base * QT + (n * QT + i + 1))
                nc.vector.tensor_reduce(neg_max[:, n % 2, i:i + 1], ps_s[i % 2][:], AX.X, ALU.max,
                                        negate=True).then_inc(maxed, 1)

            def invert(base, n, i):
                dve.wait_ge(exped, base * QT + (n * QT + i + 1))
                nc.vector.reciprocal(inv_sum[:, n % 2, i:i + 1], row_sum[:, n % 2, i:i + 1]).then_inc(inverted, 1)

            def normalise(base, n, i):
                dve.wait_ge(inverted, base * QT + (n * QT + i + 1))
                nc.vector.tensor_scalar(prob[n % 2][:, i, :], prob[n % 2][:, i, :], inv_sum[:, n % 2, i:i + 1], None,
                                        ALU.mult).then_inc(normed, 1)

            def rest(out, whole, hi):
                return nc.vector.tensor_tensor(out, whole, hi.bitcast(F32), ALU.subtract)

            def split_o(base, n):
                dve.wait_ge(o_hi, base + n + 1)
                rest(o[n % 4][1][:], ps_o[:], o[n % 4][0][:]).then_inc(o_lo, 1)

            def split_pT(base, n, j):
                dve.wait_ge(pT_hi, base * QT + (n * QT + j + 1))
                rest(pT[j % 2][1][:], ps_t[j % 2][:], pT[j % 2][0][:]).then_inc(pT_lo, 1)

            def cos_qk(base, n):
                dve.wait_ge(qk_proj, base + n + 1)
                await_(dve, qk_sum, base + n)
                nc.vector.tensor_tensor(qk_cos[:], ps_qk[:], rope[:, 0], ALU.mult).then_inc(qk_cosed, 1)

            def split_qk(base, n):
                dve.wait_ge(qk_sum, base + n + 1)
                await_(dve, scored, (base + (n - 1)) * QT)
                nc.vector.tensor_copy(qk[n % 2][0][:], qk_rot[:]).then_inc(qk_hi, 1)

            def split_v(base, n, half):
                dve.wait_ge(v_hi, base + n + half + 1)
                rows = slice(2 * half, 2 * half + 2)
                rest(v[n // 2 % 2][1][:, rows, :], ps_vy[:].rearrange("p (j d) -> p j d", j=2),
                     v[n // 2 % 2][0][:, rows, :]).then_inc(v_lo, 1)

            def add_y(base, n, half):
                b = n // 2 % B
                dve.wait_ge(y_proj, base + n + half + 1)
                into = acc[:, half, b * S:(b + 1) * S]
                nc.vector.tensor_tensor(into, ps_vy[:], into, ALU.add).then_inc(y_added, 1)

            def split_wqk(base, n):
                dve.wait_ge(wqk_in_s, 16 * (pair(base, n) + 1))
                await_(dve, qk_proj, base + n)
                nc.vector.tensor_copy(wqk[0][:], wqk_raw[:]).then_inc(wqk_hi, 1)

            def split_wv(base, n):
                dve.wait_ge(wv_in_s, 16 * (pair(base, n) + 1))
                await_(dve, v_proj, base + n)
                nc.vector.tensor_copy(wv[0][:], wv_raw[:]).then_inc(wv_hi, 1)

            def split_wo(base, n):
                dve.wait_ge(wo_in_s, 16 * (pair(base, n) + 1))
                await_(dve, y_proj, base + n)
                nc.vector.tensor_copy(wo[0][:], wo_raw[:]).then_inc(wo_hi, 1)

            def slot(base, s):
                scoring, mixing = there(base, s), there(base, s - 1)
                y_head, y_half = half_at(s, 3)
                v_head, v_half = half_at(s, -1)
                if mixing:
                    invert(base, s - 1, 3)
                if scoring:
                    row_max(base, s, 0)
                if mixing:
                    normalise(base, s - 1, 3)
                if there(base, s + 1) and s > -2:
                    split_qk(base, s + 1)
                if s % PER_PAIR == PER_PAIR - 1 and there(base, s + 1):
                    split_wv(base, s + 1)
                if there(base, s - 2):
                    split_o(base, s - 2)
                if scoring:
                    row_max(base, s, 1)
                if mixing:
                    split_pT(base, s - 1, 0)
                if there(base, s + 2):
                    cos_qk(base, s + 2)
                if scoring:
                    row_max(base, s, 2)
                    invert(base, s, 0)
                if s % PER_PAIR == PER_PAIR - 3 and there(base, s + 3):
                    split_wqk(base, s + 3)
                if mixing:
                    split_pT(base, s - 1, 1)
                if scoring:
                    normalise(base, s, 0)
                if there(base, y_head):
                    add_y(base, y_head, y_half)
                if scoring:
                    invert(base, s, 1)
                if s % PER_PAIR == 2 and there(base, s - 2):
                    split_wo(base, s - 2)
                if scoring:
                    invert(base, s, 2)
                    normalise(base, s, 1)
                if mixing:
                    split_pT(base, s - 1, 2)
                if scoring:
                    normalise(base, s, 2)
                    row_max(base, s, 3)
                if there(base, v_head):
                    split_v(base, v_head, v_half)
                if mixing:
                    split_pT(base, s - 1, 3)

            def pair(base, n):
                return base // PER_PAIR + n // PER_PAIR if isinstance(base, int) else pair_reg[0] + n // PER_PAIR

            pair_reg = [0]
            for b in range(B):
                if b == 0:
                    dve.wait_ge(wqk_in_s, 16)
                    nc.vector.tensor_copy(wqk[0][:], wqk_raw[:]).then_inc(wqk_hi, 1)
                dve.wait_ge(x_in[b], 16)
                cols = slice(b * S, (b + 1) * S)
                nc.vector.tensor_copy(x[0][:, :, cols], acc[:, :, cols]).then_inc(x_hi, 1)
            dve.wait_ge(const_in, 32)
            for s in range(-2, 4):
                slot(0, s)
            with dve.Fori(0, PAIRS - 1) as pair_index:
                pair_reg[0] = pair_index
                for s in range(4, 4 + PER_PAIR):
                    slot(pair_index * PER_PAIR, s)
            for s in range(4, 11):
                slot((PAIRS - 1) * PER_PAIR, s)

            steps = [0]

            def link(instruction):
                steps[0] += 1
                instruction.then_inc(dve_step, 1)
                dve.wait_ge(dve_step, steps[0])

            def split_low(hi_done, whole, parts, done):
                dve.wait_ge(hi_done, 1)
                rest(parts[1][:], whole[:], parts[0][:]).then_inc(done, 1)

            for t in range(TILES + 3):
                if t < TILES:
                    dve.wait_ge(r_turned, t + 1)
                    link(nc.vector.bn_stats(stats[:, t, :], ps_s[t % 2][:, 0:D]))
                    nc.vector.bn_aggr(moments[:, t, :], stats[:, t, :]).then_inc(r_stats, 1)
                if 0 <= t - 1 < TILES:
                    u = t - 1
                    dve.wait_ge(r_std, u + 1)
                    nc.vector.reciprocal(rstd[:, u:u + 1], std[:, u:u + 1]).then_inc(r_rstd, 1)
                    dve.wait_ge(r_rstd, u + 1)
                    nc.vector.tensor_scalar(x1[:, u, :], ps_s[u % 2][:, 0:D], moments[:, u, 0:1], rstd[:, u:u + 1],
                                            ALU.subtract, ALU.mult).then_inc(x1_done, 1)
                if 0 <= t - 3:
                    u = t - 3
                    dve.wait_ge(x1T_hi, u + 1)
                    rest(x[1][:, :, u * P:(u + 1) * P], ps_t[u % 2][:, 0:D].rearrange("p (c t) -> p c t", c=DC),
                         x[0][:, :, u * P:(u + 1) * P]).then_inc(x1T_lo, 1)
                if t == 1:
                    split_low(gate_hi_done, gate_raw, gate, gate_split)
                if t == 5:
                    split_low(wsg_hi_done, wsg_raw, wsg, wsg_split)
                if t == 9:
                    split_low(wsd_hi_done, wsd_raw, wsd, wsd_split)

            def over_group(ap, n):
                return ap.unsqueeze(2).broadcast_to([P, ap.shape[1], n])

            def add_shared(t):
                dve.wait_ge(sh_down, t + 1)
                if t == 0:
                    dve.wait_ge(tabled, 16)
                nc.vector.tensor_tensor(x1[:, t, :], ps_qk[:, t % 2, 0:D], x1[:, t, :], ALU.add).then_inc(sh_added, 1)

            dve.wait_ge(gated, TILES)
            link(nc.vector.tensor_copy(logits[:].rearrange("p t e -> p (t e)"), ps_o[:]))
            by_group = logits[:].rearrange("p t (g j) -> p (t g) j", g=GROUPS)
            link(nc.vector.tensor_reduce(group_max[:], by_group, AX.X, ALU.max))
            maxima = group_max[:].rearrange("p (t g) -> p t g", g=GROUPS)
            others = maxima.unsqueeze(2).broadcast_to([P, TILES, GROUPS, GROUPS])
            own = maxima.unsqueeze(3).broadcast_to([P, TILES, GROUPS, GROUPS])
            square = lambda a: a[:].rearrange("p (t g h) -> p t g h", g=GROUPS, h=GROUPS)
            nc.vector.tensor_tensor(square(above), others, own, ALU.is_gt)
            link(nc.vector.tensor_tensor(square(equal), others, own, ALU.is_equal))
            rows64 = lambda a: a[:].rearrange("p (t q) -> p t q", t=TILES)
            link(nc.vector.tensor_tensor(rows64(equal), rows64(equal),
                                         tri.unsqueeze(1).broadcast_to([P, TILES, GROUPS * GROUPS]), ALU.mult))
            link(nc.vector.tensor_tensor(above[:], above[:], equal[:], ALU.add))
            link(nc.vector.tensor_reduce(group_rank[:], above[:].rearrange("p (g h) -> p g h", h=GROUPS), AX.X, ALU.add))
            masked_by_group = masked[:].rearrange("p t (g j) -> p (t g) j", g=GROUPS)
            link(nc.vector.scalar_tensor_tensor(out=masked_by_group, in0=over_group(group_rank[:], E // GROUPS),
                                                scalar=float(KEPT), in1=by_group, op0=ALU.is_lt, op1=ALU.mult))
            for t in range(TILES):
                top8 = nc.vector.max(top[:, t, :], masked[:, t, :])
            link(top8)
            nc.vector.tensor_tensor(expd[:], masked[:], top[:, :, 0:1].broadcast_to([P, TILES, E]),
                                    ALU.subtract).then_inc(shifted, 1)
            sixth = top[:, :, PICKED - 1:PICKED].broadcast_to([P, TILES, E])
            nc.vector.tensor_tensor(over[:], masked[:], sixth, ALU.is_gt)
            link(nc.vector.tensor_tensor(same[:], masked[:], sixth, ALU.is_equal))
            nc.vector.tensor_reduce(n_over[:], over[:], AX.X, ALU.add)
            link(nc.vector.tensor_tensor_scan(upto[:].rearrange("p t e -> p (t e)"), resets,
                                              same[:].rearrange("p t e -> p (t e)"), 0.0, ALU.mult, ALU.add))
            link(nc.vector.tensor_tensor(upto[:], upto[:], over_group(n_over[:], E), ALU.add))
            link(nc.vector.scalar_tensor_tensor(out=upto[:], in0=upto[:], scalar=float(PICKED), in1=same[:],
                                                op0=ALU.is_le, op1=ALU.mult))
            link(nc.vector.tensor_tensor(picked[:], over[:], upto[:], ALU.add))
            nc.vector.tensor_copy(picked_b[:], picked[:]).then_inc(picked_done, 1)
            for t in range(QT):
                add_shared(t)
            dve.wait_ge(softexp, 1)
            link(nc.vector.tensor_reduce(total[:], expd[:], AX.X, ALU.add))
            link(nc.vector.reciprocal(inv_total[:], total[:]))
            link(nc.vector.tensor_tensor(weight[:], expd[:], over_group(inv_total[:], E), ALU.mult))
            nc.vector.scalar_tensor_tensor(out=weight[:], in0=weight[:], scalar=SCALE, in1=picked[:],
                                           op0=ALU.mult, op1=ALU.mult).then_inc(weighted, 1)

            dve.wait_ge(placed, 1)
            link(nc.vector.scalar_tensor_tensor(out=key[:].rearrange("p t e -> p (t e)"),
                                                in0=picked[:].rearrange("p t e -> p (t e)"), scalar=-FAR, in1=ps_vy[:],
                                                op0=ALU.mult, op1=ALU.add))
            dve.wait_ge(pads_zeroed, 2)
            for i in range(TILES):
                await_(dve, found_part, i - 1)
                nc.vector.tensor_tensor(onehot[i % 2][:, :, 0:CAP], key[:, i, :].unsqueeze(2).broadcast_to([P, E, CAP]),
                                        places.unsqueeze(1).broadcast_to([P, E, CAP]),
                                        ALU.is_equal).then_inc(onehot_done, 1)
                if i in (3, 11):
                    for k in range(QT):
                        add_shared((1 + i // 8) * QT + k)
            dve.wait_ge(found_part, TILES)
            link(nc.vector.tensor_copy(found[:].rearrange("p d c -> p (d c)"), ps_o[:, 0:3 * DUOS]))
            link(nc.vector.scalar_tensor_tensor(out=token[:], in0=found[:, :, 0], scalar=float(P), in1=found[:, :, 1],
                                                op0=ALU.mult, op1=ALU.add))
            nc.vector.tensor_copy(gather_row[:], token[:])
            link(nc.vector.tensor_scalar(vacant[:], found[:, :, 2], -1.0, 1.0, ALU.mult, ALU.add))
            link(nc.vector.scalar_tensor_tensor(out=row[:], in0=vacant[:], scalar=empty_row, in1=token[:],
                                                op0=ALU.mult, op1=ALU.add))
            nc.vector.tensor_scalar(add_row[:], row[:], region_of, None, ALU.add).then_inc(rows_done, 1)
            for t in range(3 * QT, TILES):
                add_shared(t)

            def keep_rows(it, base, n):
                dve.wait_ge(xg_turned, base + n + 1)
                await_(dve, e_up, base + n - 1)
                nc.vector.tensor_copy(xgT[n % 2][:], ps_s[0][:, 0:D].rearrange("p (c r) -> p c r", c=DC)).then_inc(xgT_done, 1)

            def hidden(it, base, n):
                dve.wait_ge(e_silu, base + n + 1)
                await_(dve, eh_turned, base + n - 1)
                nc.vector.tensor_tensor(eh[n % 2][:], ps_t[n % 2][:, I:2 * I], eg[n % 2][:], ALU.mult).then_inc(e_hidden, 1)

            def scale_rows(it, base, n):
                dve.wait_ge(e_down, base + n + 1)
                await_(dve, summed, (base + n - 1) * 16)
                col = base * 2 + (D + 2 * n)
                nc.vector.tensor_scalar(ey[n % 2][0:ROWS, :], ps_y[n % 2][0:ROWS, 0:D],
                                        xg[n % RING][0:ROWS, bass.ds(col, 1)], None, ALU.mult).then_inc(e_scaled0, 1)

            def duo_slot(it, base, s):
                if there(base, s, DUOS):
                    hidden(it, base, s)
                if there(base, s - 2, DUOS):
                    scale_rows(it, base, s - 2)
                if there(base, s + 1, DUOS):
                    keep_rows(it, base, s + 1)

            def experts(slot):
                for s in range(-1, 2 + RING):
                    slot(0, 0, s)
                with dve.Fori(1, DUOS // RING - 1) as it:
                    for s in range(2, 2 + RING):
                        slot(it, it * RING, s)
                for s in range(2, 2 + RING):
                    slot(DUOS // RING - 1, DUOS - RING, s)

            experts(duo_slot)

            for q in range(QUARTERS + 1):
                if q < QUARTERS:
                    tiles = slice(q * QT, (q + 1) * QT)
                    dve.wait_ge(sums_in[q], 32)
                    nc.vector.tensor_tensor(routed[:, 0, tiles, :], routed[:, 0, tiles, :], routed[:, 1, tiles, :],
                                            ALU.add).then_inc(f_sum, 1)
                    dve.wait_ge(f_sum, q + 1)
                    for t in range(q * QT, (q + 1) * QT):
                        raw = nc.vector.bn_stats(stats[:, t, :], routed[:, 0, t, :])
                    raw.then_inc(f_raw, 1)
                    dve.wait_ge(f_raw, q + 1)
                    for t in range(q * QT, (q + 1) * QT):
                        aggregated = nc.vector.bn_aggr(moments[:, t, :], stats[:, t, :])
                    aggregated.then_inc(f_stats, 1)
                if q > 0:
                    tiles = slice((q - 1) * QT, q * QT)
                    dve.wait_ge(f_std, q)
                    nc.vector.reciprocal(rstd[:, tiles], std[:, tiles]).then_inc(f_rstd, 1)
                    dve.wait_ge(f_rstd, q)
                    for t in range((q - 1) * QT, q * QT):
                        nc.vector.tensor_scalar(x1[:, t, :], routed[:, 0, t, :], moments[:, t, 0:1],
                                                rstd[:, t:t + 1], ALU.subtract, ALU.mult).then_inc(f_done, 1)

        @block.gpsimd
        def _(pool):
            def rest(out, whole, hi):
                return nc.gpsimd.tensor_tensor(out, whole, hi.bitcast(F32), ALU.subtract)

            def rotate_qk(base, n):
                pool.wait_ge(qk_swapped, base + n + 1)
                nc.gpsimd.tensor_tensor(qk_rot[:], qk_rot[:], rope[:, 1], ALU.mult).then_inc(qk_sined, 1)
                pool.wait_ge(qk_sined, base + n + 1)
                nc.gpsimd.tensor_tensor(qk_rot[:], qk_rot[:], qk_cos[:], ALU.add).then_inc(qk_sum, 1)

            def split_qk(base, n):
                pool.wait_ge(qk_hi, base + n + 1)
                rest(qk[n % 2][1][:], qk_rot[:], qk[n % 2][0][:]).then_inc(qk_lo, 1)

            def split_weights(base, s):
                if s % PER_PAIR == PER_PAIR - 3 and there(base, s + 3):
                    pool.wait_ge(wqk_hi, pair(base, s + 3) + 1)
                    rest(wqk[1][:], wqk_raw[:], wqk[0][:]).then_inc(wqk_lo, 1)
                if s % PER_PAIR == PER_PAIR - 1 and there(base, s + 1):
                    pool.wait_ge(wv_hi, pair(base, s + 1) + 1)
                    rest(wv[1][:], wv_raw[:], wv[0][:]).then_inc(wv_lo, 1)
                if s % PER_PAIR == 2 and there(base, s - 2):
                    pool.wait_ge(wo_hi, pair(base, s - 2) + 1)
                    rest(wo[1][:], wo_raw[:], wo[0][:]).then_inc(wo_lo, 1)

            def slot(base, s):
                if there(base, s + 1) and s > -2:
                    split_qk(base, s + 1)
                split_weights(base, s)
                if there(base, s + 2):
                    rotate_qk(base, s + 2)

            def pair(base, n):
                return base // PER_PAIR + n // PER_PAIR if isinstance(base, int) else pair_reg[0] + n // PER_PAIR

            pair_reg = [0]
            nc.gpsimd.memset(zeros[:], 0.0).then_inc(zeroed, 1)
            pool.wait_ge(const_in, 32)
            nc.gpsimd.tensor_copy(masks[:], consts[:, CONST_AT[-1]:]).then_inc(masks_done, 1)
            for b in range(B):
                if b == 0:
                    pool.wait_ge(wqk_hi, 1)
                    rest(wqk[1][:], wqk_raw[:], wqk[0][:]).then_inc(wqk_lo, 1)
                pool.wait_ge(x_hi, b + 1)
                cols = slice(b * S, (b + 1) * S)
                rest(x[1][:, :, cols], acc[:, :, cols], x[0][:, :, cols]).then_inc(x_lo, 1)
            for s in range(-2, 4):
                slot(0, s)
            with pool.Fori(0, PAIRS - 1) as pair_index:
                pair_reg[0] = pair_index
                for s in range(4, 4 + PER_PAIR):
                    slot(pair_index * PER_PAIR, s)
            for s in range(4, 11):
                slot((PAIRS - 1) * PER_PAIR, s)

            pool.wait_ge(y_added, HEADS)
            for i in range(2):
                nc.gpsimd.memset(onehot[i][:, :, CAP:ROWS], 0.0).then_inc(pads_zeroed, 1)

            for m in range(B * len(SH_CHUNKS)):
                j = m % len(SH_CHUNKS)
                size = SH_CHUNKS[j][1]
                up = sh_up[m % 2][0:size, :]
                pool.wait_ge(sh_copied, m + 1)
                nc.gpsimd.tensor_tensor(up, up, sh_gate[m % 2][0:size, :], ALU.mult).then_inc(sh_product, 1)
                pool.wait_ge(sh_hi, m + 1)
                rest(sh[1][0:size, j, :], up, sh[0][0:size, j, :]).then_inc(sh_lo, 1)

            def gather(n):
                if n >= RING:
                    pool.wait_ge(e_scaled0, n - RING + 1)
                    pool.wait_ge(e_scaled1, n - RING + 1)
                nc.gpsimd.indirect_dma_start(out=xg[n % RING][:], out_offset=None, in_=table,
                                             in_offset=bass.IndirectOffsetOnAxis(gather_row[:, n:n + 1], 0)
                                             ).then_inc(gathered[n % RING], 16)

            pool.wait_ge(rows_done, 1)
            pool.wait_ge(tabled, 32)
            for n in range(RING):
                gather(n)
            pool.wait_ge(cleared, 16 * (T // (2 * P) + 2))
            pool.wait_ge(based, 16)
            for n in range(DUOS):
                pool.wait_ge(e_scaled0, n + 1)
                pool.wait_ge(e_scaled1, n + 1)
                if n:
                    pool.wait_ge(summed, 16 * n)
                nc.gpsimd.indirect_dma_start(out=sums, out_offset=bass.IndirectOffsetOnAxis(add_row[:, n:n + 1], 0),
                                             in_=ey[n % 2][:], in_offset=None, compute_op=ALU.add).then_inc(summed, 16)
                if n + RING < DUOS:
                    gather(n + RING)



def _constants():
    import numpy as np

    inv_freq = 1.0 / 10000.0 ** (np.arange(0, DH, 2, dtype=np.float32) / DH)
    angle = (np.arange(S, dtype=np.float32)[:, None] * inv_freq[None].astype(np.float32)).T
    angle = np.concatenate([angle, angle])
    cos = np.cos(angle)
    sin = np.sin(angle) * np.where(np.arange(DH) < HALF, -1.0, 1.0)[:, None]
    scale = DH ** -0.5
    rope = np.stack([np.stack([cos * scale, cos], 1), np.stack([sin * scale, sin], 1)], 1)

    p = np.arange(P)
    g = np.arange(GROUPS)
    ident = np.eye(P)
    tri = np.broadcast_to((g[None, :] < g[:, None]).reshape(-1), (P, GROUPS * GROUPS))
    places = np.broadcast_to(np.arange(CAP) - FAR, (P, CAP))
    resets = np.broadcast_to(np.tile(np.arange(E) > 0, TILES), (P, TILES * E))
    empty_row = (T + p % ROWS)[:, None]
    region_of = (REGION * (p >= ROWS))[:, None]
    eps = np.full((P, 1), EPS)
    const = np.concatenate([ident, tri, places, resets, empty_row, region_of, eps], 1)

    before = p[:, None] < p[None, :]
    ones = np.ones((P, P))
    token_parts = np.stack([np.broadcast_to(np.arange(TILES), (P, TILES)),
                            np.broadcast_to(p[:, None], (P, TILES)), np.ones((P, TILES))], -1).reshape(P, -1)
    const = np.concatenate([const, before, ones, token_parts], 1)
    return rope.astype(np.float32), const.astype(np.float32)


def kernel(L0_attn_x, L0_attn_w_qkv, L0_attn_w_out, L0_ffn_gate_w, L0_ffn_w_gate_up, L0_ffn_w_down,
           L0_ffn_ws_gate_up, L0_ffn_ws_down):
    import numpy as np
    import concourse.bacc as bacc
    from concourse.bass_utils import run_bass_kernel_spmd

    qkv = np.asarray(L0_attn_w_qkv).reshape(3, H // 2, 2, DH, DC, P)
    shared_down = np.zeros((len(SH_CHUNKS) * P, D), np.float32)
    shared_down[:SH] = np.asarray(L0_ffn_ws_down)
    rope, const = _constants()
    arrays = {
        "xT": np.asarray(L0_attn_x).reshape(T, DC, P).transpose(2, 1, 0),
        "wqk": qkv[:2].transpose(1, 5, 4, 0, 2, 3).reshape(H // 2, P, DC, 4 * DH),
        "wv": qkv[2].transpose(0, 4, 3, 1, 2).reshape(H // 2, P, DC, 2 * DH),
        "wo": np.asarray(L0_attn_w_out).reshape(D, H // 2, 2, DH).transpose(1, 3, 2, 0),
        "rope": rope,
        "gate": np.asarray(L0_ffn_gate_w).reshape(E, DC, P).transpose(2, 1, 0),
        "wsg": np.asarray(L0_ffn_ws_gate_up).reshape(DC, P, 2 * SH).transpose(1, 0, 2),
        "wsd": shared_down.reshape(len(SH_CHUNKS), P, D).transpose(1, 0, 2),
        "wgu": np.asarray(L0_ffn_w_gate_up).reshape(DUOS, 2, DC, P, 2 * I).transpose(0, 3, 1, 2, 4),
        "wd": np.asarray(L0_ffn_w_down).reshape(DUOS, 2, IJ, IW, D).transpose(0, 3, 1, 2, 4),
        "const": const,
    }
    arrays = {f"in_{name}": np.ascontiguousarray(a) for name, a in arrays.items()}

    nc = bacc.Bacc("TRN2", target_bir_lowering=False, num_devices=1)
    args = [nc.dram_tensor(name, a.shape, mybir.dt.from_np(a.dtype), kind="ExternalInput").ap()
            for name, a in arrays.items()]
    out = nc.dram_tensor("out_0", (T, D), F32, kind="ExternalOutput").ap()
    layer(nc, *args, out)
    r = run_bass_kernel_spmd(nc, [arrays], core_ids=[0])
    return r.results[0]["out_0"].reshape(B, S, D)
```

```python
from contextlib import ExitStack

import concourse.bass as bass
from concourse import mybir

F32 = mybir.dt.float32
F32R = mybir.dt.float32r
BF16 = mybir.dt.bfloat16
U32 = mybir.dt.uint32
ALU = mybir.AluOpType
ACT = mybir.ActivationFunctionType
AX = mybir.AxisListType

P = 128
B, S, D = 4, 512, 256
T = B * S
DC = D // P
H, DH = 16, 128
HALF = DH // 2
PAIRS = H // 2
QT = S // P
HEADS = B * PAIRS * 2
PER_PAIR = 2 * B

TILES = T // P
QUARTERS = TILES // QT
E, I = 32, 176
GROUPS, KEPT = 8, 3
PICKED = 6
SCALE = 16.0
CAP = 48
ROWS = 64
DUOS = E // 2
IJ, IW = 2, I // 2
SH = 2 * I
SH_CHUNKS = [(f, min(P, SH - f)) for f in range(0, SH, P)]
EPS = 1e-5
XW = D + E
REGION = T + ROWS
TOP = 8
ZERO_ROWS = 3
RING = 4
TOKENS_RING = 8

CONST_AT = [0]
for _width in (P, GROUPS * GROUPS, TILES * E, TILES, 1, 1, 1):
    CONST_AT.append(CONST_AT[-1] + _width)
CONSTS = CONST_AT[-1]

PASSES = ((1, 0), (0, 1), (0, 0))

NEXT_STEPS = [("up", 2, 0), ("up", 2, 1), ("up", 2, 2), None, ("down", 2, 0), ("down", 2, 1),
              ("up", 3, 0), ("up", 3, 1), ("up", 3, 2), None, ("down", 3, 0), ("down", 3, 1)]
FIRST_UPS = 2 * len(SH_CHUNKS)



def layer(nc, xT_in, wqk_in, wv_in, wo_in, rope_in, gate_in, wsg_in, wsd_in, wgu_in, wd_in, const_in_, out):
    with ExitStack() as ctx:
        scope = [ctx]

        def sb(name, shape, dt=F32):
            return scope[0].enter_context(nc.sbuf_tensor(name, shape, dt))

        def pair_of(name, shape):
            return [sb(name + part, shape, F32R) for part in ("_hi", "_lo")]

        def bank(name, dt=F32):
            return ctx.enter_context(nc.psum_tensor(name, [P, 512], dt))

        def sem(name):
            return ctx.enter_context(nc.semaphore(name))

        acc = sb("acc", [P, DC, T])
        x = pair_of("x", [P, DC, T])
        consts = sb("consts", [P, CONSTS])
        ident, tri, resets, countdown, empty_row, region_of, eps = [
            consts[:, a:b] for a, b in zip(CONST_AT, CONST_AT[1:])]
        zeros = sb("zeros", [P, ZERO_ROWS * D])
        attention_only = ExitStack()
        scope[0] = attention_only
        rope = sb("rope", [P, 2, 2, S])
        wqk_raw = sb("wqk_raw", [P, DC, 4 * DH])
        wv_raw = sb("wv_raw", [P, DC, 2 * DH])
        wo_raw = sb("wo_raw", [P, 2, D])
        wqk = pair_of("wqk", [P, DC, 4 * DH])
        wv = pair_of("wv", [P, DC, 2 * DH])
        wo = pair_of("wo", [P, 2, D])
        qk_cos = sb("qk_cos", [P, 2, S])
        qk_rot = sb("qk_rot", [P, 2, S])
        qk = [pair_of(f"qk{i}", [P, 2, S]) for i in range(2)]
        v = [pair_of(f"v{i}", [P, QT, 2 * DH]) for i in range(2)]
        prob = [sb(f"prob{i}", [P, QT, S]) for i in range(2)]
        neg_max = sb("neg_max", [P, 2, QT])
        row_sum = sb("row_sum", [P, 2, QT])
        inv_sum = sb("inv_sum", [P, 2, QT])
        pT = [pair_of(f"pT{i}", [P, S]) for i in range(2)]
        o = [pair_of(f"o{i}", [P, S]) for i in range(4)]

        attention_only.close()

        scope[0] = ctx
        x1 = sb("x1", [P, TILES, D])
        gate_raw, gate = sb("gate_raw", [P, DC, E]), pair_of("gate", [P, DC, E])
        wsg_raw, wsg = sb("wsg_raw", [P, DC, 2 * SH]), pair_of("wsg", [P, DC, 2 * SH])
        wsd_raw, wsd = sb("wsd_raw", [P, len(SH_CHUNKS), D]), pair_of("wsd", [P, len(SH_CHUNKS), D])
        sh_gate, sh_up = [[sb(f"sh_{n}{i}", [P, S]) for i in range(2)] for n in ("gate", "up")]
        sh = pair_of("sh", [P, len(SH_CHUNKS), S])
        stats = sb("stats", [P, TILES, 6])
        moments = sb("moments", [P, TILES, 2])
        std, rstd, shift = [sb(n, [P, TILES]) for n in ("std", "rstd", "shift")]
        logits = sb("logits", [P, TILES, E])
        group_max, group_rank = sb("group_max", [P, TILES * GROUPS]), sb("group_rank", [P, TILES * GROUPS])
        above, equal = [sb(n, [P, TILES * GROUPS * GROUPS]) for n in ("above", "equal")]
        masked = sb("masked", [P, TILES, E])
        top = sb("top", [P, TILES, 8])
        expd = sb("expd", [P, TILES, E])
        over, same, upto = [sb(n, [P, TILES, E]) for n in ("over", "same", "upto")]
        n_over, total, inv_total = [sb(n, [P, TILES]) for n in ("n_over", "total", "inv_total")]
        picked = sb("picked", [P, TILES, E])
        weight = sb("weight", [P, TILES, E])
        key = sb("key", [P, TILES, E])
        left = [sb(f"left{i}", [P, S]) for i in range(2)]
        lists = sb("lists", [P, CAP])
        chosen = sb("chosen", [E, ROWS])
        found = sb("found", [P, DUOS])
        taken, counted, token, vacant, row = [sb(n, [P, DUOS]) for n in ("taken", "counted", "token", "vacant", "row")]
        gather_row, add_row = sb("gather_row", [P, DUOS], U32), sb("add_row", [P, DUOS], U32)
        xg = [sb(f"xg{i}", [P, XW]) for i in range(TOKENS_RING)]
        xgT = [sb(f"xgT{i}", [P, DC, P]) for i in range(2)]
        eg = [sb(f"eg{i}", [P, I]) for i in range(2)]
        eh = [sb(f"eh{i}", [P, I]) for i in range(2)]
        ehT = [sb(f"ehT{i}", [IW, IJ, P]) for i in range(2)]
        ey = [sb(f"ey{i}", [P, D]) for i in range(2)]
        experts_only = ExitStack()
        scope[0] = experts_only
        wgu = [sb(f"wgu{i}", [P, 2, DC, 2 * I]) for i in range(RING)]
        wd = [sb(f"wd{i}", [IW, 2, IJ, D]) for i in range(RING)]
        experts_only.close()
        scope[0] = ctx
        routed = sb("routed", [P, 2, TILES, D])
        table = nc.dram_tensor("table", (T, XW), F32, kind="Internal").ap()
        sums = nc.dram_tensor("sums", (2 * REGION, D), F32, kind="Internal").ap()

        ps_s = [bank(f"ps_s{i}") for i in range(2)]
        ps_t = [bank(f"ps_t{i}") for i in range(2)]
        ps_o = bank("ps_o")
        ps_qk = ctx.enter_context(nc.psum_tensor("ps_qk", [P, 2, 512], F32))
        ps_vy = bank("ps_vy")
        ps_y = [ps_vy, ps_o]

        x_in = [sem(f"x_in{b}") for b in range(B)]
        const_in = sem("const_in")
        wqk_in_s, wv_in_s, wo_in_s = sem("wqk_in"), sem("wv_in"), sem("wo_in")
        x_hi, x_lo = sem("x_hi"), sem("x_lo")
        wqk_hi, wqk_lo = sem("wqk_hi_s"), sem("wqk_lo_s")
        wv_hi, wv_lo = sem("wv_hi_s"), sem("wv_lo_s")
        wo_hi, wo_lo = sem("wo_hi_s"), sem("wo_lo_s")
        qk_proj = sem("qk_proj")
        qk_cosed, qk_swapped, qk_sined, qk_sum = sem("qk_cosed"), sem("qk_swapped"), sem("qk_sined"), sem("qk_sum")
        qk_hi, qk_lo = sem("qk_hi_s"), sem("qk_lo_s")
        v_proj, v_hi, v_lo = sem("v_proj"), sem("v_hi_s"), sem("v_lo_s")
        scored, maxed, exped, normed = sem("scored"), sem("maxed"), sem("exped"), sem("normed")
        inverted = sem("inverted")
        turned, pT_hi, pT_lo, mixed = sem("turned"), sem("pT_hi_s"), sem("pT_lo_s"), sem("mixed")
        o_hi, o_lo = sem("o_hi_s"), sem("o_lo_s")
        y_proj, y_added = sem("y_proj"), sem("y_added")
        stored = sem("stored")

        zeroed, cleared = sem("zeroed"), sem("cleared")
        gate_loaded, wsg_loaded, wsd_loaded = sem("gate_loaded"), sem("wsg_loaded"), sem("wsd_loaded")
        gate_hi_done, wsg_hi_done, wsd_hi_done = sem("gate_hi_done"), sem("wsg_hi_done"), sem("wsd_hi_done")
        gate_split, wsg_split, wsd_split = sem("gate_split"), sem("wsg_split"), sem("wsd_split")
        r_turned, r_stats, r_std, r_rstd = sem("r_turned"), sem("r_stats"), sem("r_std"), sem("r_rstd")
        x1_done = sem("x1_done")
        x1_turned, x1T_hi, x1T_lo, gated = sem("x1_turned"), sem("x1T_hi"), sem("x1T_lo"), sem("gated")
        dve_step, pool_step = sem("dve_step"), sem("pool_step")
        shifted, softexp = sem("shifted"), sem("softexp")
        keyed, keys_turned, weighted = sem("keyed"), sem("keys_turned"), sem("weighted")
        pads_zeroed, listed, collected = sem("pads_zeroed"), sem("listed"), sem("collected")
        chosen_done, spread = sem("chosen_done"), sem("spread")
        rows_done, x1_tabled, weight_tabled = sem("rows_done"), sem("x1_tabled"), sem("weight_tabled")
        sh_projected, sh_silu, sh_product = sem("sh_projected"), sem("sh_silu"), sem("sh_product")
        sh_hi, sh_lo, sh_down, sh_added = sem("sh_hi_s"), sem("sh_lo_s"), sem("sh_down"), sem("sh_added")
        w_loaded = [sem(f"w_loaded{i}") for i in range(RING)]
        gathered = [sem(f"gathered{i}") for i in range(TOKENS_RING)]
        xg_turned, xgT_done, e_up, e_silu, e_hidden = sem("xg_turned"), sem("xgT_done"), sem("e_up"), sem("e_silu"), sem("e_hidden")
        eh_turned, ehT_done, e_down, e_scaled0, e_scaled1 = sem("eh_turned"), sem("ehT_done"), sem("e_down"), sem("e_scaled0"), sem("e_scaled1")
        summed = sem("summed")
        sums_in = [sem(f"sums_in{q}") for q in range(QUARTERS)]
        f_raw = sem("f_raw")
        f_based, f_shift = sem("f_based"), sem("f_shift")
        f_sum, f_stats, f_std, f_rstd, f_done = sem("f_sum"), sem("f_stats"), sem("f_std"), sem("f_rstd"), sem("f_done")

        block = ctx.enter_context(nc.Block())

        def await_(eng, semaphore, count):
            if not isinstance(count, int) or count > 0:
                eng.wait_ge(semaphore, count)

        def half_at(s, lag):
            return s - lag - (s - lag) % 2, (s - lag) % 2

        def shared_banks(m):
            return (ps_s[m % 2], ps_t[m % 2]) if m < FIRST_UPS else (ps_qk[:, 0, :], ps_qk[:, 1, :])

        def next_step(s):
            return NEXT_STEPS[s] if 0 <= s < len(NEXT_STEPS) and NEXT_STEPS[s] else ("", 0, 0)

        def there(base, n, of=HEADS):
            return not isinstance(base, int) or 0 <= base + n < of

        def pipeline(eng, first, slot, last=None):
            for s in range(first, 4):
                slot(0, s)
            with eng.Fori(0, (PAIRS - 1) * PER_PAIR, PER_PAIR) as base:
                for s in range(4, 4 + PER_PAIR):
                    slot(base, s)
            for s in range(4, 11):
                slot((PAIRS - 1) * PER_PAIR, s)

        @block.sync
        def _(sp):
            for b in range(B):
                sp.dma_start(acc[:, :, b * S:(b + 1) * S], xT_in[:, :, b * S:(b + 1) * S]).then_inc(x_in[b], 16)
                if b == 0:
                    sp.dma_start(wqk_raw[:], wqk_in[0]).then_inc(wqk_in_s, 16)
                    sp.dma_start(rope[:], rope_in).then_inc(const_in, 16)
                    sp.dma_start(wv_raw[:], wv_in[0]).then_inc(wv_in_s, 16)
                    sp.dma_start(wo_raw[:], wo_in[0]).then_inc(wo_in_s, 16)
                    sp.dma_start(consts[:], const_in_).then_inc(const_in, 16)
            sp.wait_ge(zeroed, 1)
            for r in range(0, 2 * REGION, ZERO_ROWS * P):
                sp.dma_start(sums[r:r + ZERO_ROWS * P, :].rearrange("(p a) d -> p (a d)", a=ZERO_ROWS),
                             zeros[:]).then_inc(cleared, 16)
            with sp.Fori(1, PAIRS) as p:
                sp.wait_ge(wqk_lo, p)
                sp.dma_start(wqk_raw[:], wqk_in[bass.ds(p, 1)].rearrange("a p c n -> (a p) c n")).then_inc(wqk_in_s, 16)
                sp.wait_ge(wv_lo, p)
                sp.dma_start(wv_raw[:], wv_in[bass.ds(p, 1)].rearrange("a p c n -> (a p) c n")).then_inc(wv_in_s, 16)
                sp.wait_ge(wo_lo, p)
                sp.dma_start(wo_raw[:], wo_in[bass.ds(p, 1)].rearrange("a p c n -> (a p) c n")).then_inc(wo_in_s, 16)
            sp.wait_ge(y_added, HEADS)
            sp.dma_start(gate_raw[:], gate_in).then_inc(gate_loaded, 16)
            sp.dma_start(wsg_raw[:], wsg_in).then_inc(wsg_loaded, 16)
            sp.dma_start(wsd_raw[:], wsd_in).then_inc(wsd_loaded, 16)
            for k in range(RING):
                sp.dma_start(wgu[k][:], wgu_in[k]).then_inc(w_loaded[k], 16)
                sp.dma_start(wd[k][:], wd_in[k]).then_inc(w_loaded[k], 16)
            rows = table.rearrange("(t p) w -> p t w", p=P)
            sp.wait_ge(x1_done, TILES)
            sp.dma_start(rows[:, :, 0:D], x1[:]).then_inc(x1_tabled, 16)
            sp.wait_ge(weighted, 1)
            sp.dma_start(rows[:, :, D:XW], weight[:]).then_inc(weight_tabled, 16)
            with sp.Fori(1, DUOS // RING) as it:
                for k in range(RING):
                    sp.wait_ge(e_down, it * RING + (k - RING + 1))
                    sp.dma_start(wgu[k][:], wgu_in[bass.ds(it * RING + k, 1)].rearrange("a p e c i -> (a p) e c i")).then_inc(w_loaded[k], 16)
                    sp.dma_start(wd[k][:], wd_in[bass.ds(it * RING + k, 1)].rearrange("a p e j d -> (a p) e j d")).then_inc(w_loaded[k], 16)
            by_tile = lambda rows: rows.rearrange("(t p) d -> p t d", p=P)
            sp.wait_ge(summed, 16 * DUOS)
            for q in range(QUARTERS):
                for r in range(2):
                    first = r * REGION + q * QT * P
                    sp.dma_start(routed[:, r, q * QT:(q + 1) * QT, :],
                                 by_tile(sums[first:first + QT * P, :])).then_inc(sums_in[q], 16)
            for q in range(QUARTERS):
                sp.wait_ge(f_done, q + 1)
                sp.dma_start(by_tile(out[q * QT * P:(q + 1) * QT * P, :]),
                             x1[:, q * QT:(q + 1) * QT, :]).then_inc(stored, 16)
            sp.wait_ge(stored, 16 * QUARTERS)

        @block.tensor
        def _(pe):
            def project_qk(base, n, part):
                b, head = n // 2 % B, n % 2
                if part == 0:
                    await_(pe, qk_swapped, base + n)
                    if n % PER_PAIR == 0:
                        pe.wait_ge(wqk_lo, pair(base, n) + 1)
                col = (2 * part + head) * DH
                k = 0
                for c in range(DC):
                    for w_part, x_part in PASSES:
                        mm = pe.matmul(ps_qk[:, part, :], wqk[w_part][:, c, col:col + DH],
                                       x[x_part][:, c, b * S:(b + 1) * S], start=k == 0, stop=k == 5)
                        k += 1
                if part == 1:
                    mm.then_inc(qk_proj, 1)

            def project_v(base, n, half):
                b = n // 2 % B
                await_(pe, y_added, base + n - 3 + half)
                if half == 0 and n % PER_PAIR == 0:
                    pe.wait_ge(wv_lo, pair(base, n) + 1)
                for j in range(2):
                    t0 = b * S + (2 * half + j) * P
                    k = 0
                    for c in range(DC):
                        for x_part, w_part in PASSES:
                            mm = pe.matmul(ps_vy[:, j * 2 * DH:(j + 1) * 2 * DH], x[x_part][:, c, t0:t0 + P],
                                           wv[w_part][:, c, :], start=k == 0, stop=k == 5)
                            k += 1
                mm.then_inc(v_proj, 1)

            def project_y(base, n, half):
                if there(base, n + 2 + 2 * half):
                    pe.wait_ge(v_lo, base + n + 4 + half)
                else:
                    pe.wait_ge(y_added, base + n + half)
                if half == 0:
                    pe.wait_ge(o_lo, base + n + 2)
                    if n % PER_PAIR == 0:
                        pe.wait_ge(wo_lo, pair(base, n) + 1)
                k = 0
                for head in range(2):
                    for w_part, o_part in PASSES:
                        mm = pe.matmul(ps_vy[:], wo[w_part][:, head, half * P:(half + 1) * P],
                                       o[(n + head) % 4][o_part][:], start=k == 0, stop=k == 5)
                        k += 1
                mm.then_inc(y_proj, 1)

            def score(base, n, i):
                if i == 0:
                    pe.wait_ge(qk_lo, base + n + 1)
                await_(pe, exped, base * QT + (n * QT + i - 1))
                for k, (q_part, k_part) in enumerate(PASSES):
                    mm = pe.matmul(ps_s[i % 2][:], qk[n % 2][q_part][:, 0, i * P:(i + 1) * P],
                                   qk[n % 2][k_part][:, 1, :], start=k == 0, stop=k == 2)
                mm.then_inc(scored, 1)

            def turn(base, n, j):
                if j == 0:
                    pe.wait_ge(normed, base * QT + (n * QT + QT))
                await_(pe, pT_lo, base * QT + (n * QT + j - 1))
                for i in range(QT):
                    mm = pe.transpose(ps_t[j % 2][:, i * P:(i + 1) * P], prob[n % 2][:, i, j * P:(j + 1) * P], ident)
                mm.then_inc(turned, 1)

            def mix(base, n, j):
                pe.wait_ge(pT_lo, base * QT + (n * QT + j + 1))
                if j == 0:
                    pe.wait_ge(v_lo, base + (n - n % 2 + 2))
                    await_(pe, o_lo, base + n)
                head = n % 2
                for k, (v_part, p_part) in enumerate(PASSES):
                    mm = pe.matmul(ps_o[:], v[n // 2 % 2][v_part][:, j, head * DH:(head + 1) * DH],
                                   pT[j % 2][p_part][:], start=j == 0 and k == 0, stop=j == QT - 1 and k == 2)
                mm.then_inc(mixed, 1)

            def slot(base, s):
                scoring, projecting = there(base, s), there(base, s + 2)
                mixing = there(base, s - 1)
                y_head, y_half = half_at(s, 3)
                v_head, v_half = half_at(s, -1)
                if scoring:
                    score(base, s, 0)
                if projecting:
                    project_qk(base, s + 2, 0)
                if there(base, s - 2):
                    mix(base, s - 2, 3)
                if mixing:
                    turn(base, s - 1, 0)
                if scoring:
                    score(base, s, 1)
                if projecting:
                    project_qk(base, s + 2, 1)
                if mixing:
                    turn(base, s - 1, 1)
                if scoring:
                    score(base, s, 2)
                if there(base, y_head):
                    project_y(base, y_head, y_half)
                if mixing:
                    turn(base, s - 1, 2)
                    mix(base, s - 1, 0)
                if scoring:
                    score(base, s, 3)
                if mixing:
                    mix(base, s - 1, 1)
                if there(base, v_head):
                    project_v(base, v_head, v_half)
                if mixing:
                    turn(base, s - 1, 3)
                    mix(base, s - 1, 2)

            def pair(base, n):
                return base // PER_PAIR + n // PER_PAIR if isinstance(base, int) else pair_reg[0] + n // PER_PAIR

            pair_reg = [0]
            pe.wait_ge(const_in, 32)
            for s in range(-2, 4):
                if -2 <= s:
                    pe.wait_ge(x_lo, min(B, (s + 2) // 2 + 1))
                slot(0, s)
            with pe.Fori(0, PAIRS - 1) as pair_index:
                pair_reg[0] = pair_index
                for s in range(4, 4 + PER_PAIR):
                    slot(pair_index * PER_PAIR, s)
            for s in range(4, 11):
                slot((PAIRS - 1) * PER_PAIR, s)

            def turn_sum(t):
                await_(pe, x1_done, t - 1)
                for c in range(DC):
                    mm = pe.transpose(ps_s[t % 2][:, c * P:(c + 1) * P], acc[:, c, t * P:(t + 1) * P], ident)
                mm.then_inc(r_turned, 1)

            def turn_x1(t):
                pe.wait_ge(x1_done, t + 1)
                await_(pe, x1T_lo, t - 1)
                for c in range(DC):
                    mm = pe.transpose(ps_t[t % 2][:, c * P:(c + 1) * P], x1[:, t, c * P:(c + 1) * P], ident)
                mm.then_inc(x1_turned, 1)

            def project_logits(t):
                pe.wait_ge(x1T_lo, t + 1)
                if t == 0:
                    pe.wait_ge(gate_split, 1)
                k = 0
                for c in range(DC):
                    for x_part, w_part in PASSES:
                        mm = pe.matmul(ps_o[:, t * E:(t + 1) * E], x[x_part][:, c, t * P:(t + 1) * P],
                                       gate[w_part][:, c, :], start=k == 0, stop=k == 5)
                        k += 1
                mm.then_inc(gated, 1)

            pe.wait_ge(y_added, HEADS)
            for t in range(TILES + 4):
                if t < TILES:
                    turn_sum(t)
                if 0 <= t - 2 < TILES:
                    turn_x1(t - 2)
                if 0 <= t - 4:
                    project_logits(t - 4)

            def shared_up(b, j):
                m = b * len(SH_CHUNKS) + j
                f, size = SH_CHUNKS[j]
                if m == 0:
                    pe.wait_ge(wsg_split, 1)
                    pe.wait_ge(x1_done, TILES)
                    pe.wait_ge(x1T_lo, TILES)
                if m < FIRST_UPS:
                    await_(pe, sh_product, m - 1)
                else:
                    pe.wait_ge(sh_product, m)
                    pe.wait_ge(sh_added, 2 * b)
                for bank_, f0 in zip(shared_banks(m), (f, SH + f)):
                    k = 0
                    for c in range(DC):
                        for w_part, x_part in PASSES:
                            mm = pe.matmul(bank_[0:size, :], wsg[w_part][:, c, f0:f0 + size],
                                           x[x_part][:, c, b * S:(b + 1) * S], start=k == 0, stop=k == 5)
                            k += 1
                mm.then_inc(sh_projected, 1)

            def shared_down(b, half):
                u = 2 * b + half
                if half == 0:
                    pe.wait_ge(sh_lo, (b + 1) * len(SH_CHUNKS))
                if u == 0:
                    pe.wait_ge(wsd_split, 1)
                await_(pe, sh_added, u - 1)
                for i in range(2):
                    cols = slice((2 * half + i) * P, (2 * half + i + 1) * P)
                    k = 0
                    for j, (_, size) in enumerate(SH_CHUNKS):
                        for h_part, w_part in PASSES:
                            mm = pe.matmul(ps_qk[:, u % 2, i * D:(i + 1) * D], sh[h_part][0:size, j, cols],
                                           wsd[w_part][0:size, j, :], start=k == 0, stop=k == 8)
                            k += 1
                mm.then_inc(sh_down, 1)

            def turn_keys():
                pe.wait_ge(keyed, 1)
                for t in range(TILES):
                    rows = slice(t // QT * E, (t // QT + 1) * E)
                    mm = pe.matmul(ps_vy[rows, t % QT * P:(t % QT + 1) * P], key[:, t, :], ident, start=True, stop=True)
                mm.then_inc(keys_turned, 1)

            def collect_lists():
                pe.wait_ge(listed, 1)
                for q in range(QUARTERS):
                    mm = pe.matmul(ps_o[0:E, q * CAP:(q + 1) * CAP], ident[:, q * E:(q + 1) * E], lists[:],
                                   start=True, stop=True)
                mm.then_inc(collected, 1)

            def spread_chosen():
                pe.wait_ge(chosen_done, 1)
                pe.wait_ge(pads_zeroed, 1)
                for e in range(2):
                    mm = pe.matmul(ps_vy[e * ROWS:(e + 1) * ROWS, 0:DUOS], chosen[:], ident[0:E, e:E:2],
                                   start=True, stop=True)
                mm.then_inc(spread, 1)

            for j in range(len(SH_CHUNKS)):
                shared_up(0, j)
            shared_up(1, 0)
            turn_keys()
            shared_down(0, 0)
            shared_down(0, 1)
            shared_up(1, 1)
            shared_up(1, 2)
            collect_lists()
            spread_chosen()
            shared_down(1, 0)
            shared_down(1, 1)

            def turn_rows(n):
                pe.wait_ge(gathered[n % TOKENS_RING], (n // TOKENS_RING + 1) * 16)
                await_(pe, xgT_done, n)
                for c in range(DC):
                    mm = pe.transpose(ps_s[0][:, c * P:(c + 1) * P], xg[n % TOKENS_RING][:, c * P:(c + 1) * P], ident)
                mm.then_inc(xg_turned, 1)

            def expert_up(n):
                pe.wait_ge(w_loaded[n % RING], (n // RING + 1) * 32)
                pe.wait_ge(xgT_done, n + 1)
                await_(pe, e_hidden, n - 1)
                for e in range(2):
                    rows = slice(e * ROWS, (e + 1) * ROWS)
                    for c in range(DC):
                        mm = pe.matmul(ps_t[n % 2][rows, 0:2 * I], xgT[n % 2][:, c, rows], wgu[n % RING][:, e, c, :],
                                       start=c == 0, stop=c == DC - 1)
                mm.then_inc(e_up, 1)

            def turn_hidden(n):
                pe.wait_ge(e_hidden, n + 1)
                await_(pe, ehT_done, n)
                for j in range(IJ):
                    mm = pe.transpose(ps_s[1][0:IW, j * P:(j + 1) * P], eh[n % 2][:, j * IW:(j + 1) * IW], ident)
                mm.then_inc(eh_turned, 1)

            def expert_down(n):
                pe.wait_ge(ehT_done, n + 1)
                await_(pe, e_scaled0, n - 1)
                await_(pe, e_scaled1, n - 1)
                for e in range(2):
                    rows = slice(e * ROWS, (e + 1) * ROWS)
                    for j in range(IJ):
                        mm = pe.matmul(ps_y[n % 2][rows, 0:D], ehT[n % 2][:, j, rows], wd[n % RING][:, e, j, :],
                                       start=j == 0, stop=j == IJ - 1)
                mm.then_inc(e_down, 1)

            def duo_slot(s):
                if 0 <= s < DUOS:
                    expert_up(s)
                if 0 <= s - 1 < DUOS:
                    turn_hidden(s - 1)
                if 0 <= s - 2 < DUOS:
                    expert_down(s - 2)
                if 0 <= s + 1 < DUOS:
                    turn_rows(s + 1)
                kind, b, part = next_step(s)
                if kind == "up":
                    shared_up(b, part)
                if kind == "down":
                    shared_down(b, part)

            pe.wait_ge(sh_product, FIRST_UPS)
            pe.wait_ge(rows_done, 1)

            for s in range(-1, DUOS + 2):
                duo_slot(s)

        @block.scalar
        def _(act):
            def exp(base, n, i):
                act.wait_ge(maxed, base * QT + (n * QT + i + 1))
                if i == 0:
                    await_(act, turned, base * QT + (n - 1) * QT)
                nc.scalar.activation(prob[n % 2][:, i, :], ps_s[i % 2][:], ACT.Exp, bias=neg_max[:, n % 2, i:i + 1],
                                     accum_out=row_sum[:, n % 2, i:i + 1]).then_inc(exped, 1)

            def split_o(base, n):
                act.wait_ge(mixed, base * QT + (n + 1) * QT)
                nc.scalar.copy(o[n % 4][0][:], ps_o[:]).then_inc(o_hi, 1)

            def split_pT(base, n, j):
                act.wait_ge(turned, base * QT + (n * QT + j + 1))
                await_(act, mixed, base * QT + (n * QT + j - 1))
                nc.scalar.copy(pT[j % 2][0][:], ps_t[j % 2][:]).then_inc(pT_hi, 1)

            def swap_qk(base, n, half):
                if half == 0:
                    act.wait_ge(qk_cosed, base + n + 1)
                    await_(act, qk_lo, base + n)
                    nc.scalar.copy(qk_rot[0:HALF, :, :], ps_qk[HALF:P, :, :])
                else:
                    nc.scalar.copy(qk_rot[HALF:P, :, :], ps_qk[0:HALF, :, :]).then_inc(qk_swapped, 1)

            def split_v(base, n, half):
                act.wait_ge(v_proj, base + n + half + 1)
                if half == 0:
                    await_(act, mixed, (base + (n - 2)) * QT)
                nc.scalar.copy(v[n // 2 % 2][0][:, 2 * half:2 * half + 2, :],
                               ps_vy[:].rearrange("p (j d) -> p j d", j=2)).then_inc(v_hi, 1)

            def slot(base, s):
                scoring, mixing, projecting = there(base, s), there(base, s - 1), there(base, s + 2)
                v_head, v_half = half_at(s, -1)
                if scoring:
                    exp(base, s, 0)
                if there(base, s - 2):
                    split_o(base, s - 2)
                if mixing:
                    split_pT(base, s - 1, 0)
                if scoring:
                    exp(base, s, 1)
                if mixing:
                    split_pT(base, s - 1, 1)
                if projecting:
                    swap_qk(base, s + 2, 0)
                if scoring:
                    exp(base, s, 2)
                if mixing:
                    split_pT(base, s - 1, 2)
                if projecting:
                    swap_qk(base, s + 2, 1)
                if there(base, v_head):
                    split_v(base, v_head, v_half)
                if mixing:
                    split_pT(base, s - 1, 3)
                if scoring:
                    exp(base, s, 3)

            pipeline(act, -2, slot)

            for loaded, whole, parts, done in ((gate_loaded, gate_raw, gate, gate_hi_done), (wsg_loaded, wsg_raw, wsg, wsg_hi_done),
                                               (wsd_loaded, wsd_raw, wsd, wsd_hi_done)):
                act.wait_ge(loaded, 16)
                nc.scalar.copy(parts[0][:], whole[:]).then_inc(done, 1)
            for t in range(TILES + 2):
                if t < TILES:
                    act.wait_ge(r_stats, t + 1)
                    nc.scalar.activation(std[:, t:t + 1], moments[:, t, 1:2], ACT.Sqrt, bias=eps).then_inc(r_std, 1)
                if 0 <= t - 2:
                    u = t - 2
                    act.wait_ge(x1_turned, u + 1)
                    nc.scalar.copy(x[0][:, :, u * P:(u + 1) * P],
                                   ps_t[u % 2][:, 0:D].rearrange("p (c t) -> p c t", c=DC)).then_inc(x1T_hi, 1)

            def shared_act(m):
                size = SH_CHUNKS[m % len(SH_CHUNKS)][1]
                act.wait_ge(sh_projected, m + 1)
                await_(act, sh_product, m - 1)
                nc.scalar.activation(sh_gate[m % 2][0:size, :], shared_banks(m)[0][0:size, :], ACT.Silu).then_inc(sh_silu, 1)

            def shared_split(m):
                b, j = divmod(m, len(SH_CHUNKS))
                size = SH_CHUNKS[j][1]
                act.wait_ge(sh_product, m + 1)
                await_(act, sh_down, 2 * b)
                nc.scalar.copy(sh[0][0:size, j, :], sh_up[m % 2][0:size, :]).then_inc(sh_hi, 1)

            def softmax_exp():
                act.wait_ge(shifted, 1)
                nc.scalar.activation(expd[:], expd[:], ACT.Exp).then_inc(softexp, 1)

            for m in range(FIRST_UPS + 1):
                if m < FIRST_UPS:
                    shared_act(m)
                if m > 0:
                    shared_split(m - 1)
                if m == 3:
                    softmax_exp()

            def expert_silu(n):
                act.wait_ge(e_up, n + 1)
                await_(act, e_hidden, n - 1)
                nc.scalar.activation(eg[n % 2][:], ps_t[n % 2][:, 0:I], ACT.Silu).then_inc(e_silu, 1)

            def keep_hidden(n):
                act.wait_ge(eh_turned, n + 1)
                await_(act, e_down, n - 1)
                nc.scalar.copy(ehT[n % 2][:], ps_s[1][0:IW, 0:IJ * P].rearrange("p (j r) -> p j r", j=IJ)).then_inc(ehT_done, 1)

            def scale_rows(n):
                act.wait_ge(e_down, n + 1)
                await_(act, summed, 16 * (n - 1))
                col = D + 2 * n + 1
                nc.scalar.activation(ey[n % 2][ROWS:P, :], ps_y[n % 2][ROWS:P, 0:D], ACT.Copy,
                                     scale=xg[n % TOKENS_RING][ROWS:P, col:col + 1]).then_inc(e_scaled1, 1)

            def duo_slot(s):
                kind, b, part = next_step(s - 1)
                if kind == "up":
                    shared_act(b * len(SH_CHUNKS) + part)
                kind, b, part = next_step(s - 2)
                if kind == "up":
                    shared_split(b * len(SH_CHUNKS) + part)
                if 0 <= s < DUOS:
                    expert_silu(s)
                if 0 <= s - 1 < DUOS:
                    keep_hidden(s - 1)
                if 0 <= s - 2 < DUOS:
                    scale_rows(s - 2)

            for s in range(-1, DUOS + 2):
                duo_slot(s)

            for q in range(QUARTERS + 1):
                if q < QUARTERS:
                    tiles = slice(q * QT, (q + 1) * QT)
                    act.wait_ge(f_stats, q + 1)
                    nc.scalar.activation(std[:, tiles], moments[:, tiles, 1], ACT.Sqrt, bias=eps).then_inc(f_std, 1)
                if q > 0:
                    act.wait_ge(f_shift, q)
                    for t in range((q - 1) * QT, q * QT):
                        normed_tile = nc.scalar.activation(x1[:, t, :], routed[:, 0, t, :], ACT.Identity,
                                                           scale=rstd[:, t:t + 1], bias=shift[:, t:t + 1])
                    normed_tile.then_inc(f_done, 1)

        @block.vector
        def _(dve):
            def row_max(base, n, i):
                dve.wait_ge(scored, base * QT + (n * QT + i + 1))
                nc.vector.tensor_reduce(neg_max[:, n % 2, i:i + 1], ps_s[i % 2][:], AX.X, ALU.max,
                                        negate=True).then_inc(maxed, 1)

            def invert(base, n, i):
                dve.wait_ge(exped, base * QT + (n * QT + i + 1))
                nc.vector.reciprocal(inv_sum[:, n % 2, i:i + 1], row_sum[:, n % 2, i:i + 1]).then_inc(inverted, 1)

            def normalise(base, n, i):
                dve.wait_ge(inverted, base * QT + (n * QT + i + 1))
                nc.vector.tensor_scalar(prob[n % 2][:, i, :], prob[n % 2][:, i, :], inv_sum[:, n % 2, i:i + 1], None,
                                        ALU.mult).then_inc(normed, 1)

            def rest(out, whole, hi):
                return nc.vector.tensor_tensor(out, whole, hi.bitcast(F32), ALU.subtract)

            def split_o(base, n):
                dve.wait_ge(o_hi, base + n + 1)
                rest(o[n % 4][1][:], ps_o[:], o[n % 4][0][:]).then_inc(o_lo, 1)

            def split_pT(base, n, j):
                dve.wait_ge(pT_hi, base * QT + (n * QT + j + 1))
                rest(pT[j % 2][1][:], ps_t[j % 2][:], pT[j % 2][0][:]).then_inc(pT_lo, 1)

            def cos_qk(base, n):
                dve.wait_ge(qk_proj, base + n + 1)
                await_(dve, qk_sum, base + n)
                nc.vector.tensor_tensor(qk_cos[:], ps_qk[:], rope[:, 0], ALU.mult).then_inc(qk_cosed, 1)

            def split_qk(base, n):
                dve.wait_ge(qk_sum, base + n + 1)
                await_(dve, scored, (base + (n - 1)) * QT)
                nc.vector.tensor_copy(qk[n % 2][0][:], qk_rot[:]).then_inc(qk_hi, 1)

            def split_v(base, n, half):
                dve.wait_ge(v_hi, base + n + half + 1)
                rows = slice(2 * half, 2 * half + 2)
                rest(v[n // 2 % 2][1][:, rows, :], ps_vy[:].rearrange("p (j d) -> p j d", j=2),
                     v[n // 2 % 2][0][:, rows, :]).then_inc(v_lo, 1)

            def add_y(base, n, half):
                b = n // 2 % B
                dve.wait_ge(y_proj, base + n + half + 1)
                into = acc[:, half, b * S:(b + 1) * S]
                nc.vector.tensor_tensor(into, ps_vy[:], into, ALU.add).then_inc(y_added, 1)

            def split_wqk(base, n):
                dve.wait_ge(wqk_in_s, 16 * (pair(base, n) + 1))
                await_(dve, qk_proj, base + n)
                nc.vector.tensor_copy(wqk[0][:], wqk_raw[:]).then_inc(wqk_hi, 1)

            def split_wv(base, n):
                dve.wait_ge(wv_in_s, 16 * (pair(base, n) + 1))
                await_(dve, v_proj, base + n)
                nc.vector.tensor_copy(wv[0][:], wv_raw[:]).then_inc(wv_hi, 1)

            def split_wo(base, n):
                dve.wait_ge(wo_in_s, 16 * (pair(base, n) + 1))
                await_(dve, y_proj, base + n)
                nc.vector.tensor_copy(wo[0][:], wo_raw[:]).then_inc(wo_hi, 1)

            def slot(base, s):
                scoring, mixing = there(base, s), there(base, s - 1)
                y_head, y_half = half_at(s, 3)
                v_head, v_half = half_at(s, -1)
                if mixing:
                    invert(base, s - 1, 3)
                if scoring:
                    row_max(base, s, 0)
                if mixing:
                    normalise(base, s - 1, 3)
                if there(base, s + 1) and s > -2:
                    split_qk(base, s + 1)
                if s % PER_PAIR == PER_PAIR - 1 and there(base, s + 1):
                    split_wv(base, s + 1)
                if there(base, s - 2):
                    split_o(base, s - 2)
                if scoring:
                    row_max(base, s, 1)
                if mixing:
                    split_pT(base, s - 1, 0)
                if there(base, s + 2):
                    cos_qk(base, s + 2)
                if scoring:
                    row_max(base, s, 2)
                    invert(base, s, 0)
                if s % PER_PAIR == PER_PAIR - 3 and there(base, s + 3):
                    split_wqk(base, s + 3)
                if mixing:
                    split_pT(base, s - 1, 1)
                if scoring:
                    normalise(base, s, 0)
                if there(base, y_head):
                    add_y(base, y_head, y_half)
                if scoring:
                    invert(base, s, 1)
                if s % PER_PAIR == 2 and there(base, s - 2):
                    split_wo(base, s - 2)
                if scoring:
                    invert(base, s, 2)
                    normalise(base, s, 1)
                if mixing:
                    split_pT(base, s - 1, 2)
                if scoring:
                    normalise(base, s, 2)
                    row_max(base, s, 3)
                if there(base, v_head):
                    split_v(base, v_head, v_half)
                if mixing:
                    split_pT(base, s - 1, 3)

            def pair(base, n):
                return base // PER_PAIR + n // PER_PAIR if isinstance(base, int) else pair_reg[0] + n // PER_PAIR

            pair_reg = [0]
            for b in range(B):
                if b == 0:
                    dve.wait_ge(wqk_in_s, 16)
                    nc.vector.tensor_copy(wqk[0][:], wqk_raw[:]).then_inc(wqk_hi, 1)
                dve.wait_ge(x_in[b], 16)
                cols = slice(b * S, (b + 1) * S)
                nc.vector.tensor_copy(x[0][:, :, cols], acc[:, :, cols]).then_inc(x_hi, 1)
            dve.wait_ge(const_in, 32)
            for s in range(-2, 4):
                slot(0, s)
            with dve.Fori(0, PAIRS - 1) as pair_index:
                pair_reg[0] = pair_index
                for s in range(4, 4 + PER_PAIR):
                    slot(pair_index * PER_PAIR, s)
            for s in range(4, 11):
                slot((PAIRS - 1) * PER_PAIR, s)

            steps = [0]

            def link(instruction):
                steps[0] += 1
                instruction.then_inc(dve_step, 1)
                dve.wait_ge(dve_step, steps[0])

            def split_low(hi_done, whole, parts, done):
                dve.wait_ge(hi_done, 1)
                rest(parts[1][:], whole[:], parts[0][:]).then_inc(done, 1)

            for t in range(TILES + 3):
                if t < TILES:
                    dve.wait_ge(r_turned, t + 1)
                    link(nc.vector.bn_stats(stats[:, t, :], ps_s[t % 2][:, 0:D]))
                    nc.vector.bn_aggr(moments[:, t, :], stats[:, t, :]).then_inc(r_stats, 1)
                if 0 <= t - 1 < TILES:
                    u = t - 1
                    dve.wait_ge(r_std, u + 1)
                    nc.vector.reciprocal(rstd[:, u:u + 1], std[:, u:u + 1]).then_inc(r_rstd, 1)
                    dve.wait_ge(r_rstd, u + 1)
                    nc.vector.tensor_scalar(x1[:, u, :], ps_s[u % 2][:, 0:D], moments[:, u, 0:1], rstd[:, u:u + 1],
                                            ALU.subtract, ALU.mult).then_inc(x1_done, 1)
                if 0 <= t - 3:
                    u = t - 3
                    dve.wait_ge(x1T_hi, u + 1)
                    rest(x[1][:, :, u * P:(u + 1) * P], ps_t[u % 2][:, 0:D].rearrange("p (c t) -> p c t", c=DC),
                         x[0][:, :, u * P:(u + 1) * P]).then_inc(x1T_lo, 1)
                if t == 1:
                    split_low(gate_hi_done, gate_raw, gate, gate_split)
                if t == 5:
                    split_low(wsg_hi_done, wsg_raw, wsg, wsg_split)
                if t == 9:
                    split_low(wsd_hi_done, wsd_raw, wsd, wsd_split)

            def over_group(ap, n):
                return ap.unsqueeze(2).broadcast_to([P, ap.shape[1], n])

            def add_shared(u):
                dve.wait_ge(sh_down, u + 1)
                if u == 0:
                    dve.wait_ge(x1_tabled, 16)
                into = x1[:, 2 * u:2 * u + 2, :]
                nc.vector.tensor_tensor(into, ps_qk[:, u % 2, :].rearrange("p (t d) -> p t d", t=2), into,
                                        ALU.add).then_inc(sh_added, 1)

            def shared_product(m):
                size = SH_CHUNKS[m % len(SH_CHUNKS)][1]
                dve.wait_ge(sh_silu, m + 1)
                await_(dve, sh_lo, m - 1)
                nc.vector.tensor_tensor(sh_up[m % 2][0:size, :], shared_banks(m)[1][0:size, :],
                                        sh_gate[m % 2][0:size, :], ALU.mult).then_inc(sh_product, 1)

            def first_keys(source, out, rows, spare, done):
                link(nc.vector.tensor_copy(spare[1], source))
                source = spare[1]
                for r in range(CAP // TOP):
                    highest = out[rows, r * TOP:(r + 1) * TOP]
                    if r == CAP // TOP - 1:
                        nc.vector.max(highest, source).then_inc(done, 1)
                    else:
                        link(nc.vector.max(highest, source))
                        rest_of = spare[r % 2]
                        link(nc.vector.scalar_tensor_tensor(out=rest_of, in0=source, scalar=highest[:, TOP - 1:TOP],
                                                            in1=source, op0=ALU.is_lt, op1=ALU.mult))
                        source = rest_of

            dve.wait_ge(gated, TILES)
            link(nc.vector.tensor_copy(logits[:].rearrange("p t e -> p (t e)"), ps_o[:]))
            by_group = logits[:].rearrange("p t (g j) -> p (t g) j", g=GROUPS)
            link(nc.vector.tensor_reduce(group_max[:], by_group, AX.X, ALU.max))
            maxima = group_max[:].rearrange("p (t g) -> p t g", g=GROUPS)
            others = maxima.unsqueeze(2).broadcast_to([P, TILES, GROUPS, GROUPS])
            own = maxima.unsqueeze(3).broadcast_to([P, TILES, GROUPS, GROUPS])
            square = lambda a: a[:].rearrange("p (t g h) -> p t g h", g=GROUPS, h=GROUPS)
            nc.vector.tensor_tensor(square(above), others, own, ALU.is_gt)
            link(nc.vector.tensor_tensor(square(equal), others, own, ALU.is_equal))
            rows64 = lambda a: a[:].rearrange("p (t q) -> p t q", t=TILES)
            link(nc.vector.tensor_tensor(rows64(equal), rows64(equal),
                                         tri.unsqueeze(1).broadcast_to([P, TILES, GROUPS * GROUPS]), ALU.mult))
            link(nc.vector.tensor_tensor(above[:], above[:], equal[:], ALU.add))
            shared_product(0)
            link(nc.vector.tensor_reduce(group_rank[:], above[:].rearrange("p (g h) -> p g h", h=GROUPS), AX.X, ALU.add))
            masked_by_group = masked[:].rearrange("p t (g j) -> p (t g) j", g=GROUPS)
            link(nc.vector.scalar_tensor_tensor(out=masked_by_group, in0=over_group(group_rank[:], E // GROUPS),
                                                scalar=float(KEPT), in1=by_group, op0=ALU.is_lt, op1=ALU.mult))
            for t in range(TILES):
                top8 = nc.vector.max(top[:, t, :], masked[:, t, :])
            link(top8)
            nc.vector.tensor_tensor(expd[:], masked[:], top[:, :, 0:1].broadcast_to([P, TILES, E]),
                                    ALU.subtract).then_inc(shifted, 1)
            sixth = top[:, :, PICKED - 1:PICKED].broadcast_to([P, TILES, E])
            nc.vector.tensor_tensor(over[:], masked[:], sixth, ALU.is_gt)
            link(nc.vector.tensor_tensor(same[:], masked[:], sixth, ALU.is_equal))
            shared_product(1)
            nc.vector.tensor_reduce(n_over[:], over[:], AX.X, ALU.add)
            link(nc.vector.tensor_tensor_scan(upto[:].rearrange("p t e -> p (t e)"), resets,
                                              same[:].rearrange("p t e -> p (t e)"), 0.0, ALU.mult, ALU.add))
            link(nc.vector.tensor_tensor(upto[:], upto[:], over_group(n_over[:], E), ALU.add))
            link(nc.vector.scalar_tensor_tensor(out=upto[:], in0=upto[:], scalar=float(PICKED), in1=same[:],
                                                op0=ALU.is_le, op1=ALU.mult))
            link(nc.vector.tensor_tensor(picked[:], over[:], upto[:], ALU.add))
            nc.vector.tensor_tensor(key[:], picked[:], over_group(countdown, E), ALU.mult).then_inc(keyed, 1)
            shared_product(2)
            shared_product(3)
            dve.wait_ge(softexp, 1)
            link(nc.vector.tensor_reduce(total[:], expd[:], AX.X, ALU.add))
            link(nc.vector.reciprocal(inv_total[:], total[:]))
            link(nc.vector.tensor_tensor(weight[:], expd[:], over_group(inv_total[:], E), ALU.mult))
            nc.vector.scalar_tensor_tensor(out=weight[:], in0=weight[:], scalar=SCALE, in1=picked[:],
                                           op0=ALU.mult, op1=ALU.mult).then_inc(weighted, 1)

            dve.wait_ge(keys_turned, 1)
            first_keys(ps_vy[:], lists, slice(0, P), [a[:] for a in left], listed)
            add_shared(0)
            add_shared(1)
            shared_product(4)
            dve.wait_ge(collected, 1)
            first_keys(ps_o[0:E, 0:QUARTERS * CAP], chosen, slice(0, E), [a[0:E, 0:QUARTERS * CAP] for a in left],
                       chosen_done)
            shared_product(5)
            dve.wait_ge(spread, 1)
            link(nc.vector.tensor_copy(found[:], ps_vy[:, 0:DUOS]))
            nc.vector.tensor_scalar(counted[:], found[:], -1.0, float(T), ALU.mult, ALU.add)
            nc.vector.tensor_scalar(vacant[:], found[:], 0.0, None, ALU.is_le)
            link(nc.vector.tensor_scalar(taken[:], found[:], 0.0, None, ALU.is_gt))
            link(nc.vector.tensor_tensor(token[:], counted[:], taken[:], ALU.mult))
            nc.vector.tensor_copy(gather_row[:], token[:])
            link(nc.vector.scalar_tensor_tensor(out=row[:], in0=vacant[:], scalar=empty_row, in1=token[:],
                                                op0=ALU.mult, op1=ALU.add))
            nc.vector.tensor_scalar(add_row[:], row[:], region_of, None, ALU.add).then_inc(rows_done, 1)
            add_shared(2)
            add_shared(3)

            def keep_rows(n):
                dve.wait_ge(xg_turned, n + 1)
                await_(dve, e_up, n - 1)
                nc.vector.tensor_copy(xgT[n % 2][:], ps_s[0][:, 0:D].rearrange("p (c r) -> p c r", c=DC)).then_inc(xgT_done, 1)

            def hidden(n):
                dve.wait_ge(e_silu, n + 1)
                await_(dve, eh_turned, n - 1)
                nc.vector.tensor_tensor(eh[n % 2][:], ps_t[n % 2][:, I:2 * I], eg[n % 2][:], ALU.mult).then_inc(e_hidden, 1)

            def scale_rows(n):
                dve.wait_ge(e_down, n + 1)
                await_(dve, summed, 16 * (n - 1))
                col = D + 2 * n
                nc.vector.tensor_scalar(ey[n % 2][0:ROWS, :], ps_y[n % 2][0:ROWS, 0:D],
                                        xg[n % TOKENS_RING][0:ROWS, col:col + 1], None, ALU.mult).then_inc(e_scaled0, 1)

            def duo_slot(s):
                kind, b, part = next_step(s - 1)
                if kind == "up":
                    shared_product(b * len(SH_CHUNKS) + part)
                if kind == "down":
                    add_shared(2 * b + part)
                if 0 <= s < DUOS:
                    hidden(s)
                if 0 <= s - 2 < DUOS:
                    scale_rows(s - 2)
                if 0 <= s + 1 < DUOS:
                    keep_rows(s + 1)

            for s in range(-1, DUOS + 2):
                duo_slot(s)

            for q in range(QUARTERS + 1):
                if q < QUARTERS:
                    tiles = slice(q * QT, (q + 1) * QT)
                    dve.wait_ge(f_based, q + 1)
                    nc.vector.tensor_tensor(routed[:, 0, tiles, :], routed[:, 0, tiles, :], routed[:, 1, tiles, :],
                                            ALU.add).then_inc(f_sum, 1)
                    dve.wait_ge(f_sum, q + 1)
                    for t in range(q * QT, (q + 1) * QT):
                        raw = nc.vector.bn_stats(stats[:, t, :], routed[:, 0, t, :])
                    raw.then_inc(f_raw, 1)
                    dve.wait_ge(f_raw, q + 1)
                    for t in range(q * QT, (q + 1) * QT):
                        aggregated = nc.vector.bn_aggr(moments[:, t, :], stats[:, t, :])
                    aggregated.then_inc(f_stats, 1)
                if q > 0:
                    tiles = slice((q - 1) * QT, q * QT)
                    dve.wait_ge(f_std, q)
                    nc.vector.reciprocal(rstd[:, tiles], std[:, tiles]).then_inc(f_rstd, 1)
                    dve.wait_ge(f_rstd, q)
                    nc.vector.scalar_tensor_tensor(out=shift[:, tiles], in0=moments[:, tiles, 0], scalar=-1.0,
                                                   in1=rstd[:, tiles], op0=ALU.mult, op1=ALU.mult).then_inc(f_shift, 1)

        @block.gpsimd
        def _(pool):
            def rest(out, whole, hi):
                return nc.gpsimd.tensor_tensor(out, whole, hi.bitcast(F32), ALU.subtract)

            def rotate_qk(base, n):
                pool.wait_ge(qk_swapped, base + n + 1)
                nc.gpsimd.tensor_tensor(qk_rot[:], qk_rot[:], rope[:, 1], ALU.mult).then_inc(qk_sined, 1)
                pool.wait_ge(qk_sined, base + n + 1)
                nc.gpsimd.tensor_tensor(qk_rot[:], qk_rot[:], qk_cos[:], ALU.add).then_inc(qk_sum, 1)

            def split_qk(base, n):
                pool.wait_ge(qk_hi, base + n + 1)
                rest(qk[n % 2][1][:], qk_rot[:], qk[n % 2][0][:]).then_inc(qk_lo, 1)

            def split_weights(base, s):
                if s % PER_PAIR == PER_PAIR - 3 and there(base, s + 3):
                    pool.wait_ge(wqk_hi, pair(base, s + 3) + 1)
                    rest(wqk[1][:], wqk_raw[:], wqk[0][:]).then_inc(wqk_lo, 1)
                if s % PER_PAIR == PER_PAIR - 1 and there(base, s + 1):
                    pool.wait_ge(wv_hi, pair(base, s + 1) + 1)
                    rest(wv[1][:], wv_raw[:], wv[0][:]).then_inc(wv_lo, 1)
                if s % PER_PAIR == 2 and there(base, s - 2):
                    pool.wait_ge(wo_hi, pair(base, s - 2) + 1)
                    rest(wo[1][:], wo_raw[:], wo[0][:]).then_inc(wo_lo, 1)

            def slot(base, s):
                if there(base, s + 1) and s > -2:
                    split_qk(base, s + 1)
                split_weights(base, s)
                if there(base, s + 2):
                    rotate_qk(base, s + 2)

            def pair(base, n):
                return base // PER_PAIR + n // PER_PAIR if isinstance(base, int) else pair_reg[0] + n // PER_PAIR

            pair_reg = [0]
            nc.gpsimd.memset(zeros[:], 0.0).then_inc(zeroed, 1)
            for b in range(B):
                if b == 0:
                    pool.wait_ge(wqk_hi, 1)
                    rest(wqk[1][:], wqk_raw[:], wqk[0][:]).then_inc(wqk_lo, 1)
                pool.wait_ge(x_hi, b + 1)
                cols = slice(b * S, (b + 1) * S)
                rest(x[1][:, :, cols], acc[:, :, cols], x[0][:, :, cols]).then_inc(x_lo, 1)
            for s in range(-2, 4):
                slot(0, s)
            with pool.Fori(0, PAIRS - 1) as pair_index:
                pair_reg[0] = pair_index
                for s in range(4, 4 + PER_PAIR):
                    slot(pair_index * PER_PAIR, s)
            for s in range(4, 11):
                slot((PAIRS - 1) * PER_PAIR, s)

            pool.wait_ge(y_added, HEADS)
            nc.gpsimd.memset(chosen[:, CAP:ROWS], 0.0).then_inc(pads_zeroed, 1)

            def shared_low(m):
                j = m % len(SH_CHUNKS)
                size = SH_CHUNKS[j][1]
                pool.wait_ge(sh_hi, m + 1)
                rest(sh[1][0:size, j, :], sh_up[m % 2][0:size, :], sh[0][0:size, j, :]).then_inc(sh_lo, 1)

            for m in range(FIRST_UPS):
                shared_low(m)

            def gather(n):
                if n >= TOKENS_RING:
                    pool.wait_ge(e_scaled0, n - TOKENS_RING + 1)
                    pool.wait_ge(e_scaled1, n - TOKENS_RING + 1)
                nc.gpsimd.indirect_dma_start(out=xg[n % TOKENS_RING][:], out_offset=None, in_=table,
                                             in_offset=bass.IndirectOffsetOnAxis(gather_row[:, n:n + 1], 0)
                                             ).then_inc(gathered[n % TOKENS_RING], 16)

            pool.wait_ge(rows_done, 1)
            pool.wait_ge(x1_tabled, 16)
            pool.wait_ge(weight_tabled, 16)
            for n in range(TOKENS_RING):
                gather(n)
            pool.wait_ge(cleared, 16 * (2 * REGION // (ZERO_ROWS * P)))
            for n in range(DUOS):
                kind, b, part = next_step(n)
                if kind == "up":
                    shared_low(b * len(SH_CHUNKS) + part)
                pool.wait_ge(e_scaled0, n + 1)
                pool.wait_ge(e_scaled1, n + 1)
                if n:
                    pool.wait_ge(summed, 16 * n)
                nc.gpsimd.indirect_dma_start(out=sums, out_offset=bass.IndirectOffsetOnAxis(add_row[:, n:n + 1], 0),
                                             in_=ey[n % 2][:], in_offset=None, compute_op=ALU.add).then_inc(summed, 16)
                if n + TOKENS_RING < DUOS:
                    gather(n + TOKENS_RING)

            pool.wait_ge(sh_added, TILES // 2)
            for q in range(QUARTERS):
                tiles = slice(q * QT, (q + 1) * QT)
                pool.wait_ge(sums_in[q], 32)
                nc.gpsimd.tensor_tensor(routed[:, 1, tiles, :], routed[:, 1, tiles, :], x1[:, tiles, :],
                                        ALU.add).then_inc(f_based, 1)



def _constants():
    import numpy as np

    inv_freq = 1.0 / 10000.0 ** (np.arange(0, DH, 2, dtype=np.float32) / DH)
    angle = (np.arange(S, dtype=np.float32)[:, None] * inv_freq[None].astype(np.float32)).T
    angle = np.concatenate([angle, angle])
    cos = np.cos(angle)
    sin = np.sin(angle) * np.where(np.arange(DH) < HALF, -1.0, 1.0)[:, None]
    scale = DH ** -0.5
    rope = np.stack([np.stack([cos * scale, cos], 1), np.stack([sin * scale, sin], 1)], 1)

    p = np.arange(P)
    g = np.arange(GROUPS)
    ident = np.eye(P)
    tri = np.broadcast_to((g[None, :] < g[:, None]).reshape(-1), (P, GROUPS * GROUPS))
    resets = np.broadcast_to(np.tile(np.arange(E) > 0, TILES), (P, TILES * E))
    countdown = T - (np.arange(TILES)[None, :] * P + p[:, None])
    empty_row = (T + p % ROWS)[:, None]
    region_of = (REGION * (p >= ROWS))[:, None]
    eps = np.full((P, 1), EPS)
    const = np.concatenate([ident, tri, resets, countdown, empty_row, region_of, eps], 1)

    return rope.astype(np.float32), const.astype(np.float32)


def kernel(L0_attn_x, L0_attn_w_qkv, L0_attn_w_out, L0_ffn_gate_w, L0_ffn_w_gate_up, L0_ffn_w_down,
           L0_ffn_ws_gate_up, L0_ffn_ws_down):
    import numpy as np
    import concourse.bacc as bacc
    from concourse.bass_utils import run_bass_kernel_spmd

    qkv = np.asarray(L0_attn_w_qkv).reshape(3, H // 2, 2, DH, DC, P)
    shared_down = np.zeros((len(SH_CHUNKS) * P, D), np.float32)
    shared_down[:SH] = np.asarray(L0_ffn_ws_down)
    rope, const = _constants()
    arrays = {
        "xT": np.asarray(L0_attn_x).reshape(T, DC, P).transpose(2, 1, 0),
        "wqk": qkv[:2].transpose(1, 5, 4, 0, 2, 3).reshape(H // 2, P, DC, 4 * DH),
        "wv": qkv[2].transpose(0, 4, 3, 1, 2).reshape(H // 2, P, DC, 2 * DH),
        "wo": np.asarray(L0_attn_w_out).reshape(D, H // 2, 2, DH).transpose(1, 3, 2, 0),
        "rope": rope,
        "gate": np.asarray(L0_ffn_gate_w).reshape(E, DC, P).transpose(2, 1, 0),
        "wsg": np.asarray(L0_ffn_ws_gate_up).reshape(DC, P, 2 * SH).transpose(1, 0, 2),
        "wsd": shared_down.reshape(len(SH_CHUNKS), P, D).transpose(1, 0, 2),
        "wgu": np.asarray(L0_ffn_w_gate_up).reshape(DUOS, 2, DC, P, 2 * I).transpose(0, 3, 1, 2, 4),
        "wd": np.asarray(L0_ffn_w_down).reshape(DUOS, 2, IJ, IW, D).transpose(0, 3, 1, 2, 4),
        "const": const,
    }
    arrays = {f"in_{name}": np.ascontiguousarray(a) for name, a in arrays.items()}

    nc = bacc.Bacc("TRN2", target_bir_lowering=False, num_devices=1)
    args = [nc.dram_tensor(name, a.shape, mybir.dt.from_np(a.dtype), kind="ExternalInput").ap()
            for name, a in arrays.items()]
    out = nc.dram_tensor("out_0", (T, D), F32, kind="ExternalOutput").ap()
    layer(nc, *args, out)
    r = run_bass_kernel_spmd(nc, [arrays], core_ids=[0])
    return r.results[0]["out_0"].reshape(B, S, D)
```

```python
from contextlib import ExitStack

import concourse.bass as bass
from concourse import mybir

F32 = mybir.dt.float32
F32R = mybir.dt.float32r
U32 = mybir.dt.uint32
ALU = mybir.AluOpType
ACT = mybir.ActivationFunctionType
AX = mybir.AxisListType

P = 128
B, S, D = 4, 512, 256
T = B * S
DC = D // P
H, DH = 16, 128
HALF = DH // 2
PAIRS = H // 2
QT = S // P
HEADS = B * PAIRS * 2
PER_PAIR = 2 * B

TILES = T // P
QUARTERS = TILES // QT
E, I = 32, 176
GROUPS, KEPT = 8, 3
PICKED = 6
SCALE = 16.0
CAP = 48
ROWS = 64
DUOS = E // 2
IJ, IW = 2, I // 2
SH = 2 * I
SH_CHUNKS = [(f, min(P, SH - f)) for f in range(0, SH, P)]
EPS = 1e-5
XW = D + E
REGION = T + ROWS
ZERO_ROWS = 11
CLEARINGS = 2 * REGION // (ZERO_ROWS * P)
TOP = 8
RING = 6
RING_EARLY = 4
TOKENS_RING = 8

CONST_AT = [0]
for _width in (P, TILES * GROUPS, TILES * E, TILES, 1, 1, 1):
    CONST_AT.append(CONST_AT[-1] + _width)
CONSTS = CONST_AT[-1]

PASSES = ((1, 0), (0, 1), (0, 0))

NEXT_STEPS = [("up", 2, 2), None, None, ("down", 2, 0), None, ("down", 2, 1), None, ("up", 3, 0), None,
              ("up", 3, 1), None, ("up", 3, 2), None, None, ("down", 3, 0), ("down", 3, 1)]
FIRST_UPS = 2 * len(SH_CHUNKS) + 2

COUPLES = TILES // 2
NORM_STEPS = [range(1), range(1, COUPLES + 4)]
X_SPLITS = {0: 1, 2: 2}
LAST = (PAIRS - 1) * PER_PAIR


def layer(nc, xT_in, wqk_in, wv_in, wo_in, rope_in, gate_in, wsg_in, wsd_in, wgu_in, wd_in, const_in_, out):
    with ExitStack() as ctx:
        scope = [ctx]

        def sb(name, shape, dt=F32):
            return scope[0].enter_context(nc.sbuf_tensor(name, shape, dt))

        def pair_of(name, shape):
            return [sb(name + part, shape, F32R) for part in ("_hi", "_lo")]

        def bank(name, dt=F32):
            return ctx.enter_context(nc.psum_tensor(name, [P, 512], dt))

        def sem(name):
            return ctx.enter_context(nc.semaphore(name))

        acc = sb("acc", [P, DC, T])
        x = pair_of("x", [P, DC, T])
        consts = sb("consts", [P, CONSTS])
        ident, group_resets, resets, countdown, empty_row, region_of, eps = [
            consts[:, a:b] for a, b in zip(CONST_AT, CONST_AT[1:])]
        x1 = sb("x1", [P, TILES, D])
        gate_raw = sb("gate_raw", [P, DC, E])
        gate_parts = sb("gate_parts", [P, DC, 2, E], F32R)
        gate = [gate_parts[:, :, part, :] for part in range(2)]
        wsg_raw, wsg = sb("wsg_raw", [P, DC, 2 * SH]), pair_of("wsg", [P, DC, 2 * SH])
        wsd_raw, wsd = sb("wsd_raw", [P, len(SH_CHUNKS), D]), pair_of("wsd", [P, len(SH_CHUNKS), D])
        stats = sb("stats", [P, TILES, 6])
        moments = sb("moments", [P, TILES, 2])
        std, rstd, shift = [sb(n, [P, TILES]) for n in ("std", "rstd", "shift")]
        attention_only = ExitStack()
        scope[0] = attention_only
        rope = sb("rope", [P, 2, 2, S])
        wqk_raw = sb("wqk_raw", [P, DC, 4 * DH])
        wv_raw = sb("wv_raw", [P, DC, 2 * DH])
        wo_raw = sb("wo_raw", [P, 2, D])
        wqk = pair_of("wqk", [P, DC, 4 * DH])
        wv = pair_of("wv", [P, DC, 2 * DH])
        wo = pair_of("wo", [P, 2, D])
        qk_cos = sb("qk_cos", [P, 2, S])
        qk_rot = sb("qk_rot", [P, 2, S])
        qk = [pair_of(f"qk{i}", [P, 2, S]) for i in range(2)]
        v = [pair_of(f"v{i}", [P, QT, 2 * DH]) for i in range(2)]
        prob = [sb(f"prob{i}", [P, QT, S]) for i in range(2)]
        neg_max = sb("neg_max", [P, 2, QT])
        row_sum = sb("row_sum", [P, 2, QT])
        inv_sum = sb("inv_sum", [P, 2, QT])
        pT = [pair_of(f"pT{i}", [P, S]) for i in range(2)]
        o = [pair_of(f"o{i}", [P, S]) for i in range(4)]

        attention_only.close()

        scope[0] = ctx
        sh_gate, sh_up = [[sb(f"sh_{n}{i}", [P, S]) for i in range(2)] for n in ("gate", "up")]
        sh = pair_of("sh", [P, len(SH_CHUNKS), S])
        logits = sb("logits", [P, TILES, E])
        group_max, group_kept = [sb(n, [P, TILES, GROUPS]) for n in ("group_max", "group_kept")]
        masked = sb("masked", [P, TILES, E])
        top = sb("top", [P, TILES, 8])
        expd = sb("expd", [P, TILES, E])
        over, same, upto = [sb(n, [P, TILES, E]) for n in ("over", "same", "upto")]
        n_over, total, inv_total = [sb(n, [P, TILES]) for n in ("n_over", "total", "inv_total")]
        picked = sb("picked", [P, TILES, E])
        weight = sb("weight", [P, TILES, E])
        key = sb("key", [P, TILES, E])
        left = [sb(f"left{i}", [P, S]) for i in range(2)]
        lists = sb("lists", [P, CAP])
        chosen = sb("chosen", [E, ROWS])
        found = sb("found", [P, DUOS])
        taken, counted, token, vacant, row = [sb(n, [P, DUOS]) for n in ("taken", "counted", "token", "vacant", "row")]
        gather_row, add_row = sb("gather_row", [P, DUOS], U32), sb("add_row", [P, DUOS], U32)
        xg = [sb(f"xg{i}", [P, XW]) for i in range(TOKENS_RING)]
        xgT = [sb(f"xgT{i}", [P, DC, P]) for i in range(2)]
        eg = [sb(f"eg{i}", [P, I]) for i in range(2)]
        eh = [sb(f"eh{i}", [P, I]) for i in range(2)]
        ehT = [sb(f"ehT{i}", [IW, IJ, P]) for i in range(2)]
        ey = [sb(f"ey{i}", [P, D]) for i in range(2)]
        experts_only = ExitStack()
        scope[0] = experts_only
        wgu = [sb(f"wgu{i}", [P, 2, DC, 2 * I]) for i in range(RING_EARLY)] + \
            [acc[:, i, 0:2 * DC * 2 * I].rearrange("p (e c i) -> p e c i", e=2, c=DC) for i in range(RING - RING_EARLY)]
        wd = [sb(f"wd{i}", [IW, 2, IJ, D]) for i in range(RING)]
        experts_only.close()
        scope[0] = ctx
        routed = sb("routed", [P, 2, TILES, D])
        table = nc.dram_tensor("table", (T, XW), F32, kind="Internal").ap()
        sums = nc.dram_tensor("sums", (2 * REGION, D), F32, kind="Internal").ap()

        ps_s = [bank(f"ps_s{i}") for i in range(2)]
        ps_t = [bank(f"ps_t{i}") for i in range(2)]
        ps_o = bank("ps_o")
        ps_qk = ctx.enter_context(nc.psum_tensor("ps_qk", [P, 2, 512], F32))
        ps_vy = bank("ps_vy")
        ps_y = [ps_vy, ps_o]
        ps_logits = [ps_o, ps_vy]
        ps_sum = ps_s + ps_t

        x_in = [sem(f"x_in{b}") for b in range(B)]
        const_in, rope_loaded = sem("const_in"), sem("rope_loaded")
        wqk_in_s, wv_in_s, wo_in_s = sem("wqk_in"), sem("wv_in"), sem("wo_in")
        x_hi, x_lo = [[sem(f"{n}{b}") for b in range(B)] for n in ("x_hi_s", "x_lo_s")]
        wqk_hi, wqk_lo = sem("wqk_hi_s"), sem("wqk_lo_s")
        wv_hi, wv_lo = sem("wv_hi_s"), sem("wv_lo_s")
        wo_hi, wo_lo = sem("wo_hi_s"), sem("wo_lo_s")
        qk_proj = sem("qk_proj")
        qk_cosed, qk_swapped, qk_sined, qk_sum = sem("qk_cosed"), sem("qk_swapped"), sem("qk_sined"), sem("qk_sum")
        qk_hi, qk_lo = sem("qk_hi_s"), sem("qk_lo_s")
        v_proj, v_hi, v_lo = sem("v_proj"), sem("v_hi_s"), sem("v_lo_s")
        scored, maxed, exped, normed = sem("scored"), sem("maxed"), sem("exped"), sem("normed")
        inverted = sem("inverted")
        turned, pT_hi, pT_lo, mixed = sem("turned"), sem("pT_hi_s"), sem("pT_lo_s"), sem("mixed")
        o_hi, o_lo = sem("o_hi_s"), sem("o_lo_s")
        y_proj, y_added = sem("y_proj"), sem("y_added")
        stored = sem("stored")

        zeroed, cleared = sem("zeroed"), sem("cleared")
        gate_loaded, wsg_loaded, wsd_loaded = sem("gate_loaded"), sem("wsg_loaded"), sem("wsd_loaded")
        gate_hi_done, wsg_hi_done, wsd_hi_done = sem("gate_hi_done"), sem("wsg_hi_done"), sem("wsd_hi_done")
        gate_split, wsg_split, wsd_split = sem("gate_split"), sem("wsg_split"), sem("wsd_split")
        r_turned, r_raw, r_stats, r_std = sem("r_turned"), sem("r_raw"), sem("r_stats"), sem("r_std")
        r_rstd, r_shift = sem("r_rstd"), sem("r_shift")
        x1_done = sem("x1_done")
        x1_turned, x1T_hi, x1T_lo, gated = sem("x1_turned"), sem("x1T_hi"), sem("x1T_lo"), sem("gated")
        dve_step = sem("dve_step")
        shifted, softexp = sem("shifted"), sem("softexp")
        keyed, keys_turned, weighted = sem("keyed"), sem("keys_turned"), sem("weighted")
        pads_zeroed, listed, collected = sem("pads_zeroed"), sem("listed"), sem("collected")
        chosen_done, spread = sem("chosen_done"), sem("spread")
        rows_done, x1_tabled, weight_tabled = sem("rows_done"), sem("x1_tabled"), sem("weight_tabled")
        sh_projected, sh_silu, sh_product = sem("sh_projected"), sem("sh_silu"), sem("sh_product")
        sh_hi, sh_lo, sh_down, sh_added = sem("sh_hi_s"), sem("sh_lo_s"), sem("sh_down"), sem("sh_added")
        w_loaded = [sem(f"w_loaded{i}") for i in range(RING)]
        gathered = [sem(f"gathered{i}") for i in range(TOKENS_RING)]
        xg_turned, xgT_done, e_up, e_silu, e_hidden = sem("xg_turned"), sem("xgT_done"), sem("e_up"), sem("e_silu"), sem("e_hidden")
        eh_turned, ehT_done, e_down, e_scaled0, e_scaled1 = sem("eh_turned"), sem("ehT_done"), sem("e_down"), sem("e_scaled0"), sem("e_scaled1")
        summed = sem("summed")
        sums_in = [sem(f"sums_in{k}") for k in range(COUPLES)]
        f_raw = sem("f_raw")
        f_based, f_shift = sem("f_based"), sem("f_shift")
        f_sum, f_stats, f_std, f_rstd, f_done = sem("f_sum"), sem("f_stats"), sem("f_std"), sem("f_rstd"), sem("f_done")

        block = ctx.enter_context(nc.Block())

        def await_(eng, semaphore, count):
            if not isinstance(count, int) or count > 0:
                eng.wait_ge(semaphore, count)

        def half_at(s, lag):
            return s - lag - (s - lag) % 2, (s - lag) % 2

        def shared_banks(m):
            return (ps_s[m % 2], ps_t[m % 2]) if m < FIRST_UPS else (ps_qk[:, 0, :], ps_qk[:, 1, :])

        def next_step(s):
            return NEXT_STEPS[s + 1] if -1 <= s < len(NEXT_STEPS) - 1 and NEXT_STEPS[s + 1] else ("", 0, 0)

        def there(base, n, of=HEADS):
            return not isinstance(base, int) or 0 <= base + n < of

        def couple(k):
            return slice(2 * k * P, 2 * (k + 1) * P), slice(2 * k, 2 * (k + 1))

        def pipeline(eng, first, slot):
            for s in range(first, 4):
                slot(0, s)
            with eng.Fori(0, (PAIRS - 1) * PER_PAIR, PER_PAIR) as base:
                for s in range(4, 4 + PER_PAIR):
                    slot(base, s)
            for s in range(4, 9):
                slot(LAST, s)

        @block.sync
        def _(sp):
            def load_x(b):
                sp.dma_start(acc[:, :, b * S:(b + 1) * S], xT_in[:, :, b * S:(b + 1) * S]).then_inc(x_in[b], 16)

            sp.dma_start(wqk_raw[:], wqk_in[0]).then_inc(wqk_in_s, 16)
            load_x(0)
            sp.dma_start(wv_raw[:], wv_in[0]).then_inc(wv_in_s, 16)
            sp.dma_start(rope[:], rope_in).then_inc(rope_loaded, 16)
            load_x(1)
            load_x(2)
            sp.dma_start(consts[:], const_in_).then_inc(const_in, 16)
            load_x(3)
            sp.dma_start(wo_raw[:], wo_in[0]).then_inc(wo_in_s, 16)
            sp.dma_start(gate_raw[:], gate_in).then_inc(gate_loaded, 16)
            sp.dma_start(wsg_raw[:], wsg_in).then_inc(wsg_loaded, 16)
            sp.dma_start(wsd_raw[:], wsd_in).then_inc(wsd_loaded, 16)
            sp.wait_ge(zeroed, 1)
            for r in range(0, 2 * REGION, ZERO_ROWS * P):
                sp.dma_start(sums[r:r + ZERO_ROWS * P, :].rearrange("(p a) d -> p (a d)", a=ZERO_ROWS),
                             x1[:, 0:ZERO_ROWS, :].rearrange("p a d -> p (a d)")).then_inc(cleared, 16)
            with sp.Fori(1, PAIRS) as p:
                sp.wait_ge(wqk_lo, p)
                sp.dma_start(wqk_raw[:], wqk_in[bass.ds(p, 1)].rearrange("a p c n -> (a p) c n")).then_inc(wqk_in_s, 16)
                sp.wait_ge(wv_lo, p)
                sp.dma_start(wv_raw[:], wv_in[bass.ds(p, 1)].rearrange("a p c n -> (a p) c n")).then_inc(wv_in_s, 16)
                sp.wait_ge(wo_lo, p)
                sp.dma_start(wo_raw[:], wo_in[bass.ds(p, 1)].rearrange("a p c n -> (a p) c n")).then_inc(wo_in_s, 16)
            def load_experts(n):
                sp.dma_start(wgu[n % RING][:], wgu_in[n]).then_inc(w_loaded[n % RING], 16)
                sp.dma_start(wd[n % RING][:], wd_in[n]).then_inc(w_loaded[n % RING], 16)

            sp.wait_ge(y_added, HEADS)
            for n in range(RING_EARLY):
                load_experts(n)
            rows = table.rearrange("(t p) w -> p t w", p=P)
            sp.wait_ge(x1_done, COUPLES)
            sp.dma_start(rows[:, :, 0:D], x1[:]).then_inc(x1_tabled, 16)
            for n in range(RING_EARLY, RING):
                load_experts(n)
            sp.wait_ge(weighted, 1)
            sp.dma_start(rows[:, :, D:XW], weight[:]).then_inc(weight_tabled, 16)
            for n in range(RING, DUOS):
                sp.wait_ge(e_down, n - RING + 1)
                load_experts(n)
            by_tile = lambda rows: rows.rearrange("(t p) d -> p t d", p=P)
            sp.wait_ge(summed, 16 * DUOS)
            for k in range(COUPLES):
                rows, tiles = couple(k)
                for r in range(2):
                    first = r * REGION + rows.start
                    sp.dma_start(routed[:, r, tiles, :], by_tile(sums[first:first + 2 * P, :])).then_inc(sums_in[k], 16)
            for k in range(COUPLES):
                rows, tiles = couple(k)
                sp.wait_ge(f_done, k + 1)
                sp.dma_start(by_tile(out[rows, :]), x1[:, tiles, :]).then_inc(stored, 16)
            sp.wait_ge(stored, 16 * COUPLES)

        @block.tensor
        def _(pe):
            def project_qk(base, n, part):
                b, head = n // 2 % B, n % 2
                if part == 0:
                    await_(pe, qk_swapped, base + n)
                    if n % PER_PAIR == 0:
                        pe.wait_ge(wqk_lo, pair(base, n) + 1)
                col = (2 * part + head) * DH
                k = 0
                for c in range(DC):
                    for w_part, x_part in PASSES:
                        mm = pe.matmul(ps_qk[:, part, :], wqk[w_part][:, c, col:col + DH],
                                       x[x_part][:, c, b * S:(b + 1) * S], start=k == 0, stop=k == 5)
                        k += 1
                if part == 1:
                    mm.then_inc(qk_proj, 1)

            def project_v(base, n, half):
                b = n // 2 % B
                await_(pe, y_added, base + n - 3 + half)
                if half == 0 and n % PER_PAIR == 0:
                    pe.wait_ge(wv_lo, pair(base, n) + 1)
                for j in range(2):
                    t0 = b * S + (2 * half + j) * P
                    k = 0
                    for c in range(DC):
                        for x_part, w_part in PASSES:
                            mm = pe.matmul(ps_vy[:, j * 2 * DH:(j + 1) * 2 * DH], x[x_part][:, c, t0:t0 + P],
                                           wv[w_part][:, c, :], start=k == 0, stop=k == 5)
                            k += 1
                mm.then_inc(v_proj, 1)

            def project_y(base, n, half):
                last = not there(base, n + 2)
                if there(base, n + 2 + 2 * half):
                    pe.wait_ge(v_lo, base + n + 4 + half)
                elif not (last and half):
                    pe.wait_ge(y_added, base + n + half)
                bank_ = ps_y[half] if last else ps_vy
                if half == 0:
                    pe.wait_ge(o_lo, base + n + 2)
                    if n % PER_PAIR == 0:
                        pe.wait_ge(wo_lo, pair(base, n) + 1)
                k = 0
                for head in range(2):
                    for w_part, o_part in PASSES:
                        mm = pe.matmul(bank_[:], wo[w_part][:, head, half * P:(half + 1) * P],
                                       o[(n + head) % 4][o_part][:], start=k == 0, stop=k == 5)
                        k += 1
                mm.then_inc(y_proj, 1)

            def score(base, n, i):
                if i == 0:
                    pe.wait_ge(qk_lo, base + n + 1)
                await_(pe, exped, base * QT + (n * QT + i - 1))
                for k, (q_part, k_part) in enumerate(PASSES):
                    mm = pe.matmul(ps_s[i % 2][:], qk[n % 2][q_part][:, 0, i * P:(i + 1) * P],
                                   qk[n % 2][k_part][:, 1, :], start=k == 0, stop=k == 2)
                mm.then_inc(scored, 1)

            def turn(base, n, j):
                if j == 0:
                    pe.wait_ge(normed, base * QT + (n * QT + QT))
                await_(pe, pT_lo, base * QT + (n * QT + j - 1))
                for i in range(QT):
                    mm = pe.transpose(ps_t[j % 2][:, i * P:(i + 1) * P], prob[n % 2][:, i, j * P:(j + 1) * P], ident)
                mm.then_inc(turned, 1)

            def mix(base, n, j):
                pe.wait_ge(pT_lo, base * QT + (n * QT + j + 1))
                if j == 0:
                    pe.wait_ge(v_lo, base + (n - n % 2 + 2))
                    await_(pe, o_lo, base + n)
                head = n % 2
                for k, (v_part, p_part) in enumerate(PASSES):
                    mm = pe.matmul(ps_o[:], v[n // 2 % 2][v_part][:, j, head * DH:(head + 1) * DH],
                                   pT[j % 2][p_part][:], start=j == 0 and k == 0, stop=j == QT - 1 and k == 2)
                mm.then_inc(mixed, 1)

            def slot(base, s):
                scoring, projecting = there(base, s), there(base, s + 2)
                mixing = there(base, s - 1)
                y_head, y_half = half_at(s, 3)
                v_head, v_half = half_at(s, -1)
                if scoring:
                    score(base, s, 0)
                if projecting:
                    project_qk(base, s + 2, 0)
                if there(base, s - 2):
                    mix(base, s - 2, 3)
                if mixing:
                    turn(base, s - 1, 0)
                if scoring:
                    score(base, s, 1)
                if projecting:
                    project_qk(base, s + 2, 1)
                if mixing:
                    turn(base, s - 1, 1)
                if scoring:
                    score(base, s, 2)
                if there(base, y_head):
                    project_y(base, y_head, y_half)
                if mixing:
                    turn(base, s - 1, 2)
                    mix(base, s - 1, 0)
                if scoring:
                    score(base, s, 3)
                if mixing:
                    mix(base, s - 1, 1)
                if there(base, v_head):
                    project_v(base, v_head, v_half)
                if mixing:
                    turn(base, s - 1, 3)
                    mix(base, s - 1, 2)

            def pair(base, n):
                return base // PER_PAIR + n // PER_PAIR if isinstance(base, int) else pair_reg[0] + n // PER_PAIR

            def turn_sum(k):
                pe.wait_ge(y_added, (PAIRS - 1) * PER_PAIR + 2 * (k // 2 + 1))
                await_(pe, x1_done, k - 3)
                for t in range(2):
                    for c in range(DC):
                        tokens = slice((2 * k + t) * P, (2 * k + t + 1) * P)
                        mm = pe.transpose(ps_sum[k % 4][:, (DC * t + c) * P:(DC * t + c + 1) * P], acc[:, c, tokens], ident)
                mm.then_inc(r_turned, 1)

            def turn_x1(k):
                pe.wait_ge(x1_done, k + 1)
                await_(pe, x1T_lo, k - 1)
                for c in range(DC):
                    for t in range(2):
                        mm = pe.transpose(ps_qk[:, k % 2, (2 * c + t) * P:(2 * c + t + 1) * P],
                                          x1[:, 2 * k + t, c * P:(c + 1) * P], ident)
                mm.then_inc(x1_turned, 1)

            def project_logits(k):
                pe.wait_ge(x1T_lo, k + 1)
                if k == 0:
                    pe.wait_ge(gate_split, 1)
                for t in range(2 * k, 2 * k + 2):
                    bank_ = ps_logits[2 * t // TILES][:, t % (TILES // 2) * 2 * E:(t % (TILES // 2) + 1) * 2 * E]
                    for c in range(DC):
                        pe.matmul(bank_, x[0][:, c, t * P:(t + 1) * P], gate_parts[:, c].rearrange("p g e -> p (g e)"),
                                  start=c == 0, stop=False)
                        mm = pe.matmul(bank_[:, 0:E], x[1][:, c, t * P:(t + 1) * P], gate[0][:, c, :],
                                       start=False, stop=c == DC - 1)
                mm.then_inc(gated, 1)

            def norm_step(k):
                if k == 0:
                    turn_sum(0)
                if k + 1 < COUPLES:
                    turn_sum(k + 1)
                if 0 <= k - 2 < COUPLES:
                    turn_x1(k - 2)
                if 0 <= k - 4:
                    if k == 4:
                        pe.wait_ge(y_added, HEADS)
                    project_logits(k - 4)

            pair_reg = [0]
            pe.wait_ge(x_lo[0], 1)
            project_qk(0, 0, 0)
            project_qk(0, 0, 1)
            project_v(0, 0, 0)
            project_qk(0, 1, 0)
            project_qk(0, 1, 1)
            for s in range(4):
                if s in X_SPLITS:
                    pe.wait_ge(x_lo[X_SPLITS[s]], 1)
                if s == 1:
                    pe.wait_ge(const_in, 16)
                slot(0, s)
            pe.wait_ge(x_lo[B - 1], 1)
            with pe.Fori(0, PAIRS - 1) as pair_index:
                pair_reg[0] = pair_index
                for s in range(4, 4 + PER_PAIR):
                    slot(pair_index * PER_PAIR, s)
            for s in range(4, 9):
                slot(LAST, s)
            mix(LAST, PER_PAIR - 1, QT - 1)
            for k in NORM_STEPS[0]:
                norm_step(k)
            for half in range(2):
                project_y(LAST, PER_PAIR - 2, half)
            for k in NORM_STEPS[1]:
                norm_step(k)

            def shared_up(b, j):
                m = b * len(SH_CHUNKS) + j
                f, size = SH_CHUNKS[j]
                if m == 0:
                    pe.wait_ge(wsg_split, 1)
                    pe.wait_ge(x1_done, COUPLES)
                if m < FIRST_UPS:
                    await_(pe, sh_product, m - 1)
                else:
                    pe.wait_ge(sh_product, m)
                    pe.wait_ge(sh_added, 2 * b)
                for bank_, f0 in zip(shared_banks(m), (f, SH + f)):
                    k = 0
                    for c in range(DC):
                        for w_part, x_part in PASSES:
                            mm = pe.matmul(bank_[0:size, :], wsg[w_part][:, c, f0:f0 + size],
                                           x[x_part][:, c, b * S:(b + 1) * S], start=k == 0, stop=k == 5)
                            k += 1
                mm.then_inc(sh_projected, 1)

            def shared_down(b, half):
                u = 2 * b + half
                if half == 0:
                    pe.wait_ge(sh_lo, (b + 1) * len(SH_CHUNKS))
                if u == 0:
                    pe.wait_ge(wsd_split, 1)
                await_(pe, sh_added, u - 1)
                for i in range(2):
                    cols = slice((2 * half + i) * P, (2 * half + i + 1) * P)
                    k = 0
                    for j, (_, size) in enumerate(SH_CHUNKS):
                        for h_part, w_part in PASSES:
                            mm = pe.matmul(ps_qk[:, u % 2, i * D:(i + 1) * D], sh[h_part][0:size, j, cols],
                                           wsd[w_part][0:size, j, :], start=k == 0, stop=k == 8)
                            k += 1
                mm.then_inc(sh_down, 1)

            def turn_keys():
                pe.wait_ge(keyed, 1)
                for t in range(TILES):
                    rows = slice(t // QT * E, (t // QT + 1) * E)
                    mm = pe.matmul(ps_vy[rows, t % QT * P:(t % QT + 1) * P], key[:, t, :], ident, start=True, stop=True)
                mm.then_inc(keys_turned, 1)

            def collect_lists():
                pe.wait_ge(listed, 1)
                for q in range(QUARTERS):
                    mm = pe.matmul(ps_o[0:E, q * CAP:(q + 1) * CAP], ident[:, q * E:(q + 1) * E], lists[:],
                                   start=True, stop=True)
                mm.then_inc(collected, 1)

            def spread_chosen():
                pe.wait_ge(chosen_done, 1)
                pe.wait_ge(pads_zeroed, 1)
                for e in range(2):
                    mm = pe.matmul(ps_vy[e * ROWS:(e + 1) * ROWS, 0:DUOS], chosen[:], ident[0:E, e:E:2],
                                   start=True, stop=True)
                mm.then_inc(spread, 1)

            for j in range(len(SH_CHUNKS)):
                shared_up(0, j)
            shared_up(1, 0)
            turn_keys()
            shared_down(0, 0)
            shared_down(0, 1)
            shared_up(1, 1)
            shared_up(1, 2)
            collect_lists()
            shared_up(2, 0)
            shared_down(1, 0)
            spread_chosen()
            shared_down(1, 1)
            shared_up(2, 1)

            def turn_rows(n):
                pe.wait_ge(gathered[n % TOKENS_RING], (n // TOKENS_RING + 1) * 16)
                await_(pe, xgT_done, n)
                for c in range(DC):
                    mm = pe.transpose(ps_s[0][:, c * P:(c + 1) * P], xg[n % TOKENS_RING][:, c * P:(c + 1) * P], ident)
                mm.then_inc(xg_turned, 1)

            def expert_up(n):
                pe.wait_ge(w_loaded[n % RING], (n // RING + 1) * 32)
                pe.wait_ge(xgT_done, n + 1)
                await_(pe, e_hidden, n - 1)
                for e in range(2):
                    rows = slice(e * ROWS, (e + 1) * ROWS)
                    for c in range(DC):
                        mm = pe.matmul(ps_t[n % 2][rows, 0:2 * I], xgT[n % 2][:, c, rows], wgu[n % RING][:, e, c, :],
                                       start=c == 0, stop=c == DC - 1)
                mm.then_inc(e_up, 1)

            def turn_hidden(n):
                pe.wait_ge(e_hidden, n + 1)
                await_(pe, ehT_done, n)
                for j in range(IJ):
                    mm = pe.transpose(ps_s[1][0:IW, j * P:(j + 1) * P], eh[n % 2][:, j * IW:(j + 1) * IW], ident)
                mm.then_inc(eh_turned, 1)

            def expert_down(n):
                pe.wait_ge(ehT_done, n + 1)
                await_(pe, e_scaled0, n - 1)
                await_(pe, e_scaled1, n - 1)
                for e in range(2):
                    rows = slice(e * ROWS, (e + 1) * ROWS)
                    for j in range(IJ):
                        mm = pe.matmul(ps_y[n % 2][rows, 0:D], ehT[n % 2][:, j, rows], wd[n % RING][:, e, j, :],
                                       start=j == 0, stop=j == IJ - 1)
                mm.then_inc(e_down, 1)

            def duo_slot(s):
                if 0 <= s < DUOS:
                    expert_up(s)
                if 0 <= s + 1 < DUOS:
                    turn_rows(s + 1)
                if 0 <= s - 1 < DUOS:
                    turn_hidden(s - 1)
                if 0 <= s - 2 < DUOS:
                    expert_down(s - 2)
                kind, b, part = next_step(s)
                if kind == "up":
                    shared_up(b, part)
                if kind == "down":
                    shared_down(b, part)

            pe.wait_ge(sh_product, FIRST_UPS - 1)
            pe.wait_ge(rows_done, 1)

            for s in range(-1, DUOS + 2):
                duo_slot(s)

        @block.scalar
        def _(act):
            def exp(base, n, i):
                act.wait_ge(maxed, base * QT + (n * QT + i + 1))
                if i == 0:
                    await_(act, turned, base * QT + (n - 1) * QT)
                nc.scalar.activation(prob[n % 2][:, i, :], ps_s[i % 2][:], ACT.Exp, bias=neg_max[:, n % 2, i:i + 1],
                                     accum_out=row_sum[:, n % 2, i:i + 1]).then_inc(exped, 1)

            def split_o(base, n):
                act.wait_ge(mixed, base * QT + (n + 1) * QT)
                nc.scalar.copy(o[n % 4][0][:], ps_o[:]).then_inc(o_hi, 1)

            def split_pT(base, n, j):
                act.wait_ge(turned, base * QT + (n * QT + j + 1))
                await_(act, mixed, base * QT + (n * QT + j - 1))
                nc.scalar.copy(pT[j % 2][0][:], ps_t[j % 2][:]).then_inc(pT_hi, 1)

            def swap_qk(base, n, half):
                if half == 0:
                    act.wait_ge(qk_cosed, base + n + 1)
                    await_(act, qk_lo, base + n)
                    nc.scalar.copy(qk_rot[0:HALF, :, :], ps_qk[HALF:P, :, :])
                else:
                    nc.scalar.copy(qk_rot[HALF:P, :, :], ps_qk[0:HALF, :, :]).then_inc(qk_swapped, 1)

            def split_v(base, n, half):
                act.wait_ge(v_proj, base + n + half + 1)
                if half == 0:
                    await_(act, mixed, (base + (n - 2)) * QT)
                nc.scalar.copy(v[n // 2 % 2][0][:, 2 * half:2 * half + 2, :],
                               ps_vy[:].rearrange("p (j d) -> p j d", j=2)).then_inc(v_hi, 1)

            def slot(base, s):
                scoring, mixing, projecting = there(base, s), there(base, s - 1), there(base, s + 2)
                v_head, v_half = half_at(s, -1)
                if scoring:
                    exp(base, s, 0)
                if there(base, s - 2):
                    split_o(base, s - 2)
                if mixing:
                    split_pT(base, s - 1, 0)
                if scoring:
                    exp(base, s, 1)
                if mixing:
                    split_pT(base, s - 1, 1)
                if projecting:
                    swap_qk(base, s + 2, 0)
                if scoring:
                    exp(base, s, 2)
                if mixing:
                    split_pT(base, s - 1, 2)
                if projecting:
                    swap_qk(base, s + 2, 1)
                if there(base, v_head):
                    split_v(base, v_head, v_half)
                if mixing:
                    split_pT(base, s - 1, 3)
                if scoring:
                    exp(base, s, 3)
                if s == 6 and isinstance(base, int):
                    split_high(gate_loaded, gate_raw, gate, gate_hi_done)
                    split_high(wsg_loaded, wsg_raw, wsg, wsg_hi_done)
                    split_high(wsd_loaded, wsd_raw, wsd, wsd_hi_done)

            def norm_step(k):
                if k < COUPLES:
                    _, tiles = couple(k)
                    act.wait_ge(r_stats, k + 1)
                    nc.scalar.activation(std[:, tiles], moments[:, tiles, 1], ACT.Sqrt, bias=eps).then_inc(r_std, 1)
                if 0 <= k - 1 < COUPLES:
                    act.wait_ge(r_shift, k)
                    if k == 1:
                        act.wait_ge(cleared, CLEARINGS * 16)
                    for t in range(2 * (k - 1), 2 * k):
                        normed_tile = nc.scalar.activation(x1[:, t, :], ps_sum[(k - 1) % 4][:, t % 2 * D:(t % 2 + 1) * D],
                                                           ACT.Identity, scale=rstd[:, t:t + 1], bias=shift[:, t:t + 1])
                    normed_tile.then_inc(x1_done, 1)
                if 0 <= k - 2 < COUPLES:
                    cols, _ = couple(k - 2)
                    act.wait_ge(x1_turned, k - 1)
                    nc.scalar.copy(x[0][:, :, cols], ps_qk[:, k % 2, :].rearrange("p (c t) -> p c t", c=DC)
                                   ).then_inc(x1T_hi, 1)

            def split_high(loaded, whole, parts, done):
                act.wait_ge(loaded, 16)
                nc.scalar.copy(parts[0][:], whole[:]).then_inc(done, 1)

            act.wait_ge(wv_in_s, 16)
            nc.scalar.copy(wv[0][:], wv_raw[:]).then_inc(wv_hi, 1)
            for b in range(1, B):
                if b == B - 1:
                    for half in range(2):
                        swap_qk(0, 0, half)
                act.wait_ge(x_in[b], 16)
                cols = slice(b * S, (b + 1) * S)
                nc.scalar.copy(x[0][:, :, cols], acc[:, :, cols]).then_inc(x_hi[b], 1)
            split_v(0, 0, 0)
            for half in range(2):
                swap_qk(0, 1, half)
            pipeline(act, 0, slot)
            split_o(LAST, PER_PAIR - 1)
            act.wait_ge(const_in, 16)
            for part in NORM_STEPS:
                for k in part:
                    norm_step(k)


            def shared_act(m):
                size = SH_CHUNKS[m % len(SH_CHUNKS)][1]
                act.wait_ge(sh_projected, m + 1)
                await_(act, sh_product, m - 1)
                nc.scalar.activation(sh_gate[m % 2][0:size, :], shared_banks(m)[0][0:size, :], ACT.Silu).then_inc(sh_silu, 1)

            def shared_split(m):
                b, j = divmod(m, len(SH_CHUNKS))
                size = SH_CHUNKS[j][1]
                act.wait_ge(sh_product, m + 1)
                await_(act, sh_down, 2 * b)
                nc.scalar.copy(sh[0][0:size, j, :], sh_up[m % 2][0:size, :]).then_inc(sh_hi, 1)

            def softmax_exp():
                act.wait_ge(shifted, 1)
                nc.scalar.activation(expd[:], expd[:], ACT.Exp).then_inc(softexp, 1)

            for m in range(FIRST_UPS + 1):
                outputs_first = m == 2 * len(SH_CHUNKS)
                if outputs_first:
                    shared_split(m - 1)
                if m < FIRST_UPS:
                    shared_act(m)
                if m > 0 and not outputs_first:
                    shared_split(m - 1)
                if m == 3:
                    softmax_exp()

            def expert_silu(n):
                act.wait_ge(e_up, n + 1)
                await_(act, e_hidden, n - 1)
                nc.scalar.activation(eg[n % 2][:], ps_t[n % 2][:, 0:I], ACT.Silu).then_inc(e_silu, 1)

            def keep_hidden(n):
                act.wait_ge(eh_turned, n + 1)
                await_(act, e_down, n - 1)
                nc.scalar.copy(ehT[n % 2][:], ps_s[1][0:IW, 0:IJ * P].rearrange("p (j r) -> p j r", j=IJ)).then_inc(ehT_done, 1)

            def scale_rows(n):
                act.wait_ge(e_down, n + 1)
                await_(act, summed, 16 * (n - 1))
                col = D + 2 * n + 1
                nc.scalar.activation(ey[n % 2][ROWS:P, :], ps_y[n % 2][ROWS:P, 0:D], ACT.Copy,
                                     scale=xg[n % TOKENS_RING][ROWS:P, col:col + 1]).then_inc(e_scaled1, 1)

            def duo_slot(s):
                kind, b, part = next_step(s - 1)
                if kind == "up":
                    shared_act(b * len(SH_CHUNKS) + part)
                kind, b, part = next_step(s - 2)
                if kind == "up":
                    shared_split(b * len(SH_CHUNKS) + part)
                if 0 <= s < DUOS:
                    expert_silu(s)
                if 0 <= s - 1 < DUOS:
                    keep_hidden(s - 1)
                if 0 <= s - 2 < DUOS:
                    scale_rows(s - 2)

            for s in range(-1, DUOS + 2):
                duo_slot(s)

            for k in range(COUPLES + 1):
                if k < COUPLES:
                    _, tiles = couple(k)
                    act.wait_ge(f_stats, k + 1)
                    nc.scalar.activation(std[:, tiles], moments[:, tiles, 1], ACT.Sqrt, bias=eps).then_inc(f_std, 1)
                if k > 0:
                    act.wait_ge(f_shift, k)
                    for t in range(2 * (k - 1), 2 * k):
                        normed_tile = nc.scalar.activation(x1[:, t, :], routed[:, 0, t, :], ACT.Identity,
                                                           scale=rstd[:, t:t + 1], bias=shift[:, t:t + 1])
                    normed_tile.then_inc(f_done, 1)

        @block.vector
        def _(dve):
            def row_max(base, n, i):
                dve.wait_ge(scored, base * QT + (n * QT + i + 1))
                nc.vector.tensor_reduce(neg_max[:, n % 2, i:i + 1], ps_s[i % 2][:], AX.X, ALU.max,
                                        negate=True).then_inc(maxed, 1)

            def invert(base, n, i):
                dve.wait_ge(exped, base * QT + (n * QT + i + 1))
                nc.vector.reciprocal(inv_sum[:, n % 2, i:i + 1], row_sum[:, n % 2, i:i + 1]).then_inc(inverted, 1)

            def normalise(base, n, i):
                dve.wait_ge(inverted, base * QT + (n * QT + i + 1))
                nc.vector.tensor_scalar(prob[n % 2][:, i, :], prob[n % 2][:, i, :], inv_sum[:, n % 2, i:i + 1], None,
                                        ALU.mult).then_inc(normed, 1)

            def rest(out, whole, hi):
                return nc.vector.tensor_tensor(out, whole, hi.bitcast(F32), ALU.subtract)

            def split_o(base, n):
                dve.wait_ge(o_hi, base + n + 1)
                rest(o[n % 4][1][:], ps_o[:], o[n % 4][0][:]).then_inc(o_lo, 1)

            def split_pT(base, n, j):
                dve.wait_ge(pT_hi, base * QT + (n * QT + j + 1))
                rest(pT[j % 2][1][:], ps_t[j % 2][:], pT[j % 2][0][:]).then_inc(pT_lo, 1)

            def cos_qk(base, n):
                dve.wait_ge(qk_proj, base + n + 1)
                await_(dve, qk_sum, base + n)
                nc.vector.tensor_tensor(qk_cos[:], ps_qk[:], rope[:, 0], ALU.mult).then_inc(qk_cosed, 1)

            def split_qk(base, n):
                dve.wait_ge(qk_sum, base + n + 1)
                await_(dve, scored, (base + (n - 1)) * QT)
                nc.vector.tensor_copy(qk[n % 2][0][:], qk_rot[:]).then_inc(qk_hi, 1)

            def split_v(base, n, half):
                dve.wait_ge(v_hi, base + n + half + 1)
                rows = slice(2 * half, 2 * half + 2)
                rest(v[n // 2 % 2][1][:, rows, :], ps_vy[:].rearrange("p (j d) -> p j d", j=2),
                     v[n // 2 % 2][0][:, rows, :]).then_inc(v_lo, 1)

            def add_y(base, n, half):
                b = n // 2 % B
                dve.wait_ge(y_proj, base + n + half + 1)
                into = acc[:, half, b * S:(b + 1) * S]
                bank_ = ps_vy if there(base, n + 2) else ps_y[half]
                nc.vector.tensor_tensor(into, bank_[:], into, ALU.add).then_inc(y_added, 1)

            def split_wqk(base, n):
                dve.wait_ge(wqk_in_s, 16 * (pair(base, n) + 1))
                await_(dve, qk_proj, base + n)
                nc.vector.tensor_copy(wqk[0][:], wqk_raw[:]).then_inc(wqk_hi, 1)

            def split_wv(base, n):
                dve.wait_ge(wv_in_s, 16 * (pair(base, n) + 1))
                await_(dve, v_proj, base + n)
                nc.vector.tensor_copy(wv[0][:], wv_raw[:]).then_inc(wv_hi, 1)

            def split_wo(base, n):
                dve.wait_ge(wo_in_s, 16 * (pair(base, n) + 1))
                await_(dve, y_proj, base + n)
                nc.vector.tensor_copy(wo[0][:], wo_raw[:]).then_inc(wo_hi, 1)

            def slot(base, s):
                scoring, mixing = there(base, s), there(base, s - 1)
                y_head, y_half = half_at(s, 3)
                v_head, v_half = half_at(s, -1)
                if mixing:
                    invert(base, s - 1, 3)
                if scoring:
                    row_max(base, s, 0)
                if mixing:
                    normalise(base, s - 1, 3)
                if there(base, s + 1) and s > 0:
                    split_qk(base, s + 1)
                if s % PER_PAIR == PER_PAIR - 1 and there(base, s + 1):
                    split_wv(base, s + 1)
                if there(base, s - 2):
                    split_o(base, s - 2)
                if scoring:
                    row_max(base, s, 1)
                if mixing:
                    split_pT(base, s - 1, 0)
                if there(base, s + 2):
                    cos_qk(base, s + 2)
                if scoring:
                    row_max(base, s, 2)
                    invert(base, s, 0)
                if s % PER_PAIR == PER_PAIR - 3 and there(base, s + 3):
                    split_wqk(base, s + 3)
                if mixing:
                    split_pT(base, s - 1, 1)
                if scoring:
                    normalise(base, s, 0)
                if there(base, y_head):
                    add_y(base, y_head, y_half)
                if scoring:
                    invert(base, s, 1)
                if s % PER_PAIR == 2 and there(base, s - 2):
                    split_wo(base, s - 2)
                if scoring:
                    invert(base, s, 2)
                    normalise(base, s, 1)
                if mixing:
                    split_pT(base, s - 1, 2)
                if scoring:
                    normalise(base, s, 2)
                    row_max(base, s, 3)
                if there(base, v_head):
                    split_v(base, v_head, v_half)
                if mixing:
                    split_pT(base, s - 1, 3)

            def pair(base, n):
                return base // PER_PAIR + n // PER_PAIR if isinstance(base, int) else pair_reg[0] + n // PER_PAIR

            steps = [0]

            def link(instruction):
                steps[0] += 1
                instruction.then_inc(dve_step, 1)
                dve.wait_ge(dve_step, steps[0])

            def join_logits(half):
                dve.wait_ge(gated, (half + 1) * COUPLES // 2)
                tiles = logits[:, half * TILES // 2:(half + 1) * TILES // 2, :]
                products = ps_logits[half][:].rearrange("p (t g e) -> p t g e", g=2, e=E)
                link(nc.vector.tensor_copy(tiles, products[:, :, 1, :]))
                link(nc.vector.tensor_tensor(tiles, products[:, :, 0, :], tiles, ALU.add))

            def norm_step(k):
                before = 0 <= k - 1 < COUPLES
                tiles = couple(k - 1)[1]
                if k < COUPLES:
                    dve.wait_ge(r_turned, k + 1)
                    for t in range(2):
                        raw = nc.vector.bn_stats(stats[:, 2 * k + t, :], ps_sum[k % 4][:, t * D:(t + 1) * D])
                    raw.then_inc(r_raw, 1)
                if before:
                    dve.wait_ge(r_std, k)
                    nc.vector.reciprocal(rstd[:, tiles], std[:, tiles]).then_inc(r_rstd, 1)
                if k < COUPLES:
                    dve.wait_ge(r_raw, k + 1)
                    for t in range(2 * k, 2 * k + 2):
                        aggregated = nc.vector.bn_aggr(moments[:, t, :], stats[:, t, :])
                    aggregated.then_inc(r_stats, 1)
                if before:
                    dve.wait_ge(r_rstd, k)
                    nc.vector.scalar_tensor_tensor(out=shift[:, tiles], in0=moments[:, tiles, 0], scalar=-1.0,
                                                   in1=rstd[:, tiles], op0=ALU.mult, op1=ALU.mult).then_inc(r_shift, 1)
                if 0 <= k - 3 < COUPLES:
                    cols, _ = couple(k - 3)
                    dve.wait_ge(x1T_hi, k - 2)
                    rest(x[1][:, :, cols], ps_qk[:, (k - 3) % 2, :].rearrange("p (c t) -> p c t", c=DC),
                         x[0][:, :, cols]).then_inc(x1T_lo, 1)
                if k == COUPLES + 1:
                    join_logits(0)

            pair_reg = [0]
            dve.wait_ge(wqk_in_s, 16)
            nc.vector.tensor_copy(wqk[0][:], wqk_raw[:]).then_inc(wqk_hi, 1)
            dve.wait_ge(x_in[0], 16)
            nc.vector.tensor_copy(x[0][:, :, 0:S], acc[:, :, 0:S]).then_inc(x_hi[0], 1)
            dve.wait_ge(x_hi[0], 1)
            rest(x[1][:, :, 0:S], acc[:, :, 0:S], x[0][:, :, 0:S]).then_inc(x_lo[0], 1)
            dve.wait_ge(rope_loaded, 16)
            for n in range(2):
                cos_qk(0, n)
                if n == 1:
                    split_v(0, 0, 0)
                dve.wait_ge(qk_swapped, n + 1)
                nc.vector.tensor_tensor(qk_rot[:], qk_rot[:], rope[:, 1], ALU.mult).then_inc(qk_sined, 1)
                dve.wait_ge(qk_sined, n + 1)
                nc.vector.tensor_tensor(qk_rot[:], qk_rot[:], qk_cos[:], ALU.add).then_inc(qk_sum, 1)
                split_qk(0, n)
                dve.wait_ge(qk_hi, n + 1)
                rest(qk[n][1][:], qk_rot[:], qk[n][0][:]).then_inc(qk_lo, 1)
            for s in range(4):
                slot(0, s)
            dve.wait_ge(const_in, 16)
            with dve.Fori(0, PAIRS - 1) as pair_index:
                pair_reg[0] = pair_index
                for s in range(4, 4 + PER_PAIR):
                    slot(pair_index * PER_PAIR, s)
            for s in range(4, 9):
                slot(LAST, s)
            split_o(LAST, PER_PAIR - 1)
            for k in NORM_STEPS[0]:
                norm_step(k)
            for half in range(2):
                add_y(LAST, PER_PAIR - 2, half)
            for k in NORM_STEPS[1]:
                norm_step(k)


            def over_group(ap, n):
                return ap.unsqueeze(2).broadcast_to([P, ap.shape[1], n])

            def add_shared(u):
                dve.wait_ge(sh_down, u + 1)
                if u == 0:
                    dve.wait_ge(x1_tabled, 16)
                into = x1[:, 2 * u:2 * u + 2, :]
                nc.vector.tensor_tensor(into, ps_qk[:, u % 2, :].rearrange("p (t d) -> p t d", t=2), into,
                                        ALU.add).then_inc(sh_added, 1)

            def shared_product(m):
                size = SH_CHUNKS[m % len(SH_CHUNKS)][1]
                dve.wait_ge(sh_silu, m + 1)
                await_(dve, sh_lo, m - 1)
                nc.vector.tensor_tensor(sh_up[m % 2][0:size, :], shared_banks(m)[1][0:size, :],
                                        sh_gate[m % 2][0:size, :], ALU.mult).then_inc(sh_product, 1)

            def first_keys(source, out, rows, spare, done):
                link(nc.vector.tensor_copy(spare[1], source))
                source = spare[1]
                for r in range(CAP // TOP):
                    highest = out[rows, r * TOP:(r + 1) * TOP]
                    if r == CAP // TOP - 1:
                        nc.vector.max(highest, source).then_inc(done, 1)
                    else:
                        link(nc.vector.max(highest, source))
                        rest_of = spare[r % 2]
                        link(nc.vector.scalar_tensor_tensor(out=rest_of, in0=source, scalar=highest[:, TOP - 1:TOP],
                                                            in1=source, op0=ALU.is_lt, op1=ALU.mult))
                        source = rest_of

            def find_first(values, count, resets_, out, and_then=None):
                n = values.shape[2]
                over_, same_, upto_ = [a[:, :, 0:n] for a in (over, same, upto)] if n == E else \
                    [a[:, 0:TILES * n // E, :].rearrange("p a (b n) -> p (a b) n", n=n) for a in (over, same, upto)]
                for t in range(TILES):
                    top8 = nc.vector.max(top[:, t, :], values[:, t, :])
                link(top8)
                if and_then:
                    and_then()
                last = top[:, :, count - 1:count].broadcast_to([P, TILES, n])
                nc.vector.tensor_tensor(over_, values[:], last, ALU.is_gt)
                link(nc.vector.tensor_tensor(same_, values[:], last, ALU.is_equal))
                nc.vector.tensor_reduce(n_over[:], over_, AX.X, ALU.add)
                flat = lambda a: a.rearrange("p t n -> p (t n)")
                link(nc.vector.tensor_tensor_scan(flat(upto_), resets_, flat(same_), 0.0, ALU.mult, ALU.add))
                link(nc.vector.tensor_tensor(upto_, upto_, over_group(n_over[:], n), ALU.add))
                link(nc.vector.scalar_tensor_tensor(out=upto_, in0=upto_, scalar=float(count), in1=same_,
                                                    op0=ALU.is_le, op1=ALU.mult))
                link(nc.vector.tensor_tensor(out[:], over_, upto_, ALU.add))

            def shift_masked():
                nc.vector.tensor_tensor(expd[:], masked[:], top[:, :, 0:1].broadcast_to([P, TILES, E]),
                                        ALU.subtract).then_inc(shifted, 1)
                shared_product(1)

            join_logits(1)
            by_group = logits[:].rearrange("p t (g j) -> p t g j", g=GROUPS)
            link(nc.vector.tensor_reduce(group_max[:], by_group, AX.X, ALU.max))
            find_first(group_max, KEPT, group_resets, group_kept)
            link(nc.vector.tensor_tensor(masked[:].rearrange("p t (g j) -> p t g j", g=GROUPS), by_group,
                                         group_kept[:].unsqueeze(3).broadcast_to([P, TILES, GROUPS, E // GROUPS]),
                                         ALU.mult))
            shared_product(0)
            find_first(masked, PICKED, resets, picked, and_then=shift_masked)
            nc.vector.tensor_tensor(key[:], picked[:], over_group(countdown, E), ALU.mult).then_inc(keyed, 1)
            shared_product(2)
            shared_product(3)

            dve.wait_ge(keys_turned, 1)
            first_keys(ps_vy[:], lists, slice(0, P), [a[:] for a in left], listed)
            dve.wait_ge(softexp, 1)
            link(nc.vector.tensor_reduce(total[:], expd[:], AX.X, ALU.add))
            link(nc.vector.reciprocal(inv_total[:], total[:]))
            link(nc.vector.tensor_tensor(weight[:], expd[:], over_group(inv_total[:], E), ALU.mult))
            nc.vector.scalar_tensor_tensor(out=weight[:], in0=weight[:], scalar=SCALE, in1=picked[:],
                                           op0=ALU.mult, op1=ALU.mult).then_inc(weighted, 1)
            add_shared(0)
            add_shared(1)
            shared_product(4)
            shared_product(5)
            dve.wait_ge(collected, 1)
            first_keys(ps_o[0:E, 0:QUARTERS * CAP], chosen, slice(0, E), [a[0:E, 0:QUARTERS * CAP] for a in left],
                       chosen_done)
            shared_product(6)
            dve.wait_ge(spread, 1)
            link(nc.vector.tensor_copy(found[:], ps_vy[:, 0:DUOS]))
            nc.vector.tensor_scalar(counted[:], found[:], -1.0, float(T), ALU.mult, ALU.add)
            nc.vector.tensor_scalar(vacant[:], found[:], 0.0, None, ALU.is_le)
            link(nc.vector.tensor_scalar(taken[:], found[:], 0.0, None, ALU.is_gt))
            link(nc.vector.tensor_tensor(token[:], counted[:], taken[:], ALU.mult))
            nc.vector.tensor_copy(gather_row[:], token[:])
            link(nc.vector.scalar_tensor_tensor(out=row[:], in0=vacant[:], scalar=empty_row, in1=token[:],
                                                op0=ALU.mult, op1=ALU.add))
            nc.vector.tensor_scalar(add_row[:], row[:], region_of, None, ALU.add).then_inc(rows_done, 1)
            add_shared(2)
            add_shared(3)

            def keep_rows(n):
                dve.wait_ge(xg_turned, n + 1)
                await_(dve, e_up, n - 1)
                nc.vector.tensor_copy(xgT[n % 2][:], ps_s[0][:, 0:D].rearrange("p (c r) -> p c r", c=DC)).then_inc(xgT_done, 1)

            def hidden(n):
                dve.wait_ge(e_silu, n + 1)
                await_(dve, eh_turned, n - 1)
                nc.vector.tensor_tensor(eh[n % 2][:], ps_t[n % 2][:, I:2 * I], eg[n % 2][:], ALU.mult).then_inc(e_hidden, 1)

            def scale_rows(n):
                dve.wait_ge(e_down, n + 1)
                await_(dve, summed, 16 * (n - 1))
                col = D + 2 * n
                nc.vector.tensor_scalar(ey[n % 2][0:ROWS, :], ps_y[n % 2][0:ROWS, 0:D],
                                        xg[n % TOKENS_RING][0:ROWS, col:col + 1], None, ALU.mult).then_inc(e_scaled0, 1)

            def duo_slot(s):
                if s == 0:
                    shared_product(FIRST_UPS - 1)
                if 0 <= s + 1 < DUOS:
                    keep_rows(s + 1)
                kind, b, part = next_step(s - 1)
                if kind == "up":
                    shared_product(b * len(SH_CHUNKS) + part)
                if kind == "down":
                    add_shared(2 * b + part)
                if 0 <= s < DUOS:
                    hidden(s)
                if 0 <= s - 2 < DUOS:
                    scale_rows(s - 2)

            for s in range(-1, DUOS + 2):
                duo_slot(s)

            for k in range(COUPLES + 1):
                tiles, tiles_before = couple(k)[1], couple(k - 1)[1]
                if k < COUPLES:
                    dve.wait_ge(f_based, k + 1)
                    nc.vector.tensor_tensor(routed[:, 0, tiles, :], routed[:, 0, tiles, :], routed[:, 1, tiles, :],
                                            ALU.add).then_inc(f_sum, 1)
                if k > 0:
                    dve.wait_ge(f_raw, k)
                    for t in range(2 * k - 2, 2 * k):
                        aggregated = nc.vector.bn_aggr(moments[:, t, :], stats[:, t, :])
                    aggregated.then_inc(f_stats, 1)
                if k < COUPLES:
                    dve.wait_ge(f_sum, k + 1)
                    for t in range(2 * k, 2 * k + 2):
                        raw = nc.vector.bn_stats(stats[:, t, :], routed[:, 0, t, :])
                    raw.then_inc(f_raw, 1)
                if k > 0:
                    dve.wait_ge(f_std, k)
                    nc.vector.reciprocal(rstd[:, tiles_before], std[:, tiles_before]).then_inc(f_rstd, 1)
                    dve.wait_ge(f_rstd, k)
                    nc.vector.scalar_tensor_tensor(out=shift[:, tiles_before], in0=moments[:, tiles_before, 0],
                                                   scalar=-1.0, in1=rstd[:, tiles_before], op0=ALU.mult,
                                                   op1=ALU.mult).then_inc(f_shift, 1)

        @block.gpsimd
        def _(pool):
            def rest(out, whole, hi):
                return nc.gpsimd.tensor_tensor(out, whole, hi.bitcast(F32), ALU.subtract)

            def rotate_qk(base, n):
                pool.wait_ge(qk_swapped, base + n + 1)
                nc.gpsimd.tensor_tensor(qk_rot[:], qk_rot[:], rope[:, 1], ALU.mult).then_inc(qk_sined, 1)
                pool.wait_ge(qk_sined, base + n + 1)
                nc.gpsimd.tensor_tensor(qk_rot[:], qk_rot[:], qk_cos[:], ALU.add).then_inc(qk_sum, 1)

            def split_qk(base, n):
                pool.wait_ge(qk_hi, base + n + 1)
                rest(qk[n % 2][1][:], qk_rot[:], qk[n % 2][0][:]).then_inc(qk_lo, 1)

            def split_weights(base, s):
                if s % PER_PAIR == PER_PAIR - 3 and there(base, s + 3):
                    pool.wait_ge(wqk_hi, pair(base, s + 3) + 1)
                    rest(wqk[1][:], wqk_raw[:], wqk[0][:]).then_inc(wqk_lo, 1)
                if s % PER_PAIR == PER_PAIR - 1 and there(base, s + 1):
                    pool.wait_ge(wv_hi, pair(base, s + 1) + 1)
                    rest(wv[1][:], wv_raw[:], wv[0][:]).then_inc(wv_lo, 1)
                if s % PER_PAIR == 2 and there(base, s - 2):
                    pool.wait_ge(wo_hi, pair(base, s - 2) + 1)
                    rest(wo[1][:], wo_raw[:], wo[0][:]).then_inc(wo_lo, 1)

            def slot(base, s):
                if there(base, s + 1) and s > 0:
                    split_qk(base, s + 1)
                split_weights(base, s)
                if there(base, s + 2):
                    rotate_qk(base, s + 2)

            def pair(base, n):
                return base // PER_PAIR + n // PER_PAIR if isinstance(base, int) else pair_reg[0] + n // PER_PAIR

            pair_reg = [0]
            pool.wait_ge(wqk_hi, 1)
            rest(wqk[1][:], wqk_raw[:], wqk[0][:]).then_inc(wqk_lo, 1)
            pool.wait_ge(wv_hi, 1)
            rest(wv[1][:], wv_raw[:], wv[0][:]).then_inc(wv_lo, 1)
            for b in range(1, B):
                pool.wait_ge(x_hi[b], 1)
                cols = slice(b * S, (b + 1) * S)
                rest(x[1][:, :, cols], acc[:, :, cols], x[0][:, :, cols]).then_inc(x_lo[b], 1)
            pool.wait_ge(rope_loaded, 16)
            for s in range(4):
                slot(0, s)
                if s == 2:
                    nc.gpsimd.memset(x1[:, 0:ZERO_ROWS, :], 0.0).then_inc(zeroed, 1)
            with pool.Fori(0, PAIRS - 1) as pair_index:
                pair_reg[0] = pair_index
                for s in range(4, 4 + PER_PAIR):
                    slot(pair_index * PER_PAIR, s)
            for s in range(4, 9):
                slot(LAST, s)

            for hi_done, whole, parts, done in ((gate_hi_done, gate_raw, gate, gate_split),
                                                (wsg_hi_done, wsg_raw, wsg, wsg_split), (wsd_hi_done, wsd_raw, wsd, wsd_split)):
                pool.wait_ge(hi_done, 1)
                rest(parts[1][:], whole[:], parts[0][:]).then_inc(done, 1)
            pool.wait_ge(y_added, HEADS)
            nc.gpsimd.memset(chosen[:, CAP:ROWS], 0.0).then_inc(pads_zeroed, 1)

            def shared_low(m):
                j = m % len(SH_CHUNKS)
                size = SH_CHUNKS[j][1]
                pool.wait_ge(sh_hi, m + 1)
                rest(sh[1][0:size, j, :], sh_up[m % 2][0:size, :], sh[0][0:size, j, :]).then_inc(sh_lo, 1)

            for m in range(2 * len(SH_CHUNKS)):
                shared_low(m)

            def gather(n):
                if n >= TOKENS_RING:
                    pool.wait_ge(e_scaled0, n - TOKENS_RING + 1)
                    pool.wait_ge(e_scaled1, n - TOKENS_RING + 1)
                nc.gpsimd.indirect_dma_start(out=xg[n % TOKENS_RING][:], out_offset=None, in_=table,
                                             in_offset=bass.IndirectOffsetOnAxis(gather_row[:, n:n + 1], 0)
                                             ).then_inc(gathered[n % TOKENS_RING], 16)

            pool.wait_ge(rows_done, 1)
            pool.wait_ge(x1_tabled, 16)
            pool.wait_ge(weight_tabled, 16)
            for n in range(TOKENS_RING):
                gather(n)
            for m in range(2 * len(SH_CHUNKS), FIRST_UPS + 1):
                shared_low(m)
            pool.wait_ge(cleared, 16 * CLEARINGS)
            for n in range(DUOS):
                kind, b, part = next_step(n)
                if kind == "up":
                    shared_low(b * len(SH_CHUNKS) + part)
                pool.wait_ge(e_scaled0, n + 1)
                pool.wait_ge(e_scaled1, n + 1)
                if n:
                    pool.wait_ge(summed, 16 * n)
                nc.gpsimd.indirect_dma_start(out=sums, out_offset=bass.IndirectOffsetOnAxis(add_row[:, n:n + 1], 0),
                                             in_=ey[n % 2][:], in_offset=None, compute_op=ALU.add).then_inc(summed, 16)
                if n + TOKENS_RING < DUOS:
                    gather(n + TOKENS_RING)

            pool.wait_ge(sh_added, TILES // 2)
            for k in range(COUPLES):
                _, tiles = couple(k)
                pool.wait_ge(sums_in[k], 32)
                nc.gpsimd.tensor_tensor(routed[:, 1, tiles, :], routed[:, 1, tiles, :], x1[:, tiles, :],
                                        ALU.add).then_inc(f_based, 1)



def _constants():
    import numpy as np

    inv_freq = 1.0 / 10000.0 ** (np.arange(0, DH, 2, dtype=np.float32) / DH)
    angle = (np.arange(S, dtype=np.float32)[:, None] * inv_freq[None].astype(np.float32)).T
    angle = np.concatenate([angle, angle])
    cos = np.cos(angle)
    sin = np.sin(angle) * np.where(np.arange(DH) < HALF, -1.0, 1.0)[:, None]
    scale = DH ** -0.5
    rope = np.stack([np.stack([cos * scale, cos], 1), np.stack([sin * scale, sin], 1)], 1)

    p = np.arange(P)
    ident = np.eye(P)
    group_resets = np.broadcast_to(np.tile(np.arange(GROUPS) > 0, TILES), (P, TILES * GROUPS))
    resets = np.broadcast_to(np.tile(np.arange(E) > 0, TILES), (P, TILES * E))
    countdown = T - (np.arange(TILES)[None, :] * P + p[:, None])
    empty_row = (T + p % ROWS)[:, None]
    region_of = (REGION * (p >= ROWS))[:, None]
    eps = np.full((P, 1), EPS)
    const = np.concatenate([ident, group_resets, resets, countdown, empty_row, region_of, eps], 1)

    return rope.astype(np.float32), const.astype(np.float32)


def kernel(L0_attn_x, L0_attn_w_qkv, L0_attn_w_out, L0_ffn_gate_w, L0_ffn_w_gate_up, L0_ffn_w_down,
           L0_ffn_ws_gate_up, L0_ffn_ws_down):
    import numpy as np
    import concourse.bacc as bacc
    from concourse.bass_utils import run_bass_kernel_spmd

    qkv = np.asarray(L0_attn_w_qkv).reshape(3, H // 2, 2, DH, DC, P)
    shared_down = np.zeros((len(SH_CHUNKS) * P, D), np.float32)
    shared_down[:SH] = np.asarray(L0_ffn_ws_down)
    rope, const = _constants()
    arrays = {
        "xT": np.asarray(L0_attn_x).reshape(T, DC, P).transpose(2, 1, 0),
        "wqk": qkv[:2].transpose(1, 5, 4, 0, 2, 3).reshape(H // 2, P, DC, 4 * DH),
        "wv": qkv[2].transpose(0, 4, 3, 1, 2).reshape(H // 2, P, DC, 2 * DH),
        "wo": np.asarray(L0_attn_w_out).reshape(D, H // 2, 2, DH).transpose(1, 3, 2, 0),
        "rope": rope,
        "gate": np.asarray(L0_ffn_gate_w).reshape(E, DC, P).transpose(2, 1, 0),
        "wsg": np.asarray(L0_ffn_ws_gate_up).reshape(DC, P, 2 * SH).transpose(1, 0, 2),
        "wsd": shared_down.reshape(len(SH_CHUNKS), P, D).transpose(1, 0, 2),
        "wgu": np.asarray(L0_ffn_w_gate_up).reshape(DUOS, 2, DC, P, 2 * I).transpose(0, 3, 1, 2, 4),
        "wd": np.asarray(L0_ffn_w_down).reshape(DUOS, 2, IJ, IW, D).transpose(0, 3, 1, 2, 4),
        "const": const,
    }
    arrays = {f"in_{name}": np.ascontiguousarray(a) for name, a in arrays.items()}

    nc = bacc.Bacc("TRN2", target_bir_lowering=False, num_devices=1)
    args = [nc.dram_tensor(name, a.shape, mybir.dt.from_np(a.dtype), kind="ExternalInput").ap()
            for name, a in arrays.items()]
    out = nc.dram_tensor("out_0", (T, D), F32, kind="ExternalOutput").ap()
    layer(nc, *args, out)
    r = run_bass_kernel_spmd(nc, [arrays], core_ids=[0])
    return r.results[0]["out_0"].reshape(B, S, D)
```
